# Optimizing a Trainium2 kernel written in Bass

```python
import numpy as np
import jax
import jax.numpy as jnp

def _softmax(x, axis=-1):
    return jax.nn.softmax(x, axis=axis)

def _gelu(x):
    return jax.nn.gelu(x, approximate=True)

def _silu(x):
    return jax.nn.silu(x)

def _sigmoid(x):
    return jax.nn.sigmoid(x)

def _layernorm(x, axis=-1, eps=1e-05):
    m = jnp.mean(x, axis=axis, keepdims=True)
    v = jnp.var(x, axis=axis, keepdims=True)
    return (x - m) / jnp.sqrt(v + eps)

def _scatter_add(tgt, idx, src, axis=0):
    return tgt.at[idx].add(src)

def _segment_sum(src, seg, n):
    return jax.ops.segment_sum(src, seg, n)
kernel_name = 'mk_audio_tower_d2_tok_audfeat1024_r4_4730fc'

def setup_inputs(seed: int=0):
    np.random.seed(seed)
    _w = jnp.asarray

    def _rec_inputs():
        import jax
        import jax.numpy as jnp
        _rk = jax.random.key(seed)
        x = -7.10856e-05 + 0.999911 * jax.random.normal(jax.random.fold_in(_rk, 1), (64, 125, 256), jnp.float32)
        return x
    x = _rec_inputs()

    def _L0_tok_setup():
        import jax, jax.numpy as jnp
        import numpy as np
        LN_EPS = 1e-05
        key = jax.random.key(seed)
        ks = jax.random.split(key, 8)
        B, N, D, BS = (8, 2048, 256, 16)
        x = jax.random.normal(ks[0], (B, N, D), dtype=jnp.float32)
        conv_w = jax.random.normal(ks[1], (D, D, BS), dtype=jnp.float32) / np.sqrt(D * BS)
        conv_b = jax.random.normal(ks[2], (D,), dtype=jnp.float32) * 0.02
        proj_w = jax.random.normal(ks[3], (D, 3 * D), dtype=jnp.float32) / np.sqrt(3 * D)
        proj_b = jax.random.normal(ks[4], (D,), dtype=jnp.float32) * 0.02
        ln_g = jnp.ones((D,), dtype=jnp.float32)
        ln_b = jnp.zeros((D,), dtype=jnp.float32)
        pos_table = jax.random.normal(ks[5], (4096, D), dtype=jnp.float32) * 0.02
        return {'x': x, 'conv_w': conv_w, 'conv_b': conv_b, 'proj_w': proj_w, 'proj_b': proj_b, 'ln_g': ln_g, 'ln_b': ln_b, 'pos_table': pos_table}
    _L0_tok_all = _L0_tok_setup()
    _L0_tok_in = {k: v for k, v in _L0_tok_all.items() if k in ('conv_w', 'conv_b', 'proj_w', 'proj_b', 'ln_g', 'ln_b', 'pos_table')}
    del _L0_tok_all

    def _L0_attn_setup():
        import jax, jax.numpy as jnp
        import numpy as np
        B, N, C, H = (4, 1024, 256, 16)
        D = C // H
        LN_EPS = 1e-05
        key = jax.random.key(seed)
        ks = jax.random.split(key, 20)
        s = 0.02
        inp = {'x': jax.random.normal(ks[0], (B, N, C), jnp.float32)}
        for i, nm in enumerate(['q', 'k1', 'k2', 'v1', 'v2']):
            inp[f'W{nm}'] = jax.random.normal(ks[1 + i], (C, C), jnp.float32) * s
            inp[f'b{nm}'] = jnp.zeros((C,), jnp.float32)
        for i in range(4):
            inp[f'g{i + 1}'] = jax.random.normal(ks[10 + i], (H,), jnp.float32) * 0.5
        inp['ln_g'] = jnp.ones((C,), jnp.float32)
        inp['ln_b'] = jnp.zeros((C,), jnp.float32)
        inp['Wo'] = jax.random.normal(ks[14], (C, C), jnp.float32) * s
        inp['bo'] = jnp.zeros((C,), jnp.float32)
        return inp
    _L0_attn_all = _L0_attn_setup()
    _L0_attn_in = {k: v for k, v in _L0_attn_all.items() if k in ('Wq', 'bq', 'Wk1', 'bk1', 'Wk2', 'bk2', 'Wv1', 'bv1', 'Wv2', 'bv2', 'g1', 'g2', 'g3', 'g4', 'ln_g', 'ln_b', 'Wo', 'bo')}
    del _L0_attn_all

    def _L0_ffn_setup():
        import jax, jax.numpy as jnp
        import numpy as np
        CAPACITY_RATIO = 0.75
        key = jax.random.key(seed)
        k1, k2, k3 = jax.random.split(key, 3)
        B, L, D = (4, 2048, 256)
        x = jax.random.normal(k1, (B, L, D), dtype=jnp.float32)
        w_router = jax.random.normal(k2, (D,), dtype=jnp.float32) * 0.02
        w_block = jax.random.normal(k3, (D, D), dtype=jnp.float32) * 0.02
        return {'x': x, 'w_router': w_router, 'w_block': w_block}
    _L0_ffn_all = _L0_ffn_setup()
    _L0_ffn_in = {k: v for k, v in _L0_ffn_all.items() if k in ('w_router', 'w_block')}
    del _L0_ffn_all

    def _L1_attn_setup():
        import jax, jax.numpy as jnp
        import numpy as np
        B, L, D, FF = (4, 1024, 256, 1024)
        EPS = 1e-05

        def _layernorm(x, gamma, beta):
            mu = jnp.mean(x, axis=-1, keepdims=True)
            var = jnp.var(x, axis=-1, keepdims=True)
            return (x - mu) * jax.lax.rsqrt(var + EPS) * gamma + beta

        def _spiral_conv(x, phazor_re, phazor_im, phazor_init_re, phazor_init_im, last_conv_re, last_conv_im):
            length = x.shape[1]
            phazor_raw = phazor_re + 1j * phazor_im
            mag = jnp.abs(phazor_raw)
            phazor = phazor_raw / mag * jnp.exp(-mag)
            t = jnp.arange(length)[:, None]
            prog = jnp.power(phazor[None, :], t)
            phazor_init = phazor_init_re + 1j * phazor_init_im
            filt = prog * phazor_init[None, :]
            filt_fft = jnp.fft.fft(filt, n=2 * length, axis=0)
            x_fft = jnp.fft.fft(x.astype(jnp.complex64), n=2 * length, axis=1)
            conv = jnp.fft.ifft(filt_fft[None] * x_fft, axis=1)[:, :length]
            last_conv = last_conv_re + 1j * last_conv_im
            last_conv = jax.lax.stop_gradient(last_conv)
            conv_with_past = conv + last_conv[None, None, :] * prog[None] * phazor[None, None, :]
            return conv_with_past.real
        key = jax.random.key(seed)
        ks = jax.random.split(key, 10)
        return {'x': jax.random.normal(ks[0], (B, L, D), dtype=jnp.float32), 'ln_gamma': jnp.ones((D,), dtype=jnp.float32), 'ln_beta': jnp.zeros((D,), dtype=jnp.float32), 'phazor_re': jax.random.normal(ks[1], (D,), dtype=jnp.float32), 'phazor_im': jax.random.normal(ks[2], (D,), dtype=jnp.float32), 'phazor_init_re': jax.random.normal(ks[3], (D,), dtype=jnp.float32), 'phazor_init_im': jax.random.normal(ks[4], (D,), dtype=jnp.float32), 'last_conv_re': jax.random.normal(ks[5], (D,), dtype=jnp.float32), 'last_conv_im': jax.random.normal(ks[6], (D,), dtype=jnp.float32), 'w1': jax.random.normal(ks[7], (D, FF), dtype=jnp.float32) * 0.02, 'b1': jnp.zeros((FF,), dtype=jnp.float32), 'w2': jax.random.normal(ks[8], (FF, D), dtype=jnp.float32) * 0.02, 'b2': jnp.zeros((D,), dtype=jnp.float32)}
    _L1_attn_all = _L1_attn_setup()
    _L1_attn_in = {k: v for k, v in _L1_attn_all.items() if k in ('ln_gamma', 'ln_beta', 'phazor_re', 'phazor_im', 'phazor_init_re', 'phazor_init_im', 'last_conv_re', 'last_conv_im', 'w1', 'b1', 'w2', 'b2')}
    del _L1_attn_all

    def _L1_ffn_setup():
        import jax, jax.numpy as jnp
        import numpy as np
        B, S, K, N = (8, 2048, 256, 256)
        key = jax.random.key(seed)
        k1, k2, k3, k4 = jax.random.split(key, 4)
        x = jax.random.normal(k1, (B, S, K), dtype=jnp.float32)
        CB = jnp.clip(jnp.round(jax.random.normal(k2, (N, K), dtype=jnp.float32) * 42.0), -127.0, 127.0)
        SCB = jax.random.uniform(k3, (N,), dtype=jnp.float32, minval=0.5, maxval=2.0)
        bias = jax.random.normal(k4, (N,), dtype=jnp.float32) * 0.02
        return {'x': x, 'CB': CB, 'SCB': SCB, 'bias': bias}
    _L1_ffn_all = _L1_ffn_setup()
    _L1_ffn_in = {k: v for k, v in _L1_ffn_all.items() if k in ('CB', 'SCB', 'bias')}
    del _L1_ffn_all
    return {'x': x, 'L0_tok_conv_w': _L0_tok_in['conv_w'], 'L0_tok_conv_b': _L0_tok_in['conv_b'], 'L0_tok_proj_w': _L0_tok_in['proj_w'], 'L0_tok_proj_b': _L0_tok_in['proj_b'], 'L0_tok_ln_g': _L0_tok_in['ln_g'], 'L0_tok_ln_b': _L0_tok_in['ln_b'], 'L0_tok_pos_table': _L0_tok_in['pos_table'], 'L0_attn_Wq': _L0_attn_in['Wq'], 'L0_attn_bq': _L0_attn_in['bq'], 'L0_attn_Wk1': _L0_attn_in['Wk1'], 'L0_attn_bk1': _L0_attn_in['bk1'], 'L0_attn_Wk2': _L0_attn_in['Wk2'], 'L0_attn_bk2': _L0_attn_in['bk2'], 'L0_attn_Wv1': _L0_attn_in['Wv1'], 'L0_attn_bv1': _L0_attn_in['bv1'], 'L0_attn_Wv2': _L0_attn_in['Wv2'], 'L0_attn_bv2': _L0_attn_in['bv2'], 'L0_attn_g1': _L0_attn_in['g1'], 'L0_attn_g2': _L0_attn_in['g2'], 'L0_attn_g3': _L0_attn_in['g3'], 'L0_attn_g4': _L0_attn_in['g4'], 'L0_attn_ln_g': _L0_attn_in['ln_g'], 'L0_attn_ln_b': _L0_attn_in['ln_b'], 'L0_attn_Wo': _L0_attn_in['Wo'], 'L0_attn_bo': _L0_attn_in['bo'], 'L0_ffn_w_router': _L0_ffn_in['w_router'], 'L0_ffn_w_block': _L0_ffn_in['w_block'], 'L1_attn_ln_gamma': _L1_attn_in['ln_gamma'], 'L1_attn_ln_beta': _L1_attn_in['ln_beta'], 'L1_attn_phazor_re': _L1_attn_in['phazor_re'], 'L1_attn_phazor_im': _L1_attn_in['phazor_im'], 'L1_attn_phazor_init_re': _L1_attn_in['phazor_init_re'], 'L1_attn_phazor_init_im': _L1_attn_in['phazor_init_im'], 'L1_attn_last_conv_re': _L1_attn_in['last_conv_re'], 'L1_attn_last_conv_im': _L1_attn_in['last_conv_im'], 'L1_attn_w1': _L1_attn_in['w1'], 'L1_attn_b1': _L1_attn_in['b1'], 'L1_attn_w2': _L1_attn_in['w2'], 'L1_attn_b2': _L1_attn_in['b2'], 'L1_ffn_CB': _L1_ffn_in['CB'], 'L1_ffn_SCB': _L1_ffn_in['SCB'], 'L1_ffn_bias': _L1_ffn_in['bias']}

def reference(x, L0_tok_conv_w, L0_tok_conv_b, L0_tok_proj_w, L0_tok_proj_b, L0_tok_ln_g, L0_tok_ln_b, L0_tok_pos_table, L0_attn_Wq, L0_attn_bq, L0_attn_Wk1, L0_attn_bk1, L0_attn_Wk2, L0_attn_bk2, L0_attn_Wv1, L0_attn_bv1, L0_attn_Wv2, L0_attn_bv2, L0_attn_g1, L0_attn_g2, L0_attn_g3, L0_attn_g4, L0_attn_ln_g, L0_attn_ln_b, L0_attn_Wo, L0_attn_bo, L0_ffn_w_router, L0_ffn_w_block, L1_attn_ln_gamma, L1_attn_ln_beta, L1_attn_phazor_re, L1_attn_phazor_im, L1_attn_phazor_init_re, L1_attn_phazor_init_im, L1_attn_last_conv_re, L1_attn_last_conv_im, L1_attn_w1, L1_attn_b1, L1_attn_w2, L1_attn_b2, L1_ffn_CB, L1_ffn_SCB, L1_ffn_bias):
    import jax
    import jax.numpy as jnp

    def _L0_tok_ref(x, conv_w, conv_b, proj_w, proj_b, ln_g, ln_b, pos_table):
        import jax, jax.numpy as jnp
        import numpy as np
        LN_EPS = 1e-05
        B, N, D = x.shape
        bs = conv_w.shape[2]
        pad = -N % bs
        if pad:
            x = jnp.pad(x, ((0, 0), (0, pad), (0, 0)))
        nb = x.shape[1] // bs
        blocks = x.reshape(B, nb, bs, D)
        conv_out = jnp.einsum('bnkd,odk->bno', blocks, conv_w) + conv_b
        mean = blocks.mean(axis=2, keepdims=True)
        std_pool = jnp.sqrt(((blocks - mean) ** 2).sum(axis=2) / (bs - 1))
        max_pool = blocks.max(axis=2)
        combined = jnp.concatenate([conv_out, std_pool, max_pool], axis=-1)
        h = combined @ proj_w.T + proj_b
        mu = h.mean(axis=-1, keepdims=True)
        var = ((h - mu) ** 2).mean(axis=-1, keepdims=True)
        out = (h - mu) * jax.lax.rsqrt(var + LN_EPS) * ln_g + ln_b
        return out + pos_table[:nb]

    def _L0_attn_ref(x, Wq, bq, Wk1, bk1, Wk2, bk2, Wv1, bv1, Wv2, bv2, g1, g2, g3, g4, ln_g, ln_b, Wo, bo):
        import jax, jax.numpy as jnp
        import numpy as np
        B, N, C, H = (4, 1024, 256, 16)
        D = C // H
        LN_EPS = 1e-05
        b, n, c = x.shape
        h, d = (H, c // H)

        def proj_heads(W, bb):
            z = x + x @ W.T + bb
            return z.reshape(b, n, h, d).transpose(0, 2, 1, 3)
        q = proj_heads(Wq, bq).astype(jnp.float32)
        k1 = proj_heads(Wk1, bk1).astype(jnp.float32)
        k2 = proj_heads(Wk2, bk2).astype(jnp.float32)
        v1 = proj_heads(Wv1, bv1).astype(jnp.float32)
        v2 = proj_heads(Wv2, bv2).astype(jnp.float32)
        S1 = jnp.einsum('bhnd,bhne->bhde', k1, v1) / n
        S2 = jnp.einsum('bhnd,bhne->bhde', k2, v2) / n
        v1m = v1.mean(axis=2, keepdims=True)
        v2m = v2.mean(axis=2, keepdims=True)
        S12 = S1 * S2
        y1 = q @ S1 * v2m
        y2 = S12.sum(axis=2, keepdims=True)
        y3 = q @ S2 * v1m
        y4 = q @ S12
        gr = lambda g: g.reshape(1, h, 1, 1)
        out = y1 * gr(g1) + y2 * gr(g2) + y3 * gr(g3) + y4 * gr(g4)
        out = out.transpose(0, 2, 1, 3).reshape(b, n, c)
        mu = out.mean(axis=-1, keepdims=True)
        var = jnp.mean((out - mu) ** 2, axis=-1, keepdims=True)
        out = (out - mu) * jax.lax.rsqrt(var + LN_EPS) * ln_g + ln_b
        return out @ Wo.T + bo

    def _L0_ffn_ref(x, w_router, w_block):
        import jax, jax.numpy as jnp
        import numpy as np
        CAPACITY_RATIO = 0.75
        B, L, D = x.shape
        k = max(1, int(L * CAPACITY_RATIO))
        scores = jnp.einsum('bld,d->bl', x, w_router)
        _, top_idx = jax.lax.top_k(scores, k)
        selected = jnp.take_along_axis(x, top_idx[:, :, None], axis=1)
        processed = jax.nn.gelu(jnp.einsum('bkd,de->bke', selected, w_block))
        batch_idx = jnp.arange(B)[:, None]
        out = x.at[batch_idx, top_idx].set(processed)
        return out

    def _L1_attn_ref(x, ln_gamma, ln_beta, phazor_re, phazor_im, phazor_init_re, phazor_init_im, last_conv_re, last_conv_im, w1, b1, w2, b2):
        import jax, jax.numpy as jnp
        import numpy as np
        B, L, D, FF = (4, 1024, 256, 1024)
        EPS = 1e-05

        def _layernorm(x, gamma, beta):
            mu = jnp.mean(x, axis=-1, keepdims=True)
            var = jnp.var(x, axis=-1, keepdims=True)
            return (x - mu) * jax.lax.rsqrt(var + EPS) * gamma + beta

        def _spiral_conv(x, phazor_re, phazor_im, phazor_init_re, phazor_init_im, last_conv_re, last_conv_im):
            length = x.shape[1]
            phazor_raw = phazor_re + 1j * phazor_im
            mag = jnp.abs(phazor_raw)
            phazor = phazor_raw / mag * jnp.exp(-mag)
            t = jnp.arange(length)[:, None]
            prog = jnp.power(phazor[None, :], t)
            phazor_init = phazor_init_re + 1j * phazor_init_im
            filt = prog * phazor_init[None, :]
            filt_fft = jnp.fft.fft(filt, n=2 * length, axis=0)
            x_fft = jnp.fft.fft(x.astype(jnp.complex64), n=2 * length, axis=1)
            conv = jnp.fft.ifft(filt_fft[None] * x_fft, axis=1)[:, :length]
            last_conv = last_conv_re + 1j * last_conv_im
            last_conv = jax.lax.stop_gradient(last_conv)
            conv_with_past = conv + last_conv[None, None, :] * prog[None] * phazor[None, None, :]
            return conv_with_past.real
        h = _layernorm(x, ln_gamma, ln_beta)
        h = _spiral_conv(h, phazor_re, phazor_im, phazor_init_re, phazor_init_im, last_conv_re, last_conv_im)
        x1 = h + x
        h = _layernorm(x1, ln_gamma, ln_beta)
        h = jax.nn.silu(h @ w1 + b1) @ w2 + b2
        return h + x1

    def _L1_ffn_ref(x, CB, SCB, bias):
        import jax, jax.numpy as jnp
        import numpy as np
        B, S, K, N = (8, 2048, 256, 256)
        out = jnp.einsum('bsk,nk->bsn', x, CB)
        out = out * (SCB * (1.0 / 127.0)) + bias
        return out
    h = _L0_tok_ref(x, L0_tok_conv_w, L0_tok_conv_b, L0_tok_proj_w, L0_tok_proj_b, L0_tok_ln_g, L0_tok_ln_b, L0_tok_pos_table)
    h = h + _L0_attn_ref(_layernorm(h, axis=-1), L0_attn_Wq, L0_attn_bq, L0_attn_Wk1, L0_attn_bk1, L0_attn_Wk2, L0_attn_bk2, L0_attn_Wv1, L0_attn_bv1, L0_attn_Wv2, L0_attn_bv2, L0_attn_g1, L0_attn_g2, L0_attn_g3, L0_attn_g4, L0_attn_ln_g, L0_attn_ln_b, L0_attn_Wo, L0_attn_bo)
    h = h + _L0_ffn_ref(_layernorm(h, axis=-1), L0_ffn_w_router, L0_ffn_w_block)
    h = h + _L1_attn_ref(_layernorm(h, axis=-1), L1_attn_ln_gamma, L1_attn_ln_beta, L1_attn_phazor_re, L1_attn_phazor_im, L1_attn_phazor_init_re, L1_attn_phazor_init_im, L1_attn_last_conv_re, L1_attn_last_conv_im, L1_attn_w1, L1_attn_b1, L1_attn_w2, L1_attn_b2)
    h = h + _L1_ffn_ref(_layernorm(h, axis=-1), L1_ffn_CB, L1_ffn_SCB, L1_ffn_bias)
    return h

_drawn_inputs = setup_inputs


def setup_inputs(seed=0):
    import zlib

    import numpy as np

    out = dict(_drawn_inputs(seed))
    spreads = {'L0_tok_ln_g': (1.0, 0.2),
     'L0_tok_ln_b': (0.0, 0.1),
     'L0_attn_bq': (0.0, 0.8),
     'L0_attn_bk1': (0.0, 0.8),
     'L0_attn_bk2': (0.0, 0.8),
     'L0_attn_bv1': (0.0, 0.273),
     'L0_attn_bv2': (0.0, 0.436),
     'L0_attn_ln_g': (1.0, 0.2),
     'L0_attn_ln_b': (0.0, 0.287),
     'L0_attn_bo': (0.0, 0.1),
     'L1_attn_ln_gamma': (1.0, 0.2),
     'L1_attn_ln_beta': (0.0, 0.1),
     'L1_attn_b1': (0.0, 0.633),
     'L1_attn_b2': (0.0, 0.1)}
    factors = {'L0_tok_conv_b': 6.153,
     'L0_tok_proj_b': 3.757,
     'L0_attn_Wk2': 3.2,
     'L1_ffn_bias': 23.232,
     'L0_tok_pos_table': 3.095,
     'L0_attn_Wk1': 2.683}
    for name, (base, spread) in spreads.items():
        noise = np.random.default_rng([zlib.crc32(name.encode()), seed]).standard_normal(out[name].shape)
        drawn = base * np.exp(spread * noise) if base else spread * noise
        out[name] = jnp.asarray(drawn.astype(out[name].dtype))
    for name, factor in factors.items():
        out[name] = (out[name] * factor).astype(out[name].dtype)
    return out
```

```python
from contextlib import ExitStack

import concourse.bass as bass
from concourse import mybir

F32 = mybir.dt.float32
ALU = mybir.AluOpType
ACT = mybir.ActivationFunctionType
AX = mybir.AxisListType

P = 128
EPS = 1e-5

_INS = ['x', 'L0_tok_conv_w', 'L0_tok_conv_b', 'L0_tok_proj_w', 'L0_tok_proj_b', 'L0_tok_ln_g', 'L0_tok_ln_b',
        'L0_tok_pos_table', 'L0_attn_Wq', 'L0_attn_bq', 'L0_attn_Wk1', 'L0_attn_bk1', 'L0_attn_Wk2', 'L0_attn_bk2',
        'L0_attn_Wv1', 'L0_attn_bv1', 'L0_attn_Wv2', 'L0_attn_bv2', 'L0_attn_g1', 'L0_attn_g2', 'L0_attn_g3',
        'L0_attn_g4', 'L0_attn_ln_g', 'L0_attn_ln_b', 'L0_attn_Wo', 'L0_attn_bo', 'L0_ffn_w_router',
        'L0_ffn_w_block', 'L1_attn_ln_gamma', 'L1_attn_ln_beta', 'L1_attn_phazor_re', 'L1_attn_phazor_im',
        'L1_attn_phazor_init_re', 'L1_attn_phazor_init_im', 'L1_attn_last_conv_re', 'L1_attn_last_conv_im',
        'L1_attn_w1', 'L1_attn_b1', 'L1_attn_w2', 'L1_attn_b2', 'L1_ffn_CB', 'L1_ffn_SCB', 'L1_ffn_bias']


def build_tower(nc, a, out):
    NSEQ, NFRAME, D = a['x'].shape
    KB = a['L0_tok_conv_w'].shape[2]
    NB = -(-NFRAME // KB)
    LAST = NFRAME - (NB - 1) * KB
    HEADS = a['L0_attn_g1'].shape[0]
    FF = a['L1_attn_w1'].shape[1]
    DH = D // P
    TILES = NSEQ * NB // P
    SEQ = P // NB
    PAIRS = TILES // 2
    QUADS = KB * DH // 4
    FC = FF // P
    TOPK = max(1, int(NB * 0.75))
    N = NSEQ * NB
    assert (D, KB, NB, TILES, HEADS) == (256, 16, 8, 4, 16)

    ctx = ExitStack()
    with ctx:
        def sb(name, shape):
            return ctx.enter_context(nc.sbuf_tensor(name, shape, F32))

        def sem(name):
            return ctx.enter_context(nc.semaphore(name))

        psA = ctx.enter_context(nc.psum_tensor("psA", [P, 4, 512], F32))
        psB = ctx.enter_context(nc.psum_tensor("psB", [P, 4, 512], F32))

        region_x = sb("region_x", [P, KB * D])
        region_xT = sb("region_xT", [P, 2 * KB * D])
        region_wT = sb("region_wT", [P, KB * DH * D])
        region_raw = sb("region_raw", [P, DH * KB * D])
        x_in = region_x[:, :].rearrange("p (k d) -> p k d", k=KB)
        xT = region_xT[:, :].rearrange("p (s k f) -> p s k f", s=2, k=KB)
        wT = region_wT[:, :].rearrange("p (k h o) -> p k h o", k=KB, h=DH)
        conv_raw = region_raw[:, :].rearrange("p (o d k) -> p o d k", o=DH, k=KB)
        centred = region_raw[:, 0:KB * D].rearrange("p (k f) -> p k f", k=KB)
        SMALL = ['L0_attn_Wq', 'L0_attn_Wk1', 'L0_attn_Wv1', 'L0_attn_Wk2', 'L0_attn_Wv2', 'L0_attn_Wo', 'L1_ffn_CB']
        small_raw = region_raw[:, KB * D:KB * D + 7 * 512].rearrange("p (w o i) -> p w o i", w=7, o=DH)

        h = region_raw[:, 0:1024].rearrange("p (t f) -> p t f", t=4)
        haux = region_raw[:, 1024:2048].rearrange("p (t f) -> p t f", t=4)
        u = region_raw[:, 2048:3072].rearrange("p (t f) -> p t f", t=4)
        y = region_raw[:, 3072:4096].rearrange("p (t f) -> p t f", t=4)
        vmix = region_raw[:, 4608:6656].rearrange("p (t v f) -> p t v f", t=4, v=2)
        lastT = region_raw[:, 4096:4352].rearrange("p (h b n) -> p h b n", h=DH, n=NB)

        w1 = region_x[:, 0:DH * FF].rearrange("p (h f) -> p h f", h=DH)
        w2 = region_x[:, DH * FF:DH * FF + FC * D].rearrange("p (c d) -> p c d", c=FC)
        kv = region_xT[:, 0:4096].rearrange("p (t f) -> p t f", t=4)
        gT = region_xT[:, 0:4096].rearrange("p (c n) -> p c n", c=FC)
        vx = region_xT[:, 4096:8192].rearrange("p (v b f) -> p v b f", v=4, b=4)
        g_act = region_wT[:, 0:1024].rearrange("p (t f) -> p t f", t=4)
        uT = region_wT[:, 1024:2048].rearrange("p (h n) -> p h n", h=DH)
        qT = region_wT[:, 2048:3072].rearrange("p (h n) -> p h n", h=DH)
        qaT = region_wT[:, 3072:4096].rearrange("p (h n) -> p h n", h=DH)
        s12 = region_wT[:, 4096:6144].rearrange("p (s r f) -> p s r f", s=2, r=4)
        smix = region_wT[:, 6144:8192].rearrange("p (s r f) -> p s r f", s=2, r=4)

        comb = sb("comb", [P, 3 * DH, N])
        conv_tok = sb("conv_tok", [P, TILES, D])
        proj_raw = sb("proj_raw", [P, DH, 3 * D])
        projT = sb("projT", [P, 3 * DH, D])
        wqT = sb("wqT", [P, DH, D])
        wkvT = sb("wkvT", [P, DH, 4 * D])
        woT = sb("woT", [P, DH, D])
        cbT = sb("cbT", [P, DH, D])
        wblk = sb("wblk", [P, DH, D])
        diagF = sb("diagF", [P, DH, NB, P])
        negmean = sb("negmean", [P, D])
        ROWS = ['L0_tok_proj_b', 'L0_tok_ln_g', 'L0_tok_ln_b', 'L0_attn_bk1', 'L0_attn_bv1', 'L0_attn_bk2',
                'L0_attn_bv2', 'L0_attn_bo', 'L0_ffn_w_router', 'L1_attn_b2', 'L1_ffn_SCB', 'L1_ffn_bias']
        rows = sb("rows", [P, len(ROWS), D])
        g13 = sb("g13", [P, 2, D])
        pos = sb("pos", [P, D])
        COLS = ['L0_attn_bq', 'L0_tok_conv_b', 'L0_attn_ln_g', 'L0_attn_ln_b', 'L1_attn_ln_gamma',
                'L1_attn_ln_beta', 'L1_attn_phazor_re', 'L1_attn_phazor_im', 'L1_attn_phazor_init_re',
                'L1_attn_phazor_init_im', 'L1_attn_last_conv_re', 'L1_attn_last_conv_im']
        NCOL = len(COLS) + FF // D
        colrow = sb("colrow", [NCOL, D])
        QCOLS = ['L0_attn_bq', 'L0_attn_g2', 'L0_attn_g4']
        NQ = len(QCOLS)
        gq = sb("gq", [NQ, HEADS])
        g13_raw = sb("g13_raw", [P, 2, HEADS])
        colrowq = sb("colrowq", [NQ, D])
        col = sb("col", [P, DH, NCOL])
        colq = sb("colq", [P, DH, NQ])
        last_tok = sb("last_tok", [P, D])
        ident = sb("ident", [P, P])
        ident2 = sb("ident2", [P, 512])
        ones = sb("ones", [P, P])
        seq16 = sb("seq16", [P, SEQ])
        same_seq = sb("same_seq", [P, P])
        before = sb("before", [P, P])
        head8 = sb("head8", [P, 8])
        mask_seq = sb("mask_seq", [P, 4])
        mask_head = sb("mask_head", [P, 2])
        mask_head64 = sb("mask_head64", [P, 2])
        slot = sb("slot", [P, NB])
        slot_lt = sb("slot_lt", [P, NB])
        eps = sb("eps", [P, 1])
        pw = sb("pw", [P, 2, NB + 1, DH])
        pt = sb("pt", [P, 4, NB, DH])
        filt = sb("filt", [P, NB, DH])
        lastf = sb("lastf", [P, NB, DH])
        mag = sb("mag", [P, 6, DH])
        st = sb("st", [P, TILES, 6])
        mv = sb("mv", [P, TILES, 2])
        sd = sb("sd", [P, TILES])
        rs = sb("rs", [P, TILES])
        score = sb("score", [P, TILES])
        sc_rhs = sb("sc_rhs", [P, TILES, NB])
        sc_t = sb("sc_t", [P, 4, TILES, NB])
        sc_self = sb("sc_self", [P, TILES])
        rank = sb("rank", [P, TILES])
        sel = sb("sel", [P, 2, TILES])

        R = {n: rows[:, j, :] for j, n in enumerate(ROWS)}
        kv_bias = rows[:, 3:7, :].rearrange("p a f -> p (a f)")

        def vec(name, half):
            return col[:, half, COLS.index(name):COLS.index(name) + 1]

        def vecq(name, half):
            return colq[:, half, QCOLS.index(name):QCOLS.index(name) + 1]

        def by_query(ap):
            return ap.rearrange("p (c q i) -> p c q i", q=2, i=32)

        def from_query(ap):
            return ap.rearrange("p (q c i) -> p c q i", q=2, i=32)

        def both(name):
            return col[:, :, COLS.index(name)]

        cols_in, rows_in, raw_in, late_in = sem("cols_in"), sem("rows_in"), sem("raw_in"), sem("late_in")
        conv_w_in = [sem(f"conv_w_in{n}") for n in range(4)]
        x_in_half = [sem("x_in_lo"), sem("x_in_hi")]
        out_stored = sem("out_stored")
        pool_step, masks_made, consts_made = sem("pool_step"), sem("masks_made"), sem("consts_made")
        x_pad_zero = sem("x_pad_zero")
        colrowq_made = sem("colrowq_made")
        cols_T, dve_step, mag2_made, mag_made, decay_made = (sem(n) for n in (
            "cols_T", "dve_step", "mag2_made", "mag_made", "decay_made"))
        filt_made, diag_made, last_rep = sem("filt_made"), sem("diag_made"), sem("last_rep")
        w_T, w_evac_dve = sem("w_T"), sem("w_evac_dve")
        quad_T = sem("quad_T")
        ring_drained = sem("ring_drained")
        conv_bank_free = sem("conv_bank_free")
        conv_done = sem("conv_done")
        negsum, mean_made = sem("negsum"), sem("mean_made")
        max_done = sem("max_done")
        centred_done = sem("centred_done")
        squared, ssq_done = sem("squared"), sem("ssq_done")
        small_T, small_evac = sem("small_T"), sem("small_evac")
        std_made, conv_T, conv_comb = sem("std_made"), sem("conv_T"), sem("conv_comb")
        proj_done, proj_biased = sem("proj_done"), sem("proj_biased")
        ln_stat, ln_mv, ln_sd, ln_rs = sem("ln_stat"), sem("ln_mv"), sem("ln_sd"), sem("ln_rs")
        tok_scaled, tok_out, bpos_made = sem("tok_scaled"), sem("tok_out"), sem("bpos_made")
        ln_out = sem("ln_out")
        trans_done, trans_evac = sem("trans_done"), sem("trans_evac")
        kv_done, kv_biased = sem("kv_done"), sem("kv_biased")
        q_done, q_out, qa_out = sem("q_done"), sem("q_out"), sem("qa_out")
        vsum_done, vscaled, vmixed = sem("vsum_done"), sem("vscaled"), sem("vmixed")
        vx_plain, vx_mixed = sem("vx_plain"), sem("vx_mixed")
        s_done, s1_masked, s12_made = sem("s_done"), sem("s1_masked"), sem("s12_made")
        smix_done, smix_masked = sem("smix_done"), sem("smix_masked")
        y_done, y_step, y_made = sem("y_done"), sem("y_step"), sem("y_made")
        hbo_made, wo_done, h1_made = sem("hbo_made"), sem("wo_done"), sem("h1_made")
        score_made, score_rhs, score_all, sel_made = (sem(n) for n in ("score_made", "score_rhs", "score_all", "sel_made"))
        blk_done, gelu_done, kept, h2_made = sem("blk_done"), sem("gelu_done"), sem("kept"), sem("h2_made")
        u_last, spiral_done, x1_made, hx_made = sem("u_last"), sem("spiral_done"), sem("x1_made"), sem("hx_made")
        last_tok_made = sem("last_tok_made")
        filt_conv, filt_out = sem("filt_conv"), sem("filt_out")
        w1_done, silu_done, w2_done, h3_made = sem("w1_done"), sem("silu_done"), sem("w2_done"), sem("h3_made")
        hb_made, cb_done, cb_scaled, out_made = sem("hb_made"), sem("cb_done"), sem("cb_scaled"), sem("out_made")

        T_ATTN, T_WO, T_FFN, T_SPIRAL, T_MLP, T_CB = range(6)
        LN_TOK, LN_ATTN, LN_Y, LN_FFN, LN_L1, LN_SPIRAL, LN_MLP, LN_CB = range(8)
        def ln_outs(k, pr):
            return 2 * (k - 1) + pr + 1

        block = ctx.enter_context(nc.Block())

        @block.sync
        def _(sp):
            for j, name in enumerate(COLS):
                sp.dma_start(colrow[j:j + 1, :], a[name].rearrange("(a d) -> a d", a=1)).then_inc(cols_in, 16)
            for j, name in enumerate(('L0_attn_g2', 'L0_attn_g2', 'L0_attn_g4')):
                sp.dma_start(gq[j:j + 1, :], a[name].rearrange("(a d) -> a d", a=1)).then_inc(cols_in, 16)
            sp.dma_start(colrow[len(COLS):NCOL, :], a['L1_attn_b1'].rearrange("(a d) -> a d", d=D)).then_inc(cols_in, 16)
            for n in range(4):
                dh, oh = divmod(n, 2)
                sp.dma_start(conv_raw[:, oh, dh * P:(dh + 1) * P, :],
                             a['L0_tok_conv_w'][oh * P:(oh + 1) * P, dh * P:(dh + 1) * P, :]).then_inc(conv_w_in[n], 16)

            def load_x(i, half):
                k0, k1 = half * KB // 2, (half + 1) * KB // 2
                for nb in range(NB):
                    ke = k1 if nb < NB - 1 else min(k1, LAST)
                    sp.dma_start(x_in[nb * SEQ:(nb + 1) * SEQ, k0:ke, :],
                                 a['x'][bass.ds(i * SEQ, SEQ), nb * KB + k0:nb * KB + ke, :]).then_inc(x_in_half[half], 16)

            sp.wait_ge(x_pad_zero, 1)
            load_x(0, 0)
            load_x(0, 1)
            for j, name in enumerate(ROWS):
                sp.dma_start(rows[:, j, :], a[name].partition_broadcast(P)).then_inc(rows_in, 16)
            for j, name in enumerate(('L0_attn_g1', 'L0_attn_g3')):
                sp.dma_start(g13_raw[:, j, :], a[name].partition_broadcast(P)).then_inc(rows_in, 16)
            for b in range(SEQ):
                sp.dma_start(pos[b * NB:(b + 1) * NB, :], a['L0_tok_pos_table'][0:NB, :]).then_inc(rows_in, 16)
            sp.dma_start(proj_raw[:, :, :], a['L0_tok_proj_w'].rearrange("(o p) i -> p o i", p=P)).then_inc(raw_in, 16)
            sp.dma_start(wblk[:, :, :], a['L0_ffn_w_block'].rearrange("(c p) e -> p c e", p=P)).then_inc(raw_in, 16)
            sp.wait_ge(w_T, 16)
            for j, name in enumerate(SMALL):
                sp.dma_start(small_raw[:, j, :, :], a[name].rearrange("(o p) i -> p o i", p=P)).then_inc(raw_in, 16)
            with sp.Fori(1, TILES) as i:
                for half in range(2):
                    sp.wait_ge(quad_T, i * QUADS - QUADS // 2 + half * (QUADS // 2))
                    load_x(i, half)
            sp.wait_ge(quad_T, TILES * QUADS)
            sp.dma_start(w1, a['L1_attn_w1'].rearrange("(c p) f -> p c f", p=P)).then_inc(late_in, 16)
            sp.dma_start(w2, a['L1_attn_w2'].rearrange("(c p) d -> p c d", p=P)).then_inc(late_in, 16)
            out_v = out.rearrange("b n d -> (b n) d").rearrange("(t p) d -> p t d", p=P)
            for pr in range(PAIRS):
                sp.wait_ge(out_made, pr + 1)
                sp.dma_start(out_v[:, 2 * pr:2 * pr + 2, :], h[:, 2 * pr:2 * pr + 2, :]).then_inc(out_stored, 16)
            sp.wait_ge(out_stored, 16 * PAIRS)

        @block.gpsimd
        def _(pool):
            steps = [0]

            def step(ins):
                steps[0] += 1
                ins.then_inc(pool_step, 1)
                pool.wait_ge(pool_step, steps[0])

            k_lo = LAST
            nc.gpsimd.memset(x_in[96:P, k_lo:KB, :], 0.0).then_inc(x_pad_zero, 1)
            pool.wait_ge(x_pad_zero, 1)
            nc.gpsimd.memset(ones[:, :], 1.0)
            nc.gpsimd.memset(eps[:, :], EPS)
            step(nc.gpsimd.memset(ident2[:, :], 0.0))
            step(nc.gpsimd.affine_select(out=ident[:, :], in_=ones[:, :], compare_op=ALU.is_equal, fill=0.0, base=0,
                                         pattern=[[-1, P]], channel_multiplier=1))
            step(nc.gpsimd.affine_select(out=seq16[:, :], in_=ones[:, 0:SEQ], compare_op=ALU.is_ge, fill=0.0, base=0,
                                         pattern=[[-NB, SEQ]], channel_multiplier=1))
            step(nc.gpsimd.affine_select(out=seq16[:, :], in_=seq16[:, :], compare_op=ALU.is_ge, fill=0.0, base=NB - 1,
                                         pattern=[[NB, SEQ]], channel_multiplier=-1))
            step(nc.gpsimd.affine_select(out=head8[:, :], in_=ones[:, 0:8], compare_op=ALU.is_ge, fill=0.0, base=0,
                                         pattern=[[-16, 8]], channel_multiplier=1))
            step(nc.gpsimd.affine_select(out=head8[:, :], in_=head8[:, :], compare_op=ALU.is_ge, fill=0.0, base=15,
                                         pattern=[[16, 8]], channel_multiplier=-1))
            step(nc.gpsimd.tensor_copy(same_seq[:, :].rearrange("p (b n) -> p b n", n=NB),
                                       seq16[:, :].unsqueeze(2).to_broadcast([P, SEQ, NB])))
            step(nc.gpsimd.affine_select(out=before[:, :], in_=same_seq[:, :], compare_op=ALU.is_gt, fill=0.0, base=0,
                                         pattern=[[-1, P]], channel_multiplier=1))
            nc.gpsimd.tensor_copy(ident2[:, 0:P], ident[:, :])
            nc.gpsimd.tensor_copy(ident2[:, 3 * P:4 * P], ident[:, :]).then_inc(consts_made, 1)

            nc.gpsimd.memset(negmean[:, 0:1], 0.0).then_inc(centred_done, 1)
            pool.wait_ge(centred_done, 1)
            nc.gpsimd.memset(negmean[:, 1:2], 0.0).then_inc(centred_done, 1)
            def centre(i):
                pool.wait_ge(mean_made, i + 1)
                nc.gpsimd.tensor_tensor(out=centred[:, :, :],
                                        in0=xT[:, bass.ds(i % 2, 1), :, :].rearrange("p s k f -> p (s k) f"),
                                        in1=negmean[:, :].unsqueeze(1).to_broadcast([P, KB, D]),
                                        op=ALU.add).then_inc(centred_done, 1)

            centre(0)
            with pool.Fori(1, TILES) as i:
                pool.wait_ge(ssq_done, i)
                centre(i)
            pool.wait_ge(filt_made, 1)
            for dh in range(DH):
                for t in range(NB):
                    last = nc.gpsimd.tensor_scalar(diagF[:, dh, t, :], ident[:, :], filt[:, t, dh:dh + 1], None, ALU.mult)
            last.then_inc(diag_made, 1)
            pool.wait_ge(small_T, 10)
            for dh in range(DH):
                last = nc.gpsimd.tensor_copy(lastT[:, dh, :, :],
                                             lastf[:, :, dh].unsqueeze(1).to_broadcast([P, SEQ, NB]))
            last.then_inc(last_rep, 1)
            pool.wait_ge(rows_in, 16 * (len(ROWS) + 2 + SEQ))
            nc.gpsimd.tensor_tensor(out=pos[:, :], in0=pos[:, :], in1=R['L0_tok_ln_b'], op=ALU.add).then_inc(bpos_made, 1)

            def row2(name):
                return R[name].unsqueeze(1).to_broadcast([P, 2, D])

            def pair(buf, pr):
                return buf[:, 2 * pr:2 * pr + 2, :]

            for pr in range(PAIRS):
                pool.wait_ge(tok_out, pr + 1)
                nc.gpsimd.tensor_tensor(out=pair(haux, pr), in0=pair(h, pr), in1=row2('L0_attn_bo'), op=ALU.add).then_inc(hbo_made, 1)
            for pr in range(PAIRS):
                pool.wait_ge(ln_out, ln_outs(LN_L1, pr))
                pool.wait_ge(last_tok_made, 1)
                nc.gpsimd.tensor_tensor(out=pair(g_act, pr), in0=pair(u, pr),
                                        in1=last_tok[:, :].unsqueeze(1).to_broadcast([P, 2, D]), op=ALU.add).then_inc(u_last, 1)
            for pr in range(PAIRS):
                nc.gpsimd.tensor_tensor(out=pair(haux, pr), in0=pair(h, pr), in1=row2('L1_attn_b2'), op=ALU.add).then_inc(hx_made, 1)
                pool.wait_ge(hx_made, 2 * pr + 1)
                pool.wait_ge(x1_made, pr + 1)
                nc.gpsimd.tensor_tensor(out=pair(haux, pr), in0=pair(haux, pr), in1=pair(y, pr), op=ALU.add).then_inc(hx_made, 1)
            for pr in range(PAIRS):
                pool.wait_ge(h3_made, pr + 1)
                nc.gpsimd.tensor_tensor(out=pair(haux, pr), in0=pair(h, pr), in1=row2('L1_ffn_bias'), op=ALU.add).then_inc(hb_made, 1)

        @block.scalar
        def _(act):
            for n, (dst, nv) in enumerate(((col, NCOL), (colq, NQ))):
                act.wait_ge(cols_T, n + 1)
                nc.scalar.activation(dst[:, :, :], psA[:, n, 0:DH * nv].rearrange("p (h c) -> p h c", h=DH),
                                     ACT.Copy).then_inc(conv_bank_free, 1)
            act.wait_ge(mag2_made, 1)
            nc.scalar.activation(mag[:, 1, :], mag[:, 0, :], ACT.Sqrt).then_inc(mag_made, 1)
            act.wait_ge(mag_made, 1)
            nc.scalar.activation(mag[:, 2, :], mag[:, 1, :], ACT.Exp, scale=-1.0).then_inc(decay_made, 1)
            for n in [0, 2, 4, 6, 8, 10, 12, 13, 14, 15]:
                act.wait_ge(w_T, n + 1)
                dh, kk = divmod(n, 8)
                ins = nc.scalar.activation(wT[:, 2 * kk:2 * kk + 2, dh, :],
                                           psB[:, n % 4, :].rearrange("p (k o) -> p k o", k=2), ACT.Copy)
                ins.then_inc(ring_drained if n >= 12 else small_evac, 1)

            def tile_a(i):
                act.wait_ge(max_done, i + 1)
                act.wait_ge(centred_done, i + 1)
                for q in range(QUADS):
                    act.wait_ge(quad_T, i * QUADS + q + 1)
                    nc.scalar.activation(
                        xT[:, bass.ds(i % 2, 1), 2 * q:2 * q + 2, :].rearrange("p s k (h b n) -> p (s k h) b n", h=DH, n=NB),
                        psB[:, q % 4, :].rearrange("p (g n b) -> p g b n", g=4, n=NB), ACT.Copy).then_inc(ring_drained, 1)

            def conv_out(i):
                act.wait_ge(conv_done, i + 1)
                nc.scalar.activation(conv_tok[:, bass.ds(i, 1), :].rearrange("p s f -> p (s f)"),
                                     psA[:, bass.ds(i % 2, 1), 0:D].rearrange("p s f -> p (s f)"), ACT.Copy).then_inc(conv_bank_free, 1)

            def square(i):
                act.wait_ge(centred_done, i + 3)
                for n in range(2):
                    piece = centred[:, n * KB // 2:(n + 1) * KB // 2, :]
                    nc.scalar.activation(piece, piece, ACT.Square).then_inc(squared, 1)

            tile_a(0)
            with act.Fori(1, TILES) as i:
                tile_a(i)
                conv_out(i - 1)
                square(i - 1)
            conv_out(TILES - 1)

            def evac(dst, bank):
                nc.scalar.activation(dst, bank, ACT.Copy).then_inc(small_evac, 1)

            act.wait_ge(small_T, 1)
            evac(woT[:, :, :], psB[:, 0, :].rearrange("p (h o) -> p h o", h=DH))
            act.wait_ge(small_T, 2)
            evac(cbT[:, :, :], psB[:, 1, :].rearrange("p (h o) -> p h o", h=DH))
            for n in range(3):
                act.wait_ge(small_T, 3 + n)
                evac(projT[:, 2 * n:2 * n + 2, :], psB[:, (2 + n) % 4, :].rearrange("p (c o) -> p c o", c=2))
            square(TILES - 1)
            for hh in range(DH):
                act.wait_ge(conv_T, hh + 1)
                nc.scalar.activation(comb[:, hh, :], psA[:, 2 + hh, :], ACT.Identity, bias=vec('L0_tok_conv_b', hh)).then_inc(conv_comb, 1)
            act.wait_ge(ssq_done, TILES)
            nc.scalar.activation(comb[:, DH:2 * DH, :], comb[:, DH:2 * DH, :], ACT.Sqrt, scale=1.0 / (KB - 1)).then_inc(std_made, 1)

            def ln_sqrt(k, pr):
                act.wait_ge(ln_mv, 4 * k + 2 * pr + 2)
                nc.scalar.activation(sd[:, 2 * pr:2 * pr + 2], mv[:, 2 * pr:2 * pr + 2, 1], ACT.Sqrt, bias=eps[:, 0:1]).then_inc(ln_sd, 1)

            def evac_T(s, pr, scale=None, bias=None):
                act.wait_ge(trans_done, 2 * s + pr + 1)
                src = psB[:, pr, :].rearrange("p (h n) -> p h n", h=DH)
                if scale is None:
                    nc.scalar.activation(uT[:, :, 256 * pr:256 * pr + 256], src, ACT.Copy).then_inc(trans_evac, 1)
                    return
                for hh in range(DH):
                    last = nc.scalar.activation(uT[:, hh, 256 * pr:256 * pr + 256], src[:, hh, :], ACT.Identity, scale=vec(scale, hh), bias=vec(bias, hh))
                last.then_inc(trans_evac, 1)

            for pr in range(PAIRS):
                ln_sqrt(LN_TOK, pr)
            for pr in range(PAIRS):
                ln_sqrt(LN_ATTN, pr)
            for pr in range(PAIRS):
                evac_T(T_ATTN, pr)
            for hh in range(2):
                act.wait_ge(q_done, hh + 1)
                nc.scalar.activation(qT[:, hh, :], psB[:, hh, :], ACT.Identity, bias=vecq('L0_attn_bq', hh)).then_inc(q_out, 1)
                act.wait_ge(q_out, hh + 1)
                nc.scalar.activation(qaT[:, hh, :], qT[:, hh, :], ACT.Identity, scale=vecq('L0_attn_g4', hh), bias=vecq('L0_attn_g2', hh)).then_inc(qa_out, 1)

            def expand_plain(t):
                act.wait_ge(kv_biased, 2 * t + 2)
                if t >= 1:
                    act.wait_ge(s_done, t)
                vv = kv[:, t, :].rearrange("p (a b f) -> p a b f", a=2, b=2)[:, :, 1, :]
                for j in range(4):
                    last = nc.scalar.activation(vx[:, 0:2, j, :], vv, ACT.Copy, scale=mask_seq[:, j:j + 1])
                last.then_inc(vx_plain, 1)

            def head_masked(dst, ps, cols, mask):
                d = dst.rearrange("p r (g m e) -> p r g m e", m=2, e=16)
                s = ps[:, :, cols:cols + 256].rearrange("p r (g m e) -> p r g m e", m=2, e=16)
                for m in range(2):
                    last = nc.scalar.activation(d[:, :, :, m, :], s[:, :, :, m, :], ACT.Copy, scale=mask[:, m:m + 1])
                return last

            for t in range(TILES):
                expand_plain(t)
                act.wait_ge(s_done, t + 1)
                if t >= 2:
                    act.wait_ge(y_done, t - 1)
                ps_s, ps_m = (psA, psB) if (3 * t) % 2 == 0 else (psB, psA)
                head_masked(s12[:, t % 2], ps_s, 0, mask_head64).then_inc(s1_masked, 1)
                act.wait_ge(smix_done, t + 1)
                head_masked(smix[:, t % 2], ps_m, 0, mask_head).then_inc(smix_masked, 1)

            for pr in range(PAIRS):
                ln_sqrt(LN_Y, pr)
            for pr in range(PAIRS):
                evac_T(T_WO, pr, 'L0_attn_ln_g', 'L0_attn_ln_b')
            for pr in range(PAIRS):
                ln_sqrt(LN_FFN, pr)
            for pr in range(PAIRS):
                evac_T(T_FFN, pr)
            for pr in range(PAIRS):
                act.wait_ge(blk_done, pr + 1)
                nc.scalar.activation(g_act[:, 2 * pr:2 * pr + 2, :], psA[:, pr, :].rearrange("p (t f) -> p t f", t=2),
                                     ACT.Gelu_apprx_tanh).then_inc(gelu_done, 1)
            for pr in range(PAIRS):
                ln_sqrt(LN_L1, pr)
            for pr in range(PAIRS):
                ln_sqrt(LN_SPIRAL, pr)
            for pr in range(PAIRS):
                evac_T(T_SPIRAL, pr, 'L1_attn_ln_gamma', 'L1_attn_ln_beta')
            for pr in range(PAIRS):
                act.wait_ge(filt_conv, pr + 1)
                nc.scalar.activation(qT[:, :, 256 * pr:256 * pr + 256], psA[:, 2 + pr, :].rearrange("p (h n) -> p h n", h=DH),
                                     ACT.Copy).then_inc(filt_out, 1)
            for pr in range(PAIRS):
                ln_sqrt(LN_MLP, pr)
            for pr in range(PAIRS):
                evac_T(T_MLP, pr, 'L1_attn_ln_gamma', 'L1_attn_ln_beta')
            for c in range(FC):
                act.wait_ge(w1_done, c + 1)
                cc = len(COLS) + c // 2
                nc.scalar.activation(gT[:, c, :], psA[:, c % 4, :], ACT.Silu, bias=col[:, c % 2, cc:cc + 1]).then_inc(silu_done, 1)
            for pr in range(PAIRS):
                ln_sqrt(LN_CB, pr)
            for pr in range(PAIRS):
                evac_T(T_CB, pr)

        @block.vector
        def _(dve):
            steps = [0]

            def step(ins):
                steps[0] += 1
                ins.then_inc(dve_step, 1)
                dve.wait_ge(dve_step, steps[0])

            V = nc.vector
            dve.wait_ge(consts_made, 1)
            V.tensor_reduce(out=mask_seq[:, :], in_=seq16[:, :].rearrange("p (r j) -> p j r", j=4), axis=AX.X, op=ALU.add).then_inc(max_done, 1)
            dve.wait_ge(max_done, 1)
            V.tensor_reduce(out=slot[:, :], in_=ident[:, :].rearrange("p (b n) -> p n b", n=NB), axis=AX.X, op=ALU.add).then_inc(max_done, 1)
            V.tensor_reduce(out=slot_lt[:, :], in_=before[:, :].rearrange("p (b n) -> p n b", n=NB), axis=AX.X, op=ALU.add)
            step(V.tensor_reduce(out=mask_head[:, :], in_=head8[:, :].rearrange("p (c m) -> p m c", m=2), axis=AX.X, op=ALU.add))
            V.tensor_scalar(mask_head64[:, :], mask_head[:, :], 1.0 / (NB * NB), None, ALU.mult).then_inc(masks_made, 1)
            dve.wait_ge(cols_in, 16 * (len(COLS) + NQ + 1))
            for q in range(2):
                last = V.tensor_copy(from_query(colrowq[:, :])[:, :, q, :].rearrange("p c (m e) -> p c m e", m=2),
                                     gq[:, :].rearrange("p (c q m) -> p c q m", q=2, m=2)[:, :, q, :]
                                     .unsqueeze(3).to_broadcast([NQ, 4, 2, D // HEADS]))
            step(last)
            V.tensor_copy(from_query(colrowq[0:1, :]), by_query(colrow[0:1, :])).then_inc(colrowq_made, 1)
            dve.wait_ge(conv_bank_free, 2)
            V.tensor_tensor(out=mag[:, 3, :], in0=both('L1_attn_phazor_re'), in1=both('L1_attn_phazor_re'), op=ALU.mult)
            step(V.tensor_tensor(out=mag[:, 4, :], in0=both('L1_attn_phazor_im'), in1=both('L1_attn_phazor_im'), op=ALU.mult))
            V.tensor_tensor(out=mag[:, 0, :], in0=mag[:, 3, :], in1=mag[:, 4, :], op=ALU.add).then_inc(mag2_made, 1)

            for n in [1, 3, 5, 7, 9, 11]:
                dve.wait_ge(w_T, n + 1)
                dh, kk = divmod(n, 8)
                V.tensor_copy(wT[:, 2 * kk:2 * kk + 2, dh, :], psB[:, n % 4, :].rearrange("p (k o) -> p k o", k=2)).then_inc(w_evac_dve, 1)

            dve.wait_ge(decay_made, 1)
            V.memset(pw[:, 0, 0, :], 1.0)
            V.memset(pw[:, 1, 0, :], 0.0)
            step(V.reciprocal(mag[:, 3, :], mag[:, 1, :]))
            step(V.tensor_tensor(out=mag[:, 4, :], in0=mag[:, 2, :], in1=mag[:, 3, :], op=ALU.mult))
            V.tensor_tensor(out=pw[:, 0, 1, :], in0=both('L1_attn_phazor_re'), in1=mag[:, 4, :], op=ALU.mult)
            step(V.tensor_tensor(out=pw[:, 1, 1, :], in0=both('L1_attn_phazor_im'), in1=mag[:, 4, :], op=ALU.mult))
            for m in (1, 2, 4):
                def low(ri):
                    return pw[:, ri, 1:m + 1, :]

                def top(ri):
                    return pw[:, ri, m:m + 1, :].to_broadcast([P, m, DH])
                V.tensor_tensor(out=pt[:, 0, 0:m, :], in0=low(0), in1=top(0), op=ALU.mult)
                V.tensor_tensor(out=pt[:, 1, 0:m, :], in0=low(1), in1=top(1), op=ALU.mult)
                V.tensor_tensor(out=pt[:, 2, 0:m, :], in0=low(0), in1=top(1), op=ALU.mult)
                step(V.tensor_tensor(out=pt[:, 3, 0:m, :], in0=low(1), in1=top(0), op=ALU.mult))
                V.tensor_tensor(out=pw[:, 0, m + 1:2 * m + 1, :], in0=pt[:, 0, 0:m, :], in1=pt[:, 1, 0:m, :], op=ALU.subtract)
                step(V.tensor_tensor(out=pw[:, 1, m + 1:2 * m + 1, :], in0=pt[:, 2, 0:m, :], in1=pt[:, 3, 0:m, :], op=ALU.add))
            def colb(name):
                return both(name).unsqueeze(1).to_broadcast([P, NB, DH])
            V.tensor_tensor(out=pt[:, 0, :, :], in0=pw[:, 0, 0:NB, :], in1=colb('L1_attn_phazor_init_re'), op=ALU.mult)
            V.tensor_tensor(out=pt[:, 1, :, :], in0=pw[:, 1, 0:NB, :], in1=colb('L1_attn_phazor_init_im'), op=ALU.mult)
            V.tensor_tensor(out=pt[:, 2, :, :], in0=pw[:, 0, 1:NB + 1, :], in1=colb('L1_attn_last_conv_re'), op=ALU.mult)
            step(V.tensor_tensor(out=pt[:, 3, :, :], in0=pw[:, 1, 1:NB + 1, :], in1=colb('L1_attn_last_conv_im'), op=ALU.mult))
            V.tensor_tensor(out=filt[:, :, :], in0=pt[:, 0, :, :], in1=pt[:, 1, :, :], op=ALU.subtract)
            V.tensor_tensor(out=lastf[:, :, :], in0=pt[:, 2, :, :], in1=pt[:, 3, :, :], op=ALU.subtract).then_inc(filt_made, 1)

            def by_token(buf3):
                return buf3.rearrange("p k f -> p f k")

            def slot_xT(i):
                return xT[:, bass.ds(i % 2, 1), :, :].rearrange("p s k f -> p (s f) k")

            def cols_of(chunk, i):
                return comb[:, chunk:chunk + DH, bass.ds(i * P, P)]

            def mean(i):
                dve.wait_ge(ring_drained, 4 + QUADS * i + QUADS)
                dve.wait_ge(centred_done, i + 2)
                V.tensor_reduce(out=negmean[:, :], in_=slot_xT(i), axis=AX.X, op=ALU.add).then_inc(negsum, 1)
                dve.wait_ge(negsum, i + 1)
                V.tensor_scalar(negmean[:, :], negmean[:, :], -1.0 / KB, None, ALU.mult).then_inc(mean_made, 1)

            def maximum(i):
                V.tensor_reduce(out=cols_of(2 * DH, i), in_=slot_xT(i), axis=AX.X, op=ALU.max).then_inc(max_done, 1)

            def sum_squares(i):
                dve.wait_ge(squared, 2 * i + 2)
                V.tensor_reduce(out=cols_of(DH, i), in_=by_token(centred), axis=AX.X, op=ALU.add).then_inc(ssq_done, 1)

            mean(0)
            maximum(0)
            with dve.Fori(1, TILES) as i:
                mean(i)
                sum_squares(i - 1)
                maximum(i)

            for n in range(5):
                dve.wait_ge(small_T, 6 + n)
                if n == 0:
                    for c in range(DH):
                        last = V.tensor_tensor(out=from_query(wqT[:, c, :]), in0=by_query(psB[:, 1, c * D:(c + 1) * D]),
                                               in1=by_query(ident2[:, c * D:(c + 1) * D]), op=ALU.add)
                    last.then_inc(w_evac_dve, 1)
                    continue
                V.tensor_tensor(out=wkvT[:, :, (n - 1) * D:n * D], in0=psB[:, (5 + n) % 4, :].rearrange("p (h o) -> p h o", h=DH),
                                in1=ident2[:, :].rearrange("p (h o) -> p h o", h=DH), op=ALU.add).then_inc(w_evac_dve, 1)
            sum_squares(TILES - 1)
            dve.wait_ge(rows_in, 16 * (len(ROWS) + 2 + SEQ))
            V.tensor_scalar(g13[:, :, :].rearrange("p a (h e) -> p (a h) e", h=HEADS),
                            g13_raw[:, :, :].rearrange("p a h -> p (a h)").unsqueeze(2).to_broadcast([P, 2 * HEADS, D // HEADS]),
                            1.0 / (NB * NB), None, ALU.mult)
            step(V.tensor_scalar(R['L1_ffn_SCB'], R['L1_ffn_SCB'], 1.0 / 127.0, None, ALU.mult))
            dve.wait_ge(cols_T, 3)
            V.tensor_copy(last_tok[:, :], psA[:, 0, 0:D]).then_inc(last_tok_made, 1)

            def stats(k, pr, src):
                for t in (2 * pr, 2 * pr + 1):
                    V.bn_stats(st[:, t, :], src[:, t, :]).then_inc(ln_stat, 1)
                for t in (2 * pr, 2 * pr + 1):
                    dve.wait_ge(ln_stat, 4 * k + t + 1)
                    V.bn_aggr(mv[:, t, :], st[:, t, :]).then_inc(ln_mv, 1)

            def rstd(k, pr):
                dve.wait_ge(ln_sd, 2 * k + pr + 1)
                V.reciprocal(rs[:, 2 * pr:2 * pr + 2], sd[:, 2 * pr:2 * pr + 2]).then_inc(ln_rs, 1)
                dve.wait_ge(ln_rs, 2 * k + pr + 1)

            def normalise(k, pr, src, dst):
                rstd(k, pr)
                for t in (2 * pr, 2 * pr + 1):
                    last = V.tensor_scalar(dst[:, t, :], src[:, t, :], mv[:, t, 0:1], rs[:, t:t + 1], ALU.subtract, ALU.mult)
                last.then_inc(ln_out, 1)

            def pair(buf, pr):
                return buf[:, 2 * pr:2 * pr + 2, :]

            def bank2(bank):
                return bank.rearrange("p (t f) -> p t f", t=2)

            def row2(name):
                return R[name].unsqueeze(1).to_broadcast([P, 2, D])

            for pr in range(PAIRS):
                dve.wait_ge(proj_done, pr + 1)
                V.tensor_tensor(out=pair(y, pr), in0=bank2(psA[:, pr, :]), in1=row2('L0_tok_proj_b'), op=ALU.add).then_inc(proj_biased, 1)
                dve.wait_ge(proj_biased, pr + 1)
                stats(LN_TOK, pr, y)
            dve.wait_ge(bpos_made, 1)
            for pr in range(PAIRS):
                rstd(LN_TOK, pr)
                for t in (2 * pr, 2 * pr + 1):
                    V.scalar_tensor_tensor(out=y[:, t, :], in0=y[:, t, :], scalar=mv[:, t, 0:1], in1=R['L0_tok_ln_g'],
                                           op0=ALU.subtract, op1=ALU.mult).then_inc(tok_scaled, 1)
                for t in (2 * pr, 2 * pr + 1):
                    dve.wait_ge(tok_scaled, t + 1)
                    last = V.scalar_tensor_tensor(out=h[:, t, :], in0=y[:, t, :], scalar=rs[:, t:t + 1], in1=pos[:, :],
                                                  op0=ALU.mult, op1=ALU.add)
                last.then_inc(tok_out, 1)
                dve.wait_ge(tok_out, pr + 1)
                stats(LN_ATTN, pr, h)
            for pr in range(PAIRS):
                normalise(LN_ATTN, pr, h, u)

            def vv(t):
                return kv[:, t, :].rearrange("p (a b f) -> p a b f", a=2, b=2)[:, :, 1, :]
            for t in range(TILES):
                for j in range(2):
                    dve.wait_ge(kv_done, 2 * t + j + 1)
                    V.tensor_tensor(out=kv[:, t, 512 * j:512 * j + 512], in0=psA[:, 2 * (t % 2) + j, :],
                                    in1=kv_bias[:, 512 * j:512 * j + 512], op=ALU.add).then_inc(kv_biased, 1)

            for t in range(TILES):
                dve.wait_ge(vsum_done, t + 1)
                V.tensor_tensor(out=vmix[:, t], in0=bank2(psB[:, 2 + t % 2, :]), in1=g13[:, :, :], op=ALU.mult).then_inc(vscaled, 1)
                dve.wait_ge(vscaled, t + 1)
                V.tensor_tensor(out=vmix[:, t], in0=vmix[:, t], in1=vv(t), op=ALU.mult).then_inc(vmixed, 1)

            def expand_mixed(t):
                dve.wait_ge(vmixed, t + 1)
                if t >= 1:
                    dve.wait_ge(smix_done, t)
                for j in range(4):
                    last = V.tensor_scalar(vx[:, 2:4, j, :], vmix[:, t], mask_seq[:, j:j + 1], None, ALU.mult)
                last.then_inc(vx_mixed, 1)

            for t in range(TILES):
                ps_s, ps_m = (psA, psB) if (3 * t) % 2 == 0 else (psB, psA)
                expand_mixed(t)
                dve.wait_ge(s1_masked, t + 1)
                V.tensor_tensor(out=s12[:, t % 2], in0=s12[:, t % 2], in1=ps_s[:, :, 256:512], op=ALU.mult).then_inc(s12_made, 1)
                dve.wait_ge(y_done, t + 1)
                yv = y[:, t, :].rearrange("p (c i) -> p c i", c=4)
                V.tensor_scalar(yv, ps_s[:, :, 0:64], mask_seq[:, 0:1], None, ALU.mult).then_inc(y_step, 1)
                for j in range(1, 4):
                    dve.wait_ge(y_step, 3 * t + j)
                    ins = V.scalar_tensor_tensor(out=yv, in0=ps_s[:, :, 64 * j:64 * j + 64], scalar=mask_seq[:, j:j + 1],
                                                 in1=yv, op0=ALU.mult, op1=ALU.add)
                    ins.then_inc(y_step if j < 3 else y_made, 1)
            for pr in range(PAIRS):
                dve.wait_ge(y_made, 2 * pr + 2)
                stats(LN_Y, pr, y)
            for pr in range(PAIRS):
                normalise(LN_Y, pr, y, y)
            for pr in range(PAIRS):
                dve.wait_ge(wo_done, pr + 1)
                dve.wait_ge(hbo_made, pr + 1)
                V.tensor_tensor(out=pair(h, pr), in0=bank2(psA[:, pr, :]), in1=pair(haux, pr), op=ALU.add).then_inc(h1_made, 1)
                dve.wait_ge(h1_made, pr + 1)
                stats(LN_FFN, pr, h)
            for pr in range(PAIRS):
                normalise(LN_FFN, pr, h, u)

            dve.wait_ge(ln_out, ln_outs(LN_FFN, 1))
            for t in range(TILES):
                V.scalar_tensor_tensor(out=y[:, t, :], in0=u[:, t, :], scalar=1.0, in1=R['L0_ffn_w_router'],
                                       op0=ALU.mult, op1=ALU.mult, accum_out=score[:, t:t + 1]).then_inc(score_made, 1)
            dve.wait_ge(score_made, TILES)

            def tok4(m):
                return m.unsqueeze(1).to_broadcast([P, TILES, NB])

            def slot4(m):
                return m.unsqueeze(2).to_broadcast([P, TILES, NB])
            V.tensor_tensor(out=sc_rhs[:, :, :], in0=slot4(score[:, :]), in1=tok4(slot[:, :]), op=ALU.mult).then_inc(score_rhs, 1)
            dve.wait_ge(score_all, 1)
            allsc = psA[:, 2, 0:TILES * NB].rearrange("p (t j) -> p t j", t=TILES)
            step(V.tensor_tensor(out=sc_t[:, 0], in0=allsc, in1=tok4(slot[:, :]), op=ALU.mult))
            step(V.tensor_reduce(out=sc_self[:, :], in_=sc_t[:, 0], axis=AX.X, op=ALU.add))
            V.tensor_tensor(out=sc_t[:, 1], in0=allsc, in1=slot4(sc_self[:, :]), op=ALU.is_gt)
            step(V.tensor_tensor(out=sc_t[:, 2], in0=allsc, in1=slot4(sc_self[:, :]), op=ALU.is_equal))
            step(V.tensor_tensor(out=sc_t[:, 2], in0=sc_t[:, 2], in1=tok4(slot_lt[:, :]), op=ALU.mult))
            step(V.tensor_tensor(out=sc_t[:, 1], in0=sc_t[:, 1], in1=sc_t[:, 2], op=ALU.add))
            step(V.tensor_reduce(out=rank[:, :], in_=sc_t[:, 1], axis=AX.X, op=ALU.add))
            V.tensor_scalar(sel[:, 0, :], rank[:, :], TOPK - 0.5, None, ALU.is_lt)
            V.tensor_scalar(sel[:, 1, :], rank[:, :], TOPK - 0.5, None, ALU.is_gt).then_inc(sel_made, 1)
            dve.wait_ge(sel_made, 1)
            for t in range(TILES):
                V.scalar_tensor_tensor(out=h[:, t, :], in0=u[:, t, :], scalar=sel[:, 1, t:t + 1], in1=h[:, t, :],
                                       op0=ALU.mult, op1=ALU.add).then_inc(kept, 1)
            for pr in range(PAIRS):
                dve.wait_ge(gelu_done, pr + 1)
                for t in (2 * pr, 2 * pr + 1):
                    dve.wait_ge(kept, t + 1)
                    V.scalar_tensor_tensor(out=h[:, t, :], in0=g_act[:, t, :], scalar=sel[:, 0, t:t + 1], in1=h[:, t, :],
                                           op0=ALU.mult, op1=ALU.add).then_inc(h2_made, 1)
                dve.wait_ge(h2_made, 2 * pr + 2)
                stats(LN_L1, pr, h)
            for pr in range(PAIRS):
                normalise(LN_L1, pr, h, u)
                dve.wait_ge(ln_out, ln_outs(LN_L1, pr))
                stats(LN_SPIRAL, pr, u)
            for pr in range(PAIRS):
                normalise(LN_SPIRAL, pr, u, y)
            for pr in range(PAIRS):
                dve.wait_ge(spiral_done, pr + 1)
                dve.wait_ge(u_last, pr + 1)
                V.tensor_tensor(out=pair(y, pr), in0=bank2(psA[:, pr, :]), in1=pair(g_act, pr), op=ALU.add).then_inc(x1_made, 1)
                dve.wait_ge(x1_made, pr + 1)
                stats(LN_MLP, pr, y)
            for pr in range(PAIRS):
                normalise(LN_MLP, pr, y, u)
            for pr in range(PAIRS):
                dve.wait_ge(w2_done, pr + 1)
                dve.wait_ge(hx_made, 2 * pr + 2)
                V.tensor_tensor(out=pair(h, pr), in0=bank2(psB[:, 2 + pr, :]), in1=pair(haux, pr), op=ALU.add).then_inc(h3_made, 1)
                dve.wait_ge(h3_made, pr + 1)
                stats(LN_CB, pr, h)
            for pr in range(PAIRS):
                normalise(LN_CB, pr, h, u)
            for pr in range(PAIRS):
                dve.wait_ge(cb_done, pr + 1)
                V.tensor_tensor(out=pair(y, pr), in0=bank2(psA[:, pr, :]), in1=row2('L1_ffn_SCB'), op=ALU.mult).then_inc(cb_scaled, 1)
                dve.wait_ge(cb_scaled, pr + 1)
                dve.wait_ge(hb_made, pr + 1)
                V.tensor_tensor(out=pair(h, pr), in0=pair(y, pr), in1=pair(haux, pr), op=ALU.add).then_inc(out_made, 1)

        @block.tensor
        def _(pe):
            T = nc.tensor.transpose
            M = nc.tensor.matmul
            pe.wait_ge(consts_made, 1)
            pe.wait_ge(cols_in, 16 * (len(COLS) + NQ + 1))
            idc = ident[0:NCOL, 0:NCOL]
            for hh in range(DH):
                last = T(psA[:, 0, hh * NCOL:(hh + 1) * NCOL], colrow[:, hh * P:(hh + 1) * P], idc)
            last.then_inc(cols_T, 1)
            pe.wait_ge(colrowq_made, 1)
            for hh in range(2):
                last = T(psA[:, 1, hh * NQ:(hh + 1) * NQ], colrowq[:, hh * P:(hh + 1) * P], ident[0:NQ, 0:NQ])
            last.then_inc(cols_T, 1)

            for n in range(16):
                dh, kk = divmod(n, 8)
                if kk == 0:
                    pe.wait_ge(conv_w_in[2 * dh], 16)
                    pe.wait_ge(conv_w_in[2 * dh + 1], 16)
                if n >= 4:
                    m = n - 4
                    if m % 2 == 0:
                        pe.wait_ge(small_evac, m // 2 + 1)
                    else:
                        pe.wait_ge(w_evac_dve, m // 2 + 1)
                for k in range(2):
                    for oh in range(DH):
                        last = T(psB[:, n % 4, (2 * k + oh) * P:(2 * k + oh + 1) * P],
                                 conv_raw[:, oh, dh * P:(dh + 1) * P, 2 * kk + k], ident[:, :])
                last.then_inc(w_T, 1)
            pe.wait_ge(small_evac, 6)
            pe.wait_ge(w_evac_dve, 6)

            def transpose_quad(i, q):
                if q % (QUADS // 2) == 0:
                    pe.wait_ge(x_in_half[q // (QUADS // 2)], 16 * NB * (i + 1))
                pe.wait_ge(ring_drained, i * QUADS + q + 1)
                for k in range(2):
                    for dh in range(DH):
                        last = T(psB[:, q % 4, (2 * k + dh) * P:(2 * k + dh + 1) * P],
                                 x_in[:, 2 * q + k, dh * P:(dh + 1) * P], ident[:, :])
                last.then_inc(quad_T, 1)

            def conv_quad(i, s, q):
                pe.wait_ge(ring_drained, 4 + i * QUADS + q + 1)
                for k in range(2):
                    for dh in range(DH):
                        last = M(psA[:, s, 0:D], xT[:, s, 2 * q + k, dh * P:(dh + 1) * P], wT[:, 2 * q + k, dh, :],
                                 start=(q == 0 and k == 0 and dh == 0), stop=(q == QUADS - 1 and k == 1 and dh == 1))
                if q == QUADS - 1:
                    last.then_inc(conv_done, 1)

            AHEAD = 2
            with pe.Fori(0, TILES // 2) as j:
                for s in range(2):
                    i = j * 2 + s
                    pe.wait_ge(conv_bank_free, i + 1)
                    for q in range(QUADS + AHEAD):
                        if q < QUADS:
                            transpose_quad(i, q)
                        if q >= AHEAD:
                            conv_quad(i, s, q - AHEAD)

            pe.wait_ge(raw_in, 16 * (2 + len(SMALL)))
            pe.wait_ge(ring_drained, 4 + TILES * QUADS)
            order = [('s', 5), ('s', 6), ('p', 0), ('p', 1), ('p', 2), ('s', 0), ('s', 1), ('s', 2), ('s', 3), ('s', 4)]
            for n, (kind, j) in enumerate(order):
                if n >= 4:
                    m = n - 4
                    if m < 5:
                        pe.wait_ge(small_evac, 6 + m + 1)
                    else:
                        pe.wait_ge(w_evac_dve, 6 + m - 5 + 1)
                for c in range(2):
                    for oh in range(DH):
                        if kind == 's':
                            src = small_raw[:, j, oh, c * P:(c + 1) * P]
                        else:
                            src = proj_raw[:, oh, (2 * j + c) * P:(2 * j + c + 1) * P]
                        last = T(psB[:, n % 4, (2 * c + oh) * P:(2 * c + oh + 1) * P], src, ident[:, :])
                last.then_inc(small_T, 1)
            pe.wait_ge(conv_bank_free, TILES + 2)
            for hh in range(DH):
                for t in range(TILES):
                    last = T(psA[:, 2 + hh, t * P:(t + 1) * P], conv_tok[:, t, hh * P:(hh + 1) * P], ident[:, :])
                last.then_inc(conv_T, 1)
            pe.wait_ge(last_rep, 1)
            for dh in range(DH):
                last = T(psA[:, 0, dh * P:(dh + 1) * P], lastT[:, dh, :, :], ident[:, :])
            last.then_inc(cols_T, 1)
            pe.wait_ge(small_evac, 6 + 5)
            pe.wait_ge(conv_comb, DH)
            pe.wait_ge(std_made, 1)
            pe.wait_ge(last_tok_made, 1)
            for pr in range(PAIRS):
                for t in (2 * pr, 2 * pr + 1):
                    for c in range(3 * DH):
                        last = M(psA[:, pr, (t % 2) * D:(t % 2 + 1) * D], comb[:, c, t * P:(t + 1) * P], projT[:, c, :],
                                 start=(c == 0), stop=(c == 3 * DH - 1))
                last.then_inc(proj_done, 1)

            def transpose_pair(s, pr, src):
                for hh in range(DH):
                    for t in range(2):
                        last = T(psB[:, pr, (2 * hh + t) * P:(2 * hh + t + 1) * P],
                                 src[:, 2 * pr + t, hh * P:(hh + 1) * P], ident[:, :])
                last.then_inc(trans_done, 1)

            def linear_pair(pr, bank, lhs, rhs, chunks, done):
                for t in range(2):
                    for c in range(chunks):
                        last = M(bank[:, t * D:(t + 1) * D], lhs[:, c, (2 * pr + t) * P:(2 * pr + t + 1) * P], rhs[:, c, :],
                                 start=(c == 0), stop=(c == chunks - 1))
                last.then_inc(done, 1)

            for pr in range(PAIRS):
                pe.wait_ge(ln_out, ln_outs(LN_ATTN, pr))
                transpose_pair(T_ATTN, pr, u)
            pe.wait_ge(w_evac_dve, 6 + 5)
            for t in range(TILES):
                pe.wait_ge(trans_evac, 2 * T_ATTN + t // 2 + 1)
                if t >= 2:
                    pe.wait_ge(kv_biased, 2 * (t - 1))
                for j in range(2):
                    for c in range(DH):
                        last = M(psA[:, 2 * (t % 2) + j, :], uT[:, c, t * P:(t + 1) * P], wkvT[:, c, 512 * j:512 * j + 512],
                                 start=(c == 0), stop=(c == DH - 1))
                    last.then_inc(kv_done, 1)
            for hh in range(2):
                for c in range(DH):
                    last = M(psB[:, hh, :], wqT[:, c, hh * P:(hh + 1) * P], uT[:, c, :], start=(c == 0), stop=(c == DH - 1))
                last.then_inc(q_done, 1)

            def value_sums(t):
                pe.wait_ge(kv_biased, 2 * t + 2)
                if t >= 2:
                    pe.wait_ge(vscaled, t - 1)
                for j in range(2):
                    v = kv[:, t, 768:1024] if j == 0 else kv[:, t, 256:512]
                    last = M(psB[:, 2 + t % 2, j * D:(j + 1) * D], same_seq[:, :], v, start=True, stop=True)
                last.then_inc(vsum_done, 1)

            def heads(c, hf):
                return 64 * c + 32 * hf

            def products(t, ps, terms, per_bank):
                for hf in range(2):
                    for c in range(4):
                        for n, (klo, vi, o, first, end) in enumerate(terms):
                            for r in range(4):
                                f = heads(c, hf)
                                last = M(ps[32 * c:32 * c + 32, r, o + 128 * hf:o + 128 * hf + 128].rearrange("p (b f) -> p b f", b=4),
                                         kv[32 * r:32 * r + 32, t, klo + f:klo + f + 32],
                                         vx[32 * r:32 * r + 32, vi, :, f:f + 32], start=first, stop=end,
                                         tile_position=(32 * r, 32 * c))
                return last

            for t in range(TILES):
                value_sums(t)
            for t in range(TILES):
                ps_s, ps_m = (psA, psB) if (3 * t) % 2 == 0 else (psB, psA)
                pe.wait_ge(masks_made, 1)
                pe.wait_ge(vx_plain, t + 1)
                if t == 0:
                    pe.wait_ge(kv_biased, 2 * TILES)
                    pe.wait_ge(q_out, 2)
                else:
                    pe.wait_ge(smix_masked, t)
                products(t, ps_s, [(0, 0, 0, True, True), (512, 1, 256, True, True)], 4).then_inc(s_done, 1)
                pe.wait_ge(vx_mixed, t + 1)
                if t == 0:
                    pe.wait_ge(vscaled, TILES)
                if t >= 1:
                    pe.wait_ge(y_made, t)
                products(t, ps_m, [(0, 2, 0, True, False), (512, 3, 0, False, True)], 4).then_inc(smix_done, 1)
                pe.wait_ge(s12_made, t + 1)
                pe.wait_ge(smix_masked, t + 1)
                pe.wait_ge(qa_out, 2)
                for hf in range(2):
                    for r in range(4):
                        for n, (lhs, rhs) in enumerate(((qT, smix), (qaT, s12))):
                            for c in range(4):
                                last = M(ps_s[32 * r:32 * r + 32, c, 0:256].rearrange("p (b q i) -> p b q i", q=2, i=32)[:, :, hf, :],
                                         lhs[32 * c:32 * c + 32, hf, t * P + 32 * r:t * P + 32 * r + 32],
                                         rhs[32 * c:32 * c + 32, t % 2, r, 128 * hf:128 * hf + 128].rearrange("p (b i) -> p b i", b=4),
                                         start=(n == 0), stop=(n == 1), tile_position=(32 * c, 32 * r))
                last.then_inc(y_done, 1)

            for pr in range(PAIRS):
                pe.wait_ge(ln_out, ln_outs(LN_Y, pr))
                if pr == 0:
                    pe.wait_ge(y_made, TILES)
                transpose_pair(T_WO, pr, y)
            for pr in range(PAIRS):
                pe.wait_ge(trans_evac, 2 * T_WO + pr + 1)
                linear_pair(pr, psA[:, pr, :], uT, woT, DH, wo_done)
            for pr in range(PAIRS):
                pe.wait_ge(ln_out, ln_outs(LN_FFN, pr))
                transpose_pair(T_FFN, pr, u)
            for pr in range(PAIRS):
                pe.wait_ge(trans_evac, 2 * T_FFN + pr + 1)
                linear_pair(pr, psA[:, pr, :], uT, wblk, DH, blk_done)
            pe.wait_ge(score_rhs, 1)
            M(psA[:, 2, 0:TILES * NB], same_seq[:, :], sc_rhs[:, :, :].rearrange("p t j -> p (t j)"),
              start=True, stop=True).then_inc(score_all, 1)
            for pr in range(PAIRS):
                pe.wait_ge(ln_out, ln_outs(LN_SPIRAL, pr))
                transpose_pair(T_SPIRAL, pr, y)
            pe.wait_ge(diag_made, 1)
            for pr in range(PAIRS):
                pe.wait_ge(trans_evac, 2 * T_SPIRAL + pr + 1)
                for dh in range(DH):
                    seqs = slice(256 * pr, 256 * pr + 256)
                    o = psA[:, 2 + pr, dh * D:(dh + 1) * D].rearrange("p (b n) -> p b n", n=NB)
                    i = uT[:, dh, seqs].rearrange("p (b n) -> p b n", n=NB)
                    for tau in range(NB):
                        last = M(o[:, :, tau:NB], diagF[:, dh, tau, :], i[:, :, 0:NB - tau], start=(tau == 0), stop=(tau == NB - 1))
                last.then_inc(filt_conv, 1)
            for pr in range(PAIRS):
                pe.wait_ge(filt_out, pr + 1)
                for t in range(2):
                    for dh in range(DH):
                        last = T(psA[:, pr, t * D + dh * P:t * D + (dh + 1) * P],
                                 qT[:, dh, (2 * pr + t) * P:(2 * pr + t + 1) * P], ident[:, :])
                last.then_inc(spiral_done, 1)
            for pr in range(PAIRS):
                pe.wait_ge(ln_out, ln_outs(LN_MLP, pr))
                transpose_pair(T_MLP, pr, u)
            pe.wait_ge(late_in, 32)
            pe.wait_ge(trans_evac, 2 * T_MLP + 2)
            for c in range(FC):
                if c >= 4:
                    pe.wait_ge(silu_done, c - 3)
                for k in range(DH):
                    last = M(psA[:, c % 4, :], w1[:, k, c * P:(c + 1) * P], uT[:, k, :], start=(k == 0), stop=(k == DH - 1))
                last.then_inc(w1_done, 1)
            pe.wait_ge(silu_done, FC)
            for pr in range(PAIRS):
                linear_pair(pr, psB[:, 2 + pr, :], gT, w2, FC, w2_done)
            for pr in range(PAIRS):
                pe.wait_ge(ln_out, ln_outs(LN_CB, pr))
                transpose_pair(T_CB, pr, u)
            for pr in range(PAIRS):
                pe.wait_ge(trans_evac, 2 * T_CB + pr + 1)
                linear_pair(pr, psA[:, pr, :], uT, cbT, DH, cb_done)


def kernel(**inputs):
    import numpy as _np
    import concourse.bacc as _bacc
    from concourse import mybir as _mybir
    from concourse.bass_utils import run_bass_kernel_spmd as _run

    nc = _bacc.Bacc("TRN2", target_bir_lowering=False, num_devices=1)
    arrays, args = {}, {}
    for name in _INS:
        v = _np.ascontiguousarray(inputs[name])
        arrays[f"in_{name}"] = v
        args[name] = nc.dram_tensor(f"in_{name}", v.shape, _mybir.dt.from_np(v.dtype), kind="ExternalInput").ap()
    out = nc.dram_tensor("out_0", (64, 8, 256), _mybir.dt.float32, kind="ExternalOutput").ap()
    build_tower(nc, args, out)
    r = _run(nc, [arrays], core_ids=[0])
    return r.results[0]["out_0"]
```

```python
from contextlib import ExitStack

import concourse.bass as bass
from concourse import mybir

F32 = mybir.dt.float32
ALU = mybir.AluOpType
ACT = mybir.ActivationFunctionType
AX = mybir.AxisListType

P = 128
EPS = 1e-5

_INS = ['x', 'L0_tok_conv_w', 'L0_tok_conv_b', 'L0_tok_proj_w', 'L0_tok_proj_b', 'L0_tok_ln_g', 'L0_tok_ln_b',
        'L0_tok_pos_table', 'L0_attn_Wq', 'L0_attn_bq', 'L0_attn_Wk1', 'L0_attn_bk1', 'L0_attn_Wk2', 'L0_attn_bk2',
        'L0_attn_Wv1', 'L0_attn_bv1', 'L0_attn_Wv2', 'L0_attn_bv2', 'L0_attn_g1', 'L0_attn_g2', 'L0_attn_g3',
        'L0_attn_g4', 'L0_attn_ln_g', 'L0_attn_ln_b', 'L0_attn_Wo', 'L0_attn_bo', 'L0_ffn_w_router',
        'L0_ffn_w_block', 'L1_attn_ln_gamma', 'L1_attn_ln_beta', 'L1_attn_phazor_re', 'L1_attn_phazor_im',
        'L1_attn_phazor_init_re', 'L1_attn_phazor_init_im', 'L1_attn_last_conv_re', 'L1_attn_last_conv_im',
        'L1_attn_w1', 'L1_attn_b1', 'L1_attn_w2', 'L1_attn_b2', 'L1_ffn_CB', 'L1_ffn_SCB', 'L1_ffn_bias']


def build_tower(nc, a, out):
    NSEQ, NFRAME, D = a['x'].shape
    KB = a['L0_tok_conv_w'].shape[2]
    NB = -(-NFRAME // KB)
    LAST = NFRAME - (NB - 1) * KB
    HEADS = a['L0_attn_g1'].shape[0]
    FF = a['L1_attn_w1'].shape[1]
    DH = D // P
    TILES = NSEQ * NB // P
    SEQ = P // NB
    PAIRS = TILES // 2
    QUADS = KB * DH // 4
    FC = FF // P
    TOPK = max(1, int(NB * 0.75))
    N = NSEQ * NB
    assert (D, KB, NB, TILES, HEADS) == (256, 16, 8, 4, 16)

    ctx = ExitStack()
    with ctx:
        def sb(name, shape):
            return ctx.enter_context(nc.sbuf_tensor(name, shape, F32))

        def sem(name):
            return ctx.enter_context(nc.semaphore(name))

        psA = ctx.enter_context(nc.psum_tensor("psA", [P, 4, 512], F32))
        psB = ctx.enter_context(nc.psum_tensor("psB", [P, 4, 512], F32))

        region_x = sb("region_x", [P, KB * D])
        region_xT = sb("region_xT", [P, 2 * KB * D])
        region_wT = sb("region_wT", [P, KB * DH * D])
        region_raw = sb("region_raw", [P, DH * KB * D])
        proj_space = sb("proj_space", [P, 4 * DH * 3 * P])
        x_in = region_x[:, :].rearrange("p (k d) -> p k d", k=KB)
        xT = region_xT[:, :].rearrange("p (s k f) -> p s k f", s=2, k=KB)
        wT = region_wT[:, :].rearrange("p (k h o) -> p k h o", k=KB, h=DH)
        conv_raw = region_raw[:, :].rearrange("p (o d k) -> p o d k", o=DH, k=KB)
        centred = region_raw[:, 0:KB * D].rearrange("p (k f) -> p k f", k=KB)
        SMALL = ['L0_attn_Wq', 'L0_attn_Wk1', 'L0_attn_Wv1', 'L0_attn_Wk2', 'L0_attn_Wv2', 'L0_attn_Wo', 'L1_ffn_CB']
        small_raw = region_raw[:, KB * D:KB * D + 7 * 512].rearrange("p (w o i) -> p w o i", w=7, o=DH)

        h = region_raw[:, 0:1024].rearrange("p (t f) -> p t f", t=4)
        haux = region_raw[:, 1024:2048].rearrange("p (t f) -> p t f", t=4)
        u = region_raw[:, 2048:3072].rearrange("p (t f) -> p t f", t=4)
        y = region_raw[:, 3072:4096].rearrange("p (t f) -> p t f", t=4)
        vmix = region_raw[:, 4608:6656].rearrange("p (t v f) -> p t v f", t=4, v=2)
        lastT = region_raw[:, 4096:4352].rearrange("p (h b n) -> p h b n", h=DH, n=NB)

        w1 = region_x[:, 0:DH * FF].rearrange("p (h f) -> p h f", h=DH)
        w2 = region_x[:, DH * FF:DH * FF + FC * D].rearrange("p (c d) -> p c d", c=FC)
        kv = region_xT[:, 0:4096].rearrange("p (t f) -> p t f", t=4)
        gT = region_xT[:, 0:4096].rearrange("p (c n) -> p c n", c=FC)
        g_act = region_wT[:, 0:1024].rearrange("p (t f) -> p t f", t=4)
        uT = region_wT[:, 1024:2048].rearrange("p (h n) -> p h n", h=DH)
        q_tok = region_wT[:, 2048:3072].rearrange("p (t f) -> p t f", t=4)
        qa_tok = region_wT[:, 3072:4096].rearrange("p (t f) -> p t f", t=4)
        filtT = region_wT[:, 2048:3072].rearrange("p (h n) -> p h n", h=DH)
        s12 = region_wT[:, 4096:5120].rearrange("p (s f) -> p s f", s=2)
        smix = region_wT[:, 5120:6144].rearrange("p (s f) -> p s f", s=2)
        vxp = [region_xT[:, 4096:6144].rearrange("p (v b f) -> p v b f", v=2, b=4),
               proj_space[:, 0:2048].rearrange("p (v b f) -> p v b f", v=2, b=4)]
        vxm = [region_xT[:, 6144:8192].rearrange("p (v b f) -> p v b f", v=2, b=4),
               region_wT[:, 6144:8192].rearrange("p (v b f) -> p v b f", v=2, b=4)]

        comb = sb("comb", [P, 3 * DH, N])
        comb_cols = comb[:, :, :].rearrange("p a n -> p (a n)")
        kx = sb("kx", [P, 2, 2, 8, 4, 32])
        qx = comb_cols[:, 0:1024].rearrange("p (g r i) -> p g r i", g=8, r=4)
        qax = comb_cols[:, 1024:2048].rearrange("p (g r i) -> p g r i", g=8, r=4)
        conv_tok = sb("conv_tok", [P, TILES, D])
        proj_raw = proj_space[:, 0:DH * 3 * D].rearrange("p (o i) -> p o i", o=DH)
        projT = proj_space[:, DH * 3 * D:2 * DH * 3 * D].rearrange("p (c o) -> p c o", o=D)
        wqT = sb("wqT", [P, DH, D])
        wkvT = sb("wkvT", [P, DH, 4 * D])
        woT = sb("woT", [P, DH, D])
        cbT = sb("cbT", [P, DH, D])
        wblk = sb("wblk", [P, DH, D])
        diagF = sb("diagF", [P, DH, NB, P])
        negmean = sb("negmean", [P, D])
        ssq_hi = sb("ssq_hi", [P, D])
        ROWS = ['L0_tok_proj_b', 'L0_tok_ln_g', 'L0_tok_ln_b', 'L0_attn_bk1', 'L0_attn_bv1', 'L0_attn_bk2',
                'L0_attn_bv2', 'L0_attn_bq', 'L0_attn_bo', 'L0_ffn_w_router', 'L1_attn_b2', 'L1_ffn_SCB', 'L1_ffn_bias']
        rows = sb("rows", [P, len(ROWS), D])
        g_rows = sb("g_rows", [P, 4, D])
        g13 = g_rows[:, 0:2, :]
        pos = sb("pos", [P, D])
        COLS = ['L0_tok_conv_b', 'L0_attn_ln_g', 'L0_attn_ln_b', 'L1_attn_ln_gamma',
                'L1_attn_ln_beta', 'L1_attn_phazor_re', 'L1_attn_phazor_im', 'L1_attn_phazor_init_re',
                'L1_attn_phazor_init_im', 'L1_attn_last_conv_re', 'L1_attn_last_conv_im']
        NCOL = len(COLS) + FF // D
        last_tok = sb("last_tok", [P, D])
        colrow = last_tok[0:NCOL, :]
        g_raw = sb("g_raw", [P, 4, HEADS])
        col = sb("col", [P, DH, NCOL])
        ident = sb("ident", [P, P])
        ident2 = sb("ident2", [P, 512])
        ones = sb("ones", [P, P])
        seq16 = sb("seq16", [P, SEQ])
        same_seq = sb("same_seq", [P, P])
        before = sb("before", [P, P])
        head8 = sb("head8", [P, 8])
        mask_seq = sb("mask_seq", [P, 4])
        mask_head = sb("mask_head", [P, 2])
        mask_head64 = sb("mask_head64", [P, 2])
        slot = sb("slot", [P, NB])
        slot_lt = sb("slot_lt", [P, NB])
        eps = sb("eps", [P, 1])
        scratch = sb("scratch", [P, 8])
        pw = sb("pw", [P, 2, NB + 1, DH])
        pt = sb("pt", [P, 4, NB, DH])
        filt = sb("filt", [P, NB, DH])
        lastf = sb("lastf", [P, NB, DH])
        mag = sb("mag", [P, 6, DH])
        st = sb("st", [P, TILES, 6])
        mv = sb("mv", [P, TILES, 2])
        sd = sb("sd", [P, TILES])
        rs = sb("rs", [P, TILES])
        uvar, usd, urs = sb("uvar", [P, TILES]), sb("usd", [P, TILES]), sb("urs", [P, TILES])
        score = sb("score", [P, TILES])
        sc_rhs = sb("sc_rhs", [P, TILES, NB])
        sc_t = sb("sc_t", [P, 4, TILES, NB])
        sc_self = sb("sc_self", [P, TILES])
        rank = sb("rank", [P, TILES])
        sel = sb("sel", [P, 2, TILES])

        R = {n: rows[:, j, :] for j, n in enumerate(ROWS)}
        kv_bias = rows[:, 3:7, :].rearrange("p a f -> p (a f)")

        def vec(name, half):
            return col[:, half, COLS.index(name):COLS.index(name) + 1]

        def both(name):
            return col[:, :, COLS.index(name)]

        cols_in, rows_in, raw_in, late_in = sem("cols_in"), sem("rows_in"), sem("raw_in"), sem("late_in")
        conv_w_in = [sem(f"conv_w_in{n}") for n in range(4)]
        x_in_half = [sem("x_in_lo"), sem("x_in_hi")]
        out_stored = sem("out_stored")
        pool_step, masks_made, consts_made = sem("pool_step"), sem("masks_made"), sem("consts_made")
        x_pad_zero = sem("x_pad_zero")
        cols_out = sem("cols_out")
        cols_T, dve_step, mag2_made, mag_made, decay_made = (sem(n) for n in (
            "cols_T", "dve_step", "mag2_made", "mag_made", "decay_made"))
        filt_made, diag_made, last_rep = sem("filt_made"), sem("diag_made"), sem("last_rep")
        w_T, w_evac_dve = sem("w_T"), sem("w_evac_dve")
        quad_T = sem("quad_T")
        ring_drained = sem("ring_drained")
        conv_bank_free = sem("conv_bank_free")
        conv_done = sem("conv_done")
        negsum, mean_made = sem("negsum"), sem("mean_made")
        max_done = sem("max_done")
        centred_done = sem("centred_done")
        squared, ssq_half = sem("squared"), sem("ssq_half")
        ssq_done = sem("ssq_done")
        small_T, small_evac = sem("small_T"), sem("small_evac")
        std_made, conv_T, conv_comb = sem("std_made"), sem("conv_T"), sem("conv_comb")
        proj_done, proj_biased = sem("proj_done"), sem("proj_biased")
        ln_stat, ln_mv, ln_sd, ln_rs, ln_out, trans_done, trans_evac = (
            [sem(f"{n}{pr}") for pr in range(PAIRS)]
            for n in ("ln_stat", "ln_mv", "ln_sd", "ln_rs", "ln_out", "trans_done", "trans_evac"))
        tok_scaled, tok_out, bpos_made = sem("tok_scaled"), sem("tok_out"), sem("bpos_made")
        kv_done, kv_biased = sem("kv_done"), sem("kv_biased")
        q_done, q_biased, qa_scaled, qa_made = sem("q_done"), sem("q_biased"), sem("qa_scaled"), sem("qa_made")
        kx_made, qx_zero, qx_made = sem("kx_made"), sem("qx_zero"), sem("qx_made")
        uvar_step, usd_made, urs_made, un_made = sem("uvar_step"), sem("usd_made"), sem("urs_made"), sem("un_made")
        vsum_done, vscaled, vmixed = sem("vsum_done"), sem("vscaled"), sem("vmixed")
        vx_plain, vx_mixed = sem("vx_plain"), sem("vx_mixed")
        s_done, s1_masked, s12_made = sem("s_done"), sem("s1_masked"), sem("s12_made")
        smix_done, smix_masked = sem("smix_done"), sem("smix_masked")
        y_done, y_step, y_made = sem("y_done"), sem("y_step"), sem("y_made")
        hbo_made, wo_done, h1_made = sem("hbo_made"), sem("wo_done"), sem("h1_made")
        score_made, score_rhs, score_all, sel_made = (sem(n) for n in ("score_made", "score_rhs", "score_all", "sel_made"))
        blk_done, gelu_done, kept, h2_made = sem("blk_done"), sem("gelu_done"), sem("kept"), sem("h2_made")
        u_last, spiral_done, x1_made, hx_made = sem("u_last"), sem("spiral_done"), sem("x1_made"), sem("hx_made")
        last_tok_made = sem("last_tok_made")
        filt_conv, filt_out = sem("filt_conv"), sem("filt_out")
        w1_done, silu_done, w2_done, h3_made = sem("w1_done"), sem("silu_done"), sem("w2_done"), sem("h3_made")
        hb_made, cb_done, cb_scaled, out_made = sem("hb_made"), sem("cb_done"), sem("cb_scaled"), sem("out_made")

        T_ATTN, T_WO, T_FFN, T_SPIRAL, T_MLP, T_CB = range(6)
        LN_TOK, LN_ATTN, LN_Y, LN_FFN, LN_L1, LN_MLP, LN_CB = range(7)
        STEPS = 2 * TILES

        def kv_bank(t, j):
            return psA[:, 2 * ((t + 1) % 2) + j, :]

        def y_bank(n):
            return psB[:, 1 + 2 * (n % 2), :]

        def w1_bank(n):
            return (psA[:, 0, :], psA[:, 1, :], psB[:, 0, :], psB[:, 1, :])[n % 4]

        block = ctx.enter_context(nc.Block())

        @block.sync
        def _(sp):
            for n in range(4):
                dh, oh = divmod(n, 2)
                sp.dma_start(conv_raw[:, oh, dh * P:(dh + 1) * P, :],
                             a['L0_tok_conv_w'][oh * P:(oh + 1) * P, dh * P:(dh + 1) * P, :]).then_inc(conv_w_in[n], 16)

            def load_x(i, half):
                k0, k1 = half * KB // 2, (half + 1) * KB // 2
                FULL = NB - 1
                sp.dma_start(x_in[0:FULL * SEQ, k0:k1, :],
                             a['x'][bass.ds(i * SEQ, SEQ), 0:FULL * KB, :].rearrange("b (n k) d -> n b k d", k=KB)[:, :, k0:k1, :]
                             .rearrange("n b k d -> n b (k d)")).then_inc(x_in_half[half], 16)
                ke = min(k1, LAST)
                sp.dma_start(x_in[FULL * SEQ:P, k0:ke, :],
                             a['x'][bass.ds(i * SEQ, SEQ), FULL * KB + k0:FULL * KB + ke, :]).then_inc(x_in_half[half], 16)

            def load_next_x(i):
                for half in range(2):
                    sp.wait_ge(quad_T, i * QUADS - QUADS // 2 + half * (QUADS // 2))
                    load_x(i, half)

            sp.wait_ge(x_pad_zero, 1)
            load_x(0, 0)
            load_x(0, 1)
            with sp.Fori(1, TILES - 1) as i:
                load_next_x(i)
            sp.dma_start(proj_raw[:, :, :], a['L0_tok_proj_w'].rearrange("(o p) i -> p o i", p=P)).then_inc(raw_in, 16)
            sp.dma_start(wblk[:, :, :], a['L0_ffn_w_block'].rearrange("(c p) e -> p c e", p=P)).then_inc(raw_in, 16)
            sp.wait_ge(w_T, 16)
            for j, name in enumerate(SMALL):
                sp.dma_start(small_raw[:, j, :, :], a[name].rearrange("(o p) i -> p o i", p=P)).then_inc(raw_in, 16)
            load_next_x(TILES - 1)
            for j, name in enumerate(ROWS):
                sp.dma_start(rows[:, j, :], a[name].partition_broadcast(P)).then_inc(rows_in, 16)
            for j, name in enumerate(('L0_attn_g1', 'L0_attn_g3', 'L0_attn_g4', 'L0_attn_g2')):
                sp.dma_start(g_raw[:, j, :], a[name].partition_broadcast(P)).then_inc(rows_in, 16)
            sp.dma_start(pos[:, :],
                         a['L0_tok_pos_table'][0:NB, :].unsqueeze(0).to_broadcast([SEQ, NB, D])).then_inc(rows_in, 16)
            sp.wait_ge(quad_T, TILES * QUADS)
            sp.dma_start(w1, a['L1_attn_w1'].rearrange("(c p) f -> p c f", p=P)).then_inc(late_in, 16)
            sp.dma_start(w2, a['L1_attn_w2'].rearrange("(c p) d -> p c d", p=P)).then_inc(late_in, 16)
            out_v = out.rearrange("b n d -> (b n) d").rearrange("(t p) d -> p t d", p=P)
            for pr in range(PAIRS):
                sp.wait_ge(out_made, pr + 1)
                sp.dma_start(out_v[:, 2 * pr:2 * pr + 2, :], h[:, 2 * pr:2 * pr + 2, :]).then_inc(out_stored, 16)
            sp.wait_ge(out_stored, 16 * PAIRS)

        @block.gpsimd
        def _(pool):
            steps = [0]

            def step(ins):
                steps[0] += 1
                ins.then_inc(pool_step, 1)
                pool.wait_ge(pool_step, steps[0])

            k_lo = LAST
            nc.gpsimd.memset(x_in[96:P, k_lo:KB, :], 0.0).then_inc(x_pad_zero, 1)
            pool.wait_ge(x_pad_zero, 1)
            nc.gpsimd.memset(ones[:, :], 1.0)
            nc.gpsimd.memset(eps[:, :], EPS)
            step(nc.gpsimd.memset(ident2[:, :], 0.0))
            step(nc.gpsimd.affine_select(out=ident[:, :], in_=ones[:, :], compare_op=ALU.is_equal, fill=0.0, base=0,
                                         pattern=[[-1, P]], channel_multiplier=1))
            step(nc.gpsimd.affine_select(out=seq16[:, :], in_=ones[:, 0:SEQ], compare_op=ALU.is_ge, fill=0.0, base=0,
                                         pattern=[[-NB, SEQ]], channel_multiplier=1))
            step(nc.gpsimd.affine_select(out=seq16[:, :], in_=seq16[:, :], compare_op=ALU.is_ge, fill=0.0, base=NB - 1,
                                         pattern=[[NB, SEQ]], channel_multiplier=-1))
            step(nc.gpsimd.affine_select(out=head8[:, :], in_=ones[:, 0:8], compare_op=ALU.is_ge, fill=0.0, base=0,
                                         pattern=[[-16, 8]], channel_multiplier=1))
            step(nc.gpsimd.affine_select(out=head8[:, :], in_=head8[:, :], compare_op=ALU.is_ge, fill=0.0, base=15,
                                         pattern=[[16, 8]], channel_multiplier=-1))
            step(nc.gpsimd.tensor_copy(same_seq[:, :].rearrange("p (b n) -> p b n", n=NB),
                                       seq16[:, :].unsqueeze(2).to_broadcast([P, SEQ, NB])))
            step(nc.gpsimd.affine_select(out=before[:, :], in_=same_seq[:, :], compare_op=ALU.is_gt, fill=0.0, base=0,
                                         pattern=[[-1, P]], channel_multiplier=1))
            nc.gpsimd.tensor_copy(ident2[:, 0:P], ident[:, :])
            nc.gpsimd.tensor_copy(ident2[:, 3 * P:4 * P], ident[:, :]).then_inc(consts_made, 1)

            for sl in range(2):
                for which in range(2):
                    nc.gpsimd.memset(kx[:, sl, which, :, :, :].rearrange("p g r i -> p (g r i)"), 0.0).then_inc(centred_done, 1)

            def centre(i):
                pool.wait_ge(mean_made, i + 1)
                for half in range(2):
                    if half == 1:
                        pool.wait_ge(ssq_done, i + 1)
                    ks = slice(half * KB // 2, (half + 1) * KB // 2)
                    nc.gpsimd.tensor_tensor(out=centred[:, ks, :],
                                            in0=xT[:, bass.ds(i % 2, 1), ks, :].rearrange("p s k f -> p (s k) f"),
                                            in1=negmean[:, :].unsqueeze(1).to_broadcast([P, KB // 2, D]),
                                            op=ALU.add).then_inc(centred_done, 1)

            def diagonals(dh):
                pool.wait_ge(filt_made, 1)
                for t in range(NB):
                    last = nc.gpsimd.tensor_scalar(diagF[:, dh, t, :], ident[:, :], filt[:, t, dh:dh + 1], None, ALU.mult)
                last.then_inc(diag_made, 1)

            for i in range(DH):
                centre(i)
                diagonals(i)
            with pool.Fori(DH, TILES) as i:
                centre(i)
            pool.wait_ge(rows_in, 16 * (len(ROWS) + 5))
            nc.gpsimd.tensor_tensor(out=pos[:, :], in0=pos[:, :], in1=R['L0_tok_ln_b'], op=ALU.add).then_inc(bpos_made, 1)
            pool.wait_ge(small_T, 10)
            for dh in range(DH):
                last = nc.gpsimd.tensor_copy(lastT[:, dh, :, :],
                                             lastf[:, :, dh].unsqueeze(1).to_broadcast([P, SEQ, NB]))
            last.then_inc(last_rep, 1)

            def row2(name):
                return R[name].unsqueeze(1).to_broadcast([P, 2, D])

            def pair(buf, pr):
                return buf[:, 2 * pr:2 * pr + 2, :]

            pool.wait_ge(proj_done, PAIRS)
            nc.gpsimd.memset(comb_cols[:, 0:2048], 0.0).then_inc(qx_zero, 1)

            def residual_bo(pr):
                pool.wait_ge(tok_out, pr + 1)
                nc.gpsimd.tensor_tensor(out=pair(haux, pr), in0=pair(h, pr), in1=row2('L0_attn_bo'), op=ALU.add).then_inc(hbo_made, 1)

            def scaled_queries(t):
                pool.wait_ge(q_biased, t + 1)
                nc.gpsimd.tensor_tensor(out=qa_tok[:, t, :], in0=q_tok[:, t, :], in1=g_rows[:, 2, :], op=ALU.mult).then_inc(qa_scaled, 1)
                pool.wait_ge(qa_scaled, t + 1)
                nc.gpsimd.tensor_tensor(out=qa_tok[:, t, :], in0=qa_tok[:, t, :], in1=g_rows[:, 3, :], op=ALU.add).then_inc(qa_made, 1)

            def expand_plain(t):
                pool.wait_ge(kv_biased, 2 * t + 2)
                if t >= 2:
                    pool.wait_ge(s_done, 2 * (t - 1))
                vv = kv[:, t, :].rearrange("p (a b f) -> p a b f", a=2, b=2)[:, :, 1, :]
                for j in range(4):
                    last = nc.gpsimd.tensor_tensor(out=vxp[t % 2][:, :, j, :], in0=vv, in1=mask_seq[:, j:j + 1].unsqueeze(2).to_broadcast([P, 2, D]),
                                                   op=ALU.mult)
                last.then_inc(vx_plain, 1)

            pool.wait_ge(masks_made, 1)
            for t in range(TILES):
                if t == 1:
                    residual_bo(0)
                    residual_bo(1)
                expand_plain(t)
                scaled_queries(t)
            for pr in range(PAIRS):
                pool.wait_ge(ln_out[pr], LN_L1)
                pool.wait_ge(last_tok_made, 1)
                nc.gpsimd.tensor_tensor(out=pair(g_act, pr), in0=pair(u, pr),
                                        in1=last_tok[:, :].unsqueeze(1).to_broadcast([P, 2, D]), op=ALU.add).then_inc(u_last, 1)
                nc.gpsimd.tensor_tensor(out=pair(haux, pr), in0=pair(h, pr), in1=row2('L1_attn_b2'), op=ALU.add).then_inc(hx_made, 1)
                pool.wait_ge(hx_made, 2 * pr + 1)
                pool.wait_ge(x1_made, pr + 1)
                nc.gpsimd.tensor_tensor(out=pair(haux, pr), in0=pair(haux, pr), in1=pair(y, pr), op=ALU.add).then_inc(hx_made, 1)
            for pr in range(PAIRS):
                pool.wait_ge(h3_made, pr + 1)
                nc.gpsimd.tensor_tensor(out=pair(haux, pr), in0=pair(h, pr), in1=row2('L1_ffn_bias'), op=ALU.add).then_inc(hb_made, 1)

        @block.scalar
        def _(act):
            for j, name in enumerate(COLS):
                act.dma_start(colrow[j:j + 1, :], a[name].rearrange("(a d) -> a d", a=1)).then_inc(cols_in, 16)
            act.dma_start(colrow[len(COLS):NCOL, :], a['L1_attn_b1'].rearrange("(a d) -> a d", d=D)).then_inc(cols_in, 16)
            for n in [0, 2, 4, 6, 8, 10, 12, 13, 14, 15]:
                act.wait_ge(w_T, n + 1)
                dh, kk = divmod(n, 8)
                ins = nc.scalar.activation(wT[:, 2 * kk:2 * kk + 2, dh, :],
                                           psB[:, n % 4, :].rearrange("p (k o) -> p k o", k=2), ACT.Copy)
                ins.then_inc(ring_drained if n >= 12 else small_evac, 1)

            def tile_a(i, after_quad=()):
                act.wait_ge(max_done, i + 1)
                act.wait_ge(centred_done, 2 * i + 2)
                for q in range(QUADS):
                    act.wait_ge(quad_T, i * QUADS + q + 1)
                    nc.scalar.activation(
                        xT[:, bass.ds(i % 2, 1), 2 * q:2 * q + 2, :].rearrange("p s k (h b n) -> p (s k h) b n", h=DH, n=NB),
                        psB[:, q % 4, :].rearrange("p (g n b) -> p g b n", g=4, n=NB), ACT.Copy).then_inc(ring_drained, 1)
                    for at, what in after_quad:
                        if at == q:
                            what()

            def conv_out(i):
                act.wait_ge(conv_done, i + 1)
                nc.scalar.activation(conv_tok[:, bass.ds(i, 1), :].rearrange("p s f -> p (s f)"),
                                     psA[:, bass.ds(i % 2, 1), 0:D].rearrange("p s f -> p (s f)"), ACT.Copy).then_inc(conv_bank_free, 1)

            def square(i, half):
                act.wait_ge(centred_done, 4 + 2 * i + half + 1)
                piece = centred[:, half * KB // 2:(half + 1) * KB // 2, :]
                nc.scalar.activation(piece, piece, ACT.Square).then_inc(squared, 1)

            def std(pr):
                act.wait_ge(ssq_done, 1 + 2 * pr + 2)
                part = comb[:, DH:2 * DH, 2 * P * pr:2 * P * (pr + 1)]
                nc.scalar.activation(part, part, ACT.Sqrt, scale=1.0 / (KB - 1)).then_inc(std_made, 1)

            def small_out(n):
                act.wait_ge(small_T, n + 1)
                dst = projT[:, 2 * n:2 * n + 2, :] if n < 3 else (woT[:, :, :], cbT[:, :, :])[n - 3]
                nc.scalar.activation(dst, psB[:, n % 4, :].rearrange("p (c o) -> p c o", c=2), ACT.Copy).then_inc(small_evac, 1)

            def columns():
                act.wait_ge(cols_T, 1)
                for dh in range(DH):
                    nc.scalar.activation(col[:, dh, :], psA[:, 2, dh * NCOL:(dh + 1) * NCOL], ACT.Copy).then_inc(cols_out, 1)
                act.wait_ge(mag2_made, 1)
                nc.scalar.activation(mag[:, 1, :], mag[:, 0, :], ACT.Sqrt).then_inc(mag_made, 1)
                act.wait_ge(mag_made, 1)
                nc.scalar.activation(mag[:, 2, :], mag[:, 1, :], ACT.Exp, scale=-1.0).then_inc(decay_made, 1)

            tile_a(0, ((5, columns),))
            tile_a(1, ((5, lambda: square(0, 0)), (7, lambda: square(0, 1))))
            with act.Fori(2, TILES) as i:
                tile_a(i, ((1, lambda: conv_out(i - 2)), (5, lambda: square(i - 1, 0)), (7, lambda: square(i - 1, 1))))
            small_out(0)
            small_out(1)
            conv_out(TILES - 2)
            small_out(2)
            std(0)

            def conv_comb_out(pr):
                act.wait_ge(conv_T, pr + 1)
                for hh in range(DH):
                    last = nc.scalar.activation(comb[:, hh, 2 * P * pr:2 * P * (pr + 1)],
                                                psA[:, (2, 0)[pr], 2 * P * hh:2 * P * (hh + 1)],
                                                ACT.Identity, bias=vec('L0_tok_conv_b', hh))
                last.then_inc(conv_comb, 1)

            conv_comb_out(0)
            small_out(3)
            square(TILES - 1, 0)
            small_out(4)
            square(TILES - 1, 1)
            std(1)

            preloads = [0]

            def preload(func):
                n = preloads[0]
                preloads[0] += 1
                nc.scalar.activation(scratch[:, n:n + 1], eps[:, 0:1], func)

            def ln_sqrt(k, pr):
                act.wait_ge(ln_mv[pr], 2 * k + 2)
                nc.scalar.activation(sd[:, 2 * pr:2 * pr + 2], mv[:, 2 * pr:2 * pr + 2, 1], ACT.Sqrt, bias=eps[:, 0:1]).then_inc(ln_sd[pr], 1)

            def evac_T(s, pr, scale=None, bias=None):
                act.wait_ge(trans_done[pr], s + 1)
                src = psB[:, 2 + pr, :].rearrange("p (h n) -> p h n", h=DH)
                if scale is None:
                    nc.scalar.activation(uT[:, :, 256 * pr:256 * pr + 256], src, ACT.Copy).then_inc(trans_evac[pr], 1)
                    return
                for hh in range(DH):
                    last = nc.scalar.activation(uT[:, hh, 256 * pr:256 * pr + 256], src[:, hh, :], ACT.Identity, scale=vec(scale, hh), bias=vec(bias, hh))
                last.then_inc(trans_evac[pr], 1)

            def spread_keys(t):
                act.wait_ge(kv_biased, 2 * t + 2)
                if t >= 2:
                    act.wait_ge(smix_done, 2 * (t - 1))
                kk = kv[:, t, :].rearrange("p (a b g i) -> p a b g i", a=2, b=2, i=32)[:, :, 0]
                for r in range(4):
                    rr = slice(32 * r, 32 * r + 32)
                    last = nc.scalar.activation(kx[rr, t % 2, :, :, r, :], kk[rr], ACT.Copy)
                last.then_inc(kx_made, 1)

            def expand_mixed(t):
                act.wait_ge(vmixed, t + 1)
                if t >= 2:
                    act.wait_ge(smix_done, 2 * (t - 1))
                for j in range(4):
                    last = nc.scalar.activation(vxm[t % 2][:, :, j, :], vmix[:, t], ACT.Copy, scale=mask_seq[:, j:j + 1])
                last.then_inc(vx_mixed, 1)

            def head_masked(dst, ps, mask):
                d = dst.rearrange("p (g m e) -> p g m e", m=2, e=16)
                s = ps.rearrange("p (g m e) -> p g m e", m=2, e=16)
                for m in range(2):
                    last = nc.scalar.activation(d[:, :, m, :], s[:, :, m, :], ACT.Copy, scale=mask[:, m:m + 1])
                return last

            def s1_step(n):
                if n >= 2:
                    act.wait_ge(y_done, n - 1)
                act.wait_ge(s_done, n + 1)
                head_masked(s12[:, n % 2, :], psA[:, 0, :], mask_head64).then_inc(s1_masked, 1)

            def mix_step(n):
                act.wait_ge(smix_done, n + 1)
                head_masked(smix[:, n % 2, :], psB[:, 0, :], mask_head).then_inc(smix_masked, 1)

            def gelu(pr):
                preload(ACT.Gelu_apprx_tanh)
                act.wait_ge(blk_done, pr + 1)
                nc.scalar.activation(g_act[:, 2 * pr:2 * pr + 2, :], psA[:, 2 + pr, :].rearrange("p (t f) -> p t f", t=2),
                                     ACT.Gelu_apprx_tanh).then_inc(gelu_done, 1)
                preload(ACT.Sqrt)

            def u_sqrt(pr):
                act.wait_ge(uvar_step, 2 * pr + 2)
                nc.scalar.activation(usd[:, 2 * pr:2 * pr + 2], uvar[:, 2 * pr:2 * pr + 2], ACT.Sqrt, bias=eps[:, 0:1]).then_inc(usd_made, 1)

            def filtered(pr):
                act.wait_ge(filt_conv, pr + 1)
                nc.scalar.activation(filtT[:, :, 256 * pr:256 * pr + 256], psA[:, 2 + pr, :].rearrange("p (h n) -> p h n", h=DH),
                                     ACT.Copy).then_inc(filt_out, 1)

            def silu(pr, c):
                n = FC * pr + c
                act.wait_ge(w1_done, n + 1)
                cc = len(COLS) + c // 2
                nc.scalar.activation(gT[:, c, 2 * P * pr:2 * P * (pr + 1)], w1_bank(n)[:, 0:2 * P], ACT.Silu,
                                     bias=col[:, c % 2, cc:cc + 1]).then_inc(silu_done, 1)

            ln_sqrt(LN_TOK, 0)
            conv_out(TILES - 1)
            conv_comb_out(1)
            ln_sqrt(LN_ATTN, 0)
            evac_T(T_ATTN, 0)
            ln_sqrt(LN_TOK, 1)
            ln_sqrt(LN_ATTN, 1)
            act.wait_ge(masks_made, 1)
            act.wait_ge(centred_done, 4)
            spread_keys(0)
            evac_T(T_ATTN, 1)
            spread_keys(1)
            expand_mixed(0)
            expand_mixed(1)
            for n in range(STEPS):
                if n == 6:
                    ln_sqrt(LN_FFN, 0)
                if n == 7:
                    gelu(0)
                s1_step(n)
                if n == 5:
                    ln_sqrt(LN_Y, 0)
                mix_step(n)
                if n in (1, 3):
                    spread_keys(n // 2 + 2)
                if n in (2, 4):
                    expand_mixed(n // 2 + 1)
                if n == 5:
                    evac_T(T_WO, 0, 'L0_attn_ln_g', 'L0_attn_ln_b')
                if n == 6:
                    evac_T(T_FFN, 0)
            ln_sqrt(LN_L1, 0)
            ln_sqrt(LN_Y, 1)
            u_sqrt(0)
            evac_T(T_WO, 1, 'L0_attn_ln_g', 'L0_attn_ln_b')
            evac_T(T_SPIRAL, 0, 'L1_attn_ln_gamma', 'L1_attn_ln_beta')
            ln_sqrt(LN_FFN, 1)
            filtered(0)
            evac_T(T_FFN, 1)
            ln_sqrt(LN_MLP, 0)
            evac_T(T_MLP, 0, 'L1_attn_ln_gamma', 'L1_attn_ln_beta')
            gelu(1)
            ln_sqrt(LN_L1, 1)
            u_sqrt(1)
            preload(ACT.Silu)
            for c in range(FC):
                if c == 4:
                    evac_T(T_SPIRAL, 1, 'L1_attn_ln_gamma', 'L1_attn_ln_beta')
                if c == 6:
                    filtered(1)
                silu(0, c)
            preload(ACT.Sqrt)
            ln_sqrt(LN_MLP, 1)
            evac_T(T_MLP, 1, 'L1_attn_ln_gamma', 'L1_attn_ln_beta')
            ln_sqrt(LN_CB, 0)
            preload(ACT.Silu)
            for c in range(FC):
                if c == FC - 2:
                    evac_T(T_CB, 0)
                silu(1, c)
            preload(ACT.Sqrt)
            ln_sqrt(LN_CB, 1)
            evac_T(T_CB, 1)

        @block.vector
        def _(dve):
            steps = [0]

            def step(ins):
                steps[0] += 1
                ins.then_inc(dve_step, 1)
                dve.wait_ge(dve_step, steps[0])

            V = nc.vector
            dve.wait_ge(consts_made, 1)
            V.tensor_reduce(out=mask_seq[:, :], in_=seq16[:, :].rearrange("p (r j) -> p j r", j=4), axis=AX.X, op=ALU.add).then_inc(max_done, 1)
            dve.wait_ge(max_done, 1)
            V.tensor_reduce(out=slot[:, :], in_=ident[:, :].rearrange("p (b n) -> p n b", n=NB), axis=AX.X, op=ALU.add).then_inc(max_done, 1)
            V.tensor_reduce(out=slot_lt[:, :], in_=before[:, :].rearrange("p (b n) -> p n b", n=NB), axis=AX.X, op=ALU.add).then_inc(ssq_done, 1)
            step(V.tensor_reduce(out=mask_head[:, :], in_=head8[:, :].rearrange("p (c m) -> p m c", m=2), axis=AX.X, op=ALU.add))
            V.tensor_scalar(mask_head64[:, :], mask_head[:, :], 1.0 / (NB * NB), None, ALU.mult).then_inc(masks_made, 1)
            for n in [1, 3, 5, 7, 9, 11]:
                dve.wait_ge(w_T, n + 1)
                dh, kk = divmod(n, 8)
                V.tensor_copy(wT[:, 2 * kk:2 * kk + 2, dh, :], psB[:, n % 4, :].rearrange("p (k o) -> p k o", k=2)).then_inc(w_evac_dve, 1)

            dve.wait_ge(cols_out, 2)
            V.tensor_tensor(out=mag[:, 3, :], in0=both('L1_attn_phazor_re'), in1=both('L1_attn_phazor_re'), op=ALU.mult)
            step(V.tensor_tensor(out=mag[:, 4, :], in0=both('L1_attn_phazor_im'), in1=both('L1_attn_phazor_im'), op=ALU.mult))
            V.tensor_tensor(out=mag[:, 0, :], in0=mag[:, 3, :], in1=mag[:, 4, :], op=ALU.add).then_inc(mag2_made, 1)

            dve.wait_ge(decay_made, 1)
            V.memset(pw[:, 0, 0, :], 1.0)
            V.memset(pw[:, 1, 0, :], 0.0)
            step(V.reciprocal(mag[:, 3, :], mag[:, 1, :]))
            step(V.tensor_tensor(out=mag[:, 4, :], in0=mag[:, 2, :], in1=mag[:, 3, :], op=ALU.mult))
            V.tensor_tensor(out=pw[:, 0, 1, :], in0=both('L1_attn_phazor_re'), in1=mag[:, 4, :], op=ALU.mult)
            step(V.tensor_tensor(out=pw[:, 1, 1, :], in0=both('L1_attn_phazor_im'), in1=mag[:, 4, :], op=ALU.mult))
            for m in (1, 2, 4):
                def low(ri):
                    return pw[:, ri, 1:m + 1, :]

                def top(ri):
                    return pw[:, ri, m:m + 1, :].to_broadcast([P, m, DH])
                V.tensor_tensor(out=pt[:, 0, 0:m, :], in0=low(0), in1=top(0), op=ALU.mult)
                V.tensor_tensor(out=pt[:, 1, 0:m, :], in0=low(1), in1=top(1), op=ALU.mult)
                V.tensor_tensor(out=pt[:, 2, 0:m, :], in0=low(0), in1=top(1), op=ALU.mult)
                step(V.tensor_tensor(out=pt[:, 3, 0:m, :], in0=low(1), in1=top(0), op=ALU.mult))
                V.tensor_tensor(out=pw[:, 0, m + 1:2 * m + 1, :], in0=pt[:, 0, 0:m, :], in1=pt[:, 1, 0:m, :], op=ALU.subtract)
                step(V.tensor_tensor(out=pw[:, 1, m + 1:2 * m + 1, :], in0=pt[:, 2, 0:m, :], in1=pt[:, 3, 0:m, :], op=ALU.add))
            def colb(name):
                return both(name).unsqueeze(1).to_broadcast([P, NB, DH])
            V.tensor_tensor(out=pt[:, 0, :, :], in0=pw[:, 0, 0:NB, :], in1=colb('L1_attn_phazor_init_re'), op=ALU.mult)
            V.tensor_tensor(out=pt[:, 1, :, :], in0=pw[:, 1, 0:NB, :], in1=colb('L1_attn_phazor_init_im'), op=ALU.mult)
            V.tensor_tensor(out=pt[:, 2, :, :], in0=pw[:, 0, 1:NB + 1, :], in1=colb('L1_attn_last_conv_re'), op=ALU.mult)
            step(V.tensor_tensor(out=pt[:, 3, :, :], in0=pw[:, 1, 1:NB + 1, :], in1=colb('L1_attn_last_conv_im'), op=ALU.mult))
            V.tensor_tensor(out=filt[:, :, :], in0=pt[:, 0, :, :], in1=pt[:, 1, :, :], op=ALU.subtract)
            V.tensor_tensor(out=lastf[:, :, :], in0=pt[:, 2, :, :], in1=pt[:, 3, :, :], op=ALU.subtract).then_inc(filt_made, 1)

            def by_feature(buf3):
                return buf3.rearrange("p k f -> p f k")

            def slot_xT(i):
                return xT[:, bass.ds(i % 2, 1), :, :].rearrange("p s k f -> p (s f) k")

            def cols_of(chunk, i):
                return comb[:, chunk:chunk + DH, bass.ds(i * P, P)]

            def mean(i):
                dve.wait_ge(ring_drained, 4 + QUADS * i + QUADS)
                dve.wait_ge(centred_done, 4 + 2 * i)
                V.tensor_reduce(out=negmean[:, :], in_=slot_xT(i), axis=AX.X, op=ALU.add).then_inc(negsum, 1)
                dve.wait_ge(negsum, i + 1)
                V.tensor_scalar(negmean[:, :], negmean[:, :], -1.0 / KB, None, ALU.mult).then_inc(mean_made, 1)

            def maximum(i):
                V.tensor_reduce(out=cols_of(2 * DH, i), in_=slot_xT(i), axis=AX.X, op=ALU.max).then_inc(max_done, 1)

            def sum_squares(i, half):
                dve.wait_ge(squared, 2 * i + half + 1)
                dst = cols_of(DH, i) if half == 0 else ssq_hi[:, :]
                V.tensor_reduce(out=dst, in_=by_feature(centred[:, half * KB // 2:(half + 1) * KB // 2, :]),
                                axis=AX.X, op=ALU.add).then_inc(ssq_half, 1)

            def add_halves(i):
                dve.wait_ge(ssq_half, 2 * i + 2)
                V.tensor_tensor(out=cols_of(DH, i), in0=cols_of(DH, i), in1=ssq_hi[:, :].rearrange("p (h f) -> p h f", h=DH),
                                op=ALU.add).then_inc(ssq_done, 1)
                dve.wait_ge(ssq_done, i + 2)

            def plus_identity(n):
                dve.wait_ge(small_T, 6 + n)
                dst = wqT[:, :, :] if n == 0 else wkvT[:, :, (n - 1) * D:n * D]
                V.tensor_tensor(out=dst,
                                in0=psB[:, (5 + n) % 4, :].rearrange("p (h o) -> p h o", h=DH),
                                in1=ident2[:, :].rearrange("p (h o) -> p h o", h=DH), op=ALU.add).then_inc(w_evac_dve, 1)

            mean(0)
            maximum(0)
            sum_squares(0, 0)
            with dve.Fori(1, TILES - 1) as i:
                mean(i)
                sum_squares(i - 1, 1)
                add_halves(i - 1)
                maximum(i)
                sum_squares(i, 0)
            i = TILES - 1
            mean(i)
            sum_squares(i - 1, 1)
            add_halves(i - 1)
            maximum(i)
            sum_squares(i, 0)
            plus_identity(0)
            sum_squares(i, 1)
            add_halves(i)
            plus_identity(1)

            def stats(k, pr, src):
                for t in (2 * pr, 2 * pr + 1):
                    V.bn_stats(st[:, t, :], src[:, t, :]).then_inc(ln_stat[pr], 1)
                for n, t in enumerate((2 * pr, 2 * pr + 1)):
                    dve.wait_ge(ln_stat[pr], 2 * k + n + 1)
                    V.bn_aggr(mv[:, t, :], st[:, t, :]).then_inc(ln_mv[pr], 1)

            def rstd(k, pr):
                dve.wait_ge(ln_sd[pr], k + 1)
                V.reciprocal(rs[:, 2 * pr:2 * pr + 2], sd[:, 2 * pr:2 * pr + 2]).then_inc(ln_rs[pr], 1)
                dve.wait_ge(ln_rs[pr], k + 1)

            def normalise(k, pr, src, dst):
                rstd(k, pr)
                for t in (2 * pr, 2 * pr + 1):
                    last = V.tensor_scalar(dst[:, t, :], src[:, t, :], mv[:, t, 0:1], rs[:, t:t + 1], ALU.subtract, ALU.mult)
                last.then_inc(ln_out[pr], 1)

            def pair(buf, pr):
                return buf[:, 2 * pr:2 * pr + 2, :]

            def bank2(bank):
                return bank.rearrange("p (t f) -> p t f", t=2)

            def row2(name):
                return R[name].unsqueeze(1).to_broadcast([P, 2, D])

            def tok_bias(pr):
                dve.wait_ge(proj_done, pr + 1)
                V.tensor_tensor(out=pair(y, pr), in0=bank2(psA[:, (3, 1)[pr], :]), in1=row2('L0_tok_proj_b'), op=ALU.add).then_inc(proj_biased, 1)
                dve.wait_ge(proj_biased, pr + 1)
                stats(LN_TOK, pr, y)

            def tok_norm(pr):
                rstd(LN_TOK, pr)
                for t in (2 * pr, 2 * pr + 1):
                    V.scalar_tensor_tensor(out=y[:, t, :], in0=y[:, t, :], scalar=mv[:, t, 0:1], in1=R['L0_tok_ln_g'],
                                           op0=ALU.subtract, op1=ALU.mult).then_inc(tok_scaled, 1)
                for t in (2 * pr, 2 * pr + 1):
                    dve.wait_ge(tok_scaled, t + 1)
                    last = V.scalar_tensor_tensor(out=h[:, t, :], in0=y[:, t, :], scalar=rs[:, t:t + 1], in1=pos[:, :],
                                                  op0=ALU.mult, op1=ALU.add)
                last.then_inc(tok_out, 1)
                dve.wait_ge(tok_out, pr + 1)
                stats(LN_ATTN, pr, h)

            def vv(t):
                return kv[:, t, :].rearrange("p (a b f) -> p a b f", a=2, b=2)[:, :, 1, :]

            def q_bias_add(t):
                dve.wait_ge(q_done, t + 1)
                V.tensor_tensor(out=q_tok[:, t, :], in0=psB[:, 1, 0:D], in1=R['L0_attn_bq'], op=ALU.add).then_inc(q_biased, 1)

            def kv_bias_add(t):
                for j in range(2):
                    dve.wait_ge(kv_done, 2 * t + j + 1)
                    V.tensor_tensor(out=kv[:, t, 512 * j:512 * j + 512], in0=kv_bank(t, j),
                                    in1=kv_bias[:, 512 * j:512 * j + 512], op=ALU.add).then_inc(kv_biased, 1)

            def mix_values(t):
                dve.wait_ge(vsum_done, t + 1)
                V.tensor_tensor(out=vmix[:, t], in0=bank2(psB[:, 0, :]), in1=g13, op=ALU.mult).then_inc(vscaled, 1)
                dve.wait_ge(vscaled, t + 1)
                V.tensor_tensor(out=vmix[:, t], in0=vmix[:, t], in1=vv(t), op=ALU.mult).then_inc(vmixed, 1)

            def spread_queries(n):
                t, hh = divmod(n, 2)
                if n == 0:
                    dve.wait_ge(qx_zero, 1)
                if n >= 2:
                    dve.wait_ge(y_done, n - 1)
                dve.wait_ge(qa_made, t + 1)
                for dst, src in ((qx, q_tok), (qax, qa_tok)):
                    for r in range(4):
                        rr = slice(32 * r, 32 * r + 32)
                        last = V.transpose(dst[rr, 4 * hh:4 * hh + 4, r, :],
                                           src[rr, t, hh * P:(hh + 1) * P].rearrange("p (g i) -> p g i", i=32))
                last.then_inc(qx_made, 1)

            def own_sequence(n):
                t, hh = divmod(n, 2)
                dve.wait_ge(y_done, n + 1)
                yv = y[:, t, hh * P:(hh + 1) * P].rearrange("p (g i) -> p g i", i=32)
                ps = y_bank(n).rearrange("p (g b i) -> p g b i", b=4, i=32)
                V.tensor_scalar(yv, ps[:, :, 0, :], mask_seq[:, 0:1], None, ALU.mult).then_inc(y_step, 1)
                for j in range(1, 4):
                    dve.wait_ge(y_step, 3 * n + j)
                    ins = V.scalar_tensor_tensor(out=yv, in0=ps[:, :, j, :], scalar=mask_seq[:, j:j + 1],
                                                 in1=yv, op0=ALU.mult, op1=ALU.add)
                    ins.then_inc(y_step if j < 3 else y_made, 1)

            def s12_step(n):
                dve.wait_ge(s1_masked, n + 1)
                V.tensor_tensor(out=s12[:, n % 2, :], in0=s12[:, n % 2, :], in1=psA[:, 1, :],
                                op=ALU.mult).then_inc(s12_made, 1)

            def y_stats(pr):
                dve.wait_ge(y_made, 4 * pr + 4)
                stats(LN_Y, pr, y)

            def wo_residual(pr):
                dve.wait_ge(wo_done, pr + 1)
                dve.wait_ge(hbo_made, pr + 1)
                V.tensor_tensor(out=pair(h, pr), in0=bank2(psA[:, 2 + pr, :]), in1=pair(haux, pr), op=ALU.add).then_inc(h1_made, 1)
                dve.wait_ge(h1_made, pr + 1)
                stats(LN_FFN, pr, h)

            def tok2(m):
                return m.unsqueeze(1).to_broadcast([P, 2, NB])

            def slot2(m):
                return m.unsqueeze(2).to_broadcast([P, 2, NB])

            def router_scores(pr):
                normalise(LN_FFN, pr, h, u)
                dve.wait_ge(ln_out[pr], LN_FFN)
                for t in (2 * pr, 2 * pr + 1):
                    V.scalar_tensor_tensor(out=y[:, t, :], in0=u[:, t, :], scalar=1.0, in1=R['L0_ffn_w_router'],
                                           op0=ALU.mult, op1=ALU.mult, accum_out=score[:, t:t + 1]).then_inc(score_made, 1)
                dve.wait_ge(score_made, 2 * pr + 2)
                part = slice(2 * pr, 2 * pr + 2)
                V.tensor_tensor(out=sc_rhs[:, part, :], in0=slot2(score[:, part]), in1=tok2(slot[:, :]), op=ALU.mult).then_inc(score_rhs, 1)

            def router_select(pr):
                part = slice(2 * pr, 2 * pr + 2)
                dve.wait_ge(score_all, pr + 1)
                allsc = psB[:, 2 + pr, 0:2 * NB].rearrange("p (t j) -> p t j", t=2)
                own, higher, tied = (sc_t[:, n, part] for n in range(3))
                step(V.tensor_tensor(out=own, in0=allsc, in1=tok2(slot[:, :]), op=ALU.mult))
                step(V.tensor_reduce(out=sc_self[:, part], in_=own, axis=AX.X, op=ALU.add))
                V.tensor_tensor(out=higher, in0=allsc, in1=slot2(sc_self[:, part]), op=ALU.is_gt)
                step(V.tensor_tensor(out=tied, in0=allsc, in1=slot2(sc_self[:, part]), op=ALU.is_equal))
                step(V.tensor_tensor(out=tied, in0=tied, in1=tok2(slot_lt[:, :]), op=ALU.mult))
                step(V.tensor_tensor(out=higher, in0=higher, in1=tied, op=ALU.add))
                step(V.tensor_reduce(out=rank[:, part], in_=higher, axis=AX.X, op=ALU.add))
                V.tensor_scalar(sel[:, 0, part], rank[:, part], TOPK - 0.5, None, ALU.is_lt)
                V.tensor_scalar(sel[:, 1, part], rank[:, part], TOPK - 0.5, None, ALU.is_gt).then_inc(sel_made, 1)
                dve.wait_ge(sel_made, pr + 1)
                for t in (2 * pr, 2 * pr + 1):
                    V.scalar_tensor_tensor(out=h[:, t, :], in0=u[:, t, :], scalar=sel[:, 1, t:t + 1], in1=h[:, t, :],
                                           op0=ALU.mult, op1=ALU.add).then_inc(kept, 1)

            def ffn_residual(pr):
                dve.wait_ge(gelu_done, pr + 1)
                for t in (2 * pr, 2 * pr + 1):
                    dve.wait_ge(kept, t + 1)
                    V.scalar_tensor_tensor(out=h[:, t, :], in0=g_act[:, t, :], scalar=sel[:, 0, t:t + 1], in1=h[:, t, :],
                                           op0=ALU.mult, op1=ALU.add).then_inc(h2_made, 1)
                dve.wait_ge(h2_made, 2 * pr + 2)
                stats(LN_L1, pr, h)

            def l1_norm(pr):
                normalise(LN_L1, pr, h, u)
                part = slice(2 * pr, 2 * pr + 2)
                V.scalar_tensor_tensor(out=uvar[:, part], in0=mv[:, part, 1], scalar=1.0, in1=rs[:, part],
                                       op0=ALU.mult, op1=ALU.mult).then_inc(uvar_step, 1)
                dve.wait_ge(uvar_step, 2 * pr + 1)
                V.tensor_tensor(out=uvar[:, part], in0=uvar[:, part], in1=rs[:, part], op=ALU.mult).then_inc(uvar_step, 1)

            def u_norm(pr):
                part = slice(2 * pr, 2 * pr + 2)
                dve.wait_ge(usd_made, pr + 1)
                V.reciprocal(urs[:, part], usd[:, part]).then_inc(urs_made, 1)
                dve.wait_ge(urs_made, pr + 1)
                dve.wait_ge(ln_out[pr], LN_L1)
                for t in (2 * pr, 2 * pr + 1):
                    last = V.tensor_scalar(y[:, t, :], u[:, t, :], urs[:, t:t + 1], None, ALU.mult)
                last.then_inc(un_made, 1)

            def spiral_residual(pr):
                dve.wait_ge(spiral_done, pr + 1)
                dve.wait_ge(u_last, pr + 1)
                V.tensor_tensor(out=pair(y, pr), in0=bank2(psB[:, 2 + pr, :]), in1=pair(g_act, pr), op=ALU.add).then_inc(x1_made, 1)
                dve.wait_ge(x1_made, pr + 1)
                stats(LN_MLP, pr, y)

            def mlp_residual(pr):
                dve.wait_ge(w2_done, pr + 1)
                dve.wait_ge(hx_made, 2 * pr + 2)
                V.tensor_tensor(out=pair(h, pr), in0=bank2(psA[:, 2 + pr, :]), in1=pair(haux, pr), op=ALU.add).then_inc(h3_made, 1)
                dve.wait_ge(h3_made, pr + 1)
                stats(LN_CB, pr, h)

            def cb_residual(pr):
                dve.wait_ge(cb_done, pr + 1)
                V.tensor_tensor(out=pair(y, pr), in0=bank2(psA[:, 2 + pr, :]), in1=row2('L1_ffn_SCB'), op=ALU.mult).then_inc(cb_scaled, 1)
                dve.wait_ge(cb_scaled, pr + 1)
                dve.wait_ge(hb_made, pr + 1)
                V.tensor_tensor(out=pair(h, pr), in0=pair(y, pr), in1=pair(haux, pr), op=ALU.add).then_inc(out_made, 1)

            dve.wait_ge(rows_in, 16 * (len(ROWS) + 5))
            tok_bias(0)
            dve.wait_ge(bpos_made, 1)
            tok_norm(0)
            plus_identity(2)
            normalise(LN_ATTN, 0, h, u)
            plus_identity(3)
            plus_identity(4)
            for part, factor in ((slice(0, 2), 1.0 / (NB * NB)), (slice(2, 4), 1.0)):
                V.tensor_scalar(g_rows[:, part, :].rearrange("p a (h e) -> p (a h) e", h=HEADS),
                                g_raw[:, part, :].rearrange("p a h -> p (a h)").unsqueeze(2).to_broadcast([P, 2 * HEADS, D // HEADS]),
                                factor, None, ALU.mult)
            step(V.tensor_scalar(R['L1_ffn_SCB'], R['L1_ffn_SCB'], 1.0 / 127.0, None, ALU.mult))

            tok_bias(1)
            q_bias_add(0)
            tok_norm(1)
            dve.wait_ge(cols_T, 2)
            V.tensor_copy(last_tok[:, :], psB[:, 0, 0:D]).then_inc(last_tok_made, 1)
            normalise(LN_ATTN, 1, h, u)
            kv_bias_add(0)
            q_bias_add(1)
            kv_bias_add(1)
            for t in (2, 3):
                mix_values(t - 2)
                q_bias_add(t)
                kv_bias_add(t)
            for t in (2, 3):
                mix_values(t)
            spread_queries(0)
            spread_queries(1)
            for n in range(STEPS):
                if n == 5:
                    normalise(LN_Y, 0, y, y)
                if n == 6:
                    wo_residual(0)
                if n == 7:
                    router_select(0)
                s12_step(n)
                if n == 6:
                    router_scores(0)
                if n >= 5:
                    spread_queries(n)
                if n == 7:
                    ffn_residual(0)
                if n >= 1:
                    own_sequence(n - 1)
                if n == 4:
                    y_stats(0)
                if 1 <= n <= 3:
                    spread_queries(n + 1)
            own_sequence(STEPS - 1)
            y_stats(1)
            l1_norm(0)
            normalise(LN_Y, 1, y, y)
            u_norm(0)
            wo_residual(1)
            router_scores(1)
            spiral_residual(0)
            normalise(LN_MLP, 0, y, u)
            router_select(1)
            ffn_residual(1)
            l1_norm(1)
            u_norm(1)
            spiral_residual(1)
            normalise(LN_MLP, 1, y, u)
            mlp_residual(0)
            normalise(LN_CB, 0, h, u)
            cb_residual(0)
            mlp_residual(1)
            normalise(LN_CB, 1, h, u)
            cb_residual(1)

        @block.tensor
        def _(pe):
            T = nc.tensor.transpose
            M = nc.tensor.matmul
            pe.wait_ge(consts_made, 1)
            for n in range(16):
                dh, kk = divmod(n, 8)
                if kk == 0:
                    pe.wait_ge(conv_w_in[2 * dh], 16)
                    pe.wait_ge(conv_w_in[2 * dh + 1], 16)
                if n >= 4:
                    m = n - 4
                    if m % 2 == 0:
                        pe.wait_ge(small_evac, m // 2 + 1)
                    else:
                        pe.wait_ge(w_evac_dve, m // 2 + 1)
                for k in range(2):
                    for oh in range(DH):
                        last = T(psB[:, n % 4, (2 * k + oh) * P:(2 * k + oh + 1) * P],
                                 conv_raw[:, oh, dh * P:(dh + 1) * P, 2 * kk + k], ident[:, :])
                last.then_inc(w_T, 1)
            pe.wait_ge(cols_in, 16 * (len(COLS) + 1))
            for hh in range(DH):
                last = T(psA[:, 2, hh * NCOL:(hh + 1) * NCOL], colrow[:, hh * P:(hh + 1) * P], ident[0:NCOL, 0:NCOL])
            last.then_inc(cols_T, 1)
            pe.wait_ge(small_evac, 6)
            pe.wait_ge(w_evac_dve, 6)

            def transpose_quad(n):
                i, q = divmod(n, QUADS)
                if q % (QUADS // 2) == 0:
                    pe.wait_ge(x_in_half[q // (QUADS // 2)], 32 * (i + 1))
                pe.wait_ge(ring_drained, n + 1)
                for k in range(2):
                    for dh in range(DH):
                        last = T(psB[:, q % 4, (2 * k + dh) * P:(2 * k + dh + 1) * P],
                                 x_in[:, 2 * q + k, dh * P:(dh + 1) * P], ident[:, :])
                last.then_inc(quad_T, 1)

            def conv_quad(n):
                i, q = divmod(n, QUADS)
                if q == 0 and i >= 2:
                    pe.wait_ge(conv_bank_free, i - 1)
                pe.wait_ge(ring_drained, 4 + n + 1)
                for k in range(2):
                    for dh in range(DH):
                        last = M(psA[:, i % 2, 0:D], xT[:, i % 2, 2 * q + k, dh * P:(dh + 1) * P], wT[:, 2 * q + k, dh, :],
                                 start=(q == 0 and k == 0 and dh == 0), stop=(q == QUADS - 1 and k == 1 and dh == 1))
                if q == QUADS - 1:
                    last.then_inc(conv_done, 1)

            order = [('p', 0), ('p', 1), ('p', 2), ('s', 5), ('s', 6), ('s', 0), ('s', 1), ('s', 2), ('s', 3), ('s', 4)]

            def small_quad(n):
                if n == 0:
                    pe.wait_ge(raw_in, 16 * (2 + len(SMALL)))
                    pe.wait_ge(ring_drained, 4 + TILES * QUADS)
                if n >= 4:
                    m = n - 4
                    if m < 5:
                        pe.wait_ge(small_evac, 6 + m + 1)
                    else:
                        pe.wait_ge(w_evac_dve, 6 + m - 5 + 1)
                kind, j = order[n]
                for c in range(2):
                    for oh in range(DH):
                        if kind == 's':
                            src = small_raw[:, j, oh, c * P:(c + 1) * P]
                        else:
                            src = proj_raw[:, oh, (2 * j + c) * P:(2 * j + c + 1) * P]
                        last = T(psB[:, n % 4, (2 * c + oh) * P:(2 * c + oh + 1) * P], src, ident[:, :])
                last.then_inc(small_T, 1)

            def ahead(m):
                return m + 5 if m < QUADS // 2 else 2 * m + 2 if m < QUADS else m + QUADS + 1

            def conv_tokens_T(pr):
                if pr == 0:
                    pe.wait_ge(cols_out, 2)
                pe.wait_ge(conv_bank_free, 2 * pr + 2)
                for hh in range(DH):
                    for t in range(2):
                        last = T(psA[:, (2, 0)[pr], (2 * hh + t) * P:(2 * hh + t + 1) * P],
                                 conv_tok[:, 2 * pr + t, hh * P:(hh + 1) * P], ident[:, :])
                last.then_inc(conv_T, 1)

            def project(pr):
                pe.wait_ge(small_evac, 6 + 3)
                pe.wait_ge(conv_comb, pr + 1)
                pe.wait_ge(std_made, pr + 1)
                pe.wait_ge(max_done, 2 + 2 * pr + 2)
                for t in (2 * pr, 2 * pr + 1):
                    if t == TILES - 1:
                        attn_T(0)
                    for c in range(3 * DH):
                        last = M(psA[:, (3, 1)[pr], (t % 2) * D:(t % 2 + 1) * D], comb[:, c, t * P:(t + 1) * P], projT[:, c, :],
                                 start=(c == 0), stop=(c == 3 * DH - 1))
                last.then_inc(proj_done, 1)

            def transpose_pair(s, pr, src):
                for hh in range(DH):
                    for t in range(2):
                        last = T(psB[:, 2 + pr, (2 * hh + t) * P:(2 * hh + t + 1) * P],
                                 src[:, 2 * pr + t, hh * P:(hh + 1) * P], ident[:, :])
                last.then_inc(trans_done[pr], 1)

            def attn_T(pr):
                pe.wait_ge(ln_out[pr], LN_ATTN)
                transpose_pair(T_ATTN, pr, u)

            done = 0
            for m in range(TILES * QUADS):
                while done < ahead(m):
                    if done < TILES * QUADS:
                        transpose_quad(done)
                    else:
                        small_quad(done - TILES * QUADS)
                    done += 1
                if m == TILES * QUADS - 4:
                    conv_tokens_T(0)
                if m == TILES * QUADS - 2:
                    project(0)
                conv_quad(m)
            for n in range(done - TILES * QUADS, len(order)):
                small_quad(n)
            conv_tokens_T(1)
            project(1)
            pe.wait_ge(last_rep, 1)
            pe.wait_ge(w_evac_dve, 6 + 5)
            pe.wait_ge(small_evac, 6 + 5)
            for dh in range(DH):
                last = T(psB[:, 0, dh * P:(dh + 1) * P], lastT[:, dh, :, :], ident[:, :])
            last.then_inc(cols_T, 1)

            def linear_pair(pr, lhs, rhs, chunks, done):
                for t in range(2):
                    for c in range(chunks):
                        last = M(psA[:, 2 + pr, t * D:(t + 1) * D], lhs[:, c, (2 * pr + t) * P:(2 * pr + t + 1) * P], rhs[:, c, :],
                                 start=(c == 0), stop=(c == chunks - 1))
                last.then_inc(done, 1)

            def keys_queries(t):
                if t % 2 == 0:
                    pe.wait_ge(trans_evac[t // 2], T_ATTN + 1)
                if t >= 1:
                    pe.wait_ge(q_biased, t)
                for c in range(DH):
                    last = M(psB[:, 1, 0:D], uT[:, c, t * P:(t + 1) * P], wqT[:, c, :], start=(c == 0), stop=(c == DH - 1))
                last.then_inc(q_done, 1)
                if t == 1:
                    pe.wait_ge(proj_biased, PAIRS)
                if t >= 2:
                    pe.wait_ge(kv_biased, 2 * (t - 1))
                for j in range(2):
                    for c in range(DH):
                        last = M(kv_bank(t, j), uT[:, c, t * P:(t + 1) * P], wkvT[:, c, 512 * j:512 * j + 512],
                                 start=(c == 0), stop=(c == DH - 1))
                    last.then_inc(kv_done, 1)

            def value_sums(t):
                pe.wait_ge(kv_biased, 2 * t + 2)
                if t == 0:
                    pe.wait_ge(last_tok_made, 1)
                else:
                    pe.wait_ge(vscaled, t)
                for j in range(2):
                    v = kv[:, t, 768:1024] if j == 0 else kv[:, t, 256:512]
                    last = M(psB[:, 0, j * D:(j + 1) * D], same_seq[:, :], v, start=True, stop=True)
                last.then_inc(vsum_done, 1)

            def keys_values(n, bank, terms):
                t, hh = divmod(n, 2)
                for g in range(4):
                    for m, (which, v) in enumerate(terms):
                        G = 4 * hh + g
                        last = M(bank[:, g * P:(g + 1) * P].rearrange("p (b i) -> p b i", b=4),
                                 kx[:, t % 2, which, G, :, :], v[:, :, 32 * G:32 * G + 32],
                                 start=(m == 0), stop=(m == len(terms) - 1))
                return last

            def s_step(n):
                t = n // 2
                pe.wait_ge(kx_made, t + 1)
                pe.wait_ge(vx_plain, t + 1)
                if n == 0:
                    pe.wait_ge(kv_biased, 2 * TILES)
                else:
                    pe.wait_ge(s12_made, n)
                keys_values(n, psA[:, 0, :], ((0, vxp[t % 2][:, 0]),))
                keys_values(n, psA[:, 1, :], ((1, vxp[t % 2][:, 1]),)).then_inc(s_done, 1)

            def mix_step(n):
                t = n // 2
                pe.wait_ge(vx_mixed, t + 1)
                if n == 0:
                    pe.wait_ge(vscaled, TILES)
                else:
                    pe.wait_ge(smix_masked, n)
                keys_values(n, psB[:, 0, :], ((0, vxm[t % 2][:, 0]), (1, vxm[t % 2][:, 1]))).then_inc(smix_done, 1)

            def query_step(n):
                t, hh = divmod(n, 2)
                pe.wait_ge(qx_made, n + 1)
                pe.wait_ge(s12_made, n + 1)
                pe.wait_ge(smix_masked, n + 1)
                if n == 0:
                    pe.wait_ge(q_biased, TILES)
                if n >= 2:
                    pe.wait_ge(y_made, n - 1)
                for g in range(4):
                    for m, (q, s) in enumerate(((qx, smix), (qax, s12))):
                        last = M(y_bank(n)[:, g * P:(g + 1) * P], q[:, 4 * hh + g, :, :], s[:, n % 2, g * P:(g + 1) * P],
                                 start=(m == 0), stop=(m == 1))
                last.then_inc(y_done, 1)

            def after_ln_T(s, pr, src, made, count):
                pe.wait_ge(made, count)
                transpose_pair(s, pr, src)

            def after_T(s, pr):
                pe.wait_ge(trans_evac[pr], s + 1)

            def wo_linear(pr):
                after_T(T_WO, pr)
                linear_pair(pr, uT, woT, DH, wo_done)

            def ffn_linear(pr):
                after_T(T_FFN, pr)
                linear_pair(pr, uT, wblk, DH, blk_done)
                pe.wait_ge(score_rhs, pr + 1)
                M(psB[:, 2 + pr, 0:2 * NB], same_seq[:, :], sc_rhs[:, 2 * pr:2 * pr + 2, :].rearrange("p t j -> p (t j)"),
                  start=True, stop=True).then_inc(score_all, 1)

            def spiral_filter(pr):
                after_T(T_SPIRAL, pr)
                for dh in range(DH):
                    seqs = slice(256 * pr, 256 * pr + 256)
                    o = psA[:, 2 + pr, dh * D:(dh + 1) * D].rearrange("p (b n) -> p b n", n=NB)
                    i = uT[:, dh, seqs].rearrange("p (b n) -> p b n", n=NB)
                    for tau in range(NB):
                        last = M(o[:, :, tau:NB], diagF[:, dh, tau, :], i[:, :, 0:NB - tau], start=(tau == 0), stop=(tau == NB - 1))
                last.then_inc(filt_conv, 1)

            def spiral_back(pr):
                pe.wait_ge(filt_out, pr + 1)
                for t in range(2):
                    for dh in range(DH):
                        last = T(psB[:, 2 + pr, t * D + dh * P:t * D + (dh + 1) * P],
                                 filtT[:, dh, (2 * pr + t) * P:(2 * pr + t + 1) * P], ident[:, :])
                last.then_inc(spiral_done, 1)

            def w1_chunk(pr, c):
                n = FC * pr + c
                if n >= 4:
                    pe.wait_ge(silu_done, n - 3)
                for k in range(DH):
                    last = M(w1_bank(n)[:, 0:2 * P], w1[:, k, c * P:(c + 1) * P], uT[:, k, 2 * P * pr:2 * P * (pr + 1)],
                             start=(k == 0), stop=(k == DH - 1))
                last.then_inc(w1_done, 1)

            def w2_linear(pr):
                pe.wait_ge(silu_done, FC * (pr + 1))
                linear_pair(pr, gT, w2, FC, w2_done)

            def cb_linear(pr):
                after_T(T_CB, pr)
                linear_pair(pr, uT, cbT, DH, cb_done)

            keys_queries(0)
            keys_queries(1)
            attn_T(1)
            for t in (2, 3):
                value_sums(t - 2)
                keys_queries(t)
            for t in (2, 3):
                value_sums(t)
            for n in range(STEPS):
                s_step(n)
                mix_step(n)
                if n == 5:
                    after_ln_T(T_WO, 0, y, ln_out[0], LN_Y)
                if n == 6:
                    after_ln_T(T_FFN, 0, u, ln_out[0], LN_FFN)
                if n >= 1:
                    query_step(n - 1)
                if n == 5:
                    wo_linear(0)
                if n == 6:
                    ffn_linear(0)
            query_step(STEPS - 1)
            after_ln_T(T_WO, 1, y, ln_out[1], LN_Y)
            after_ln_T(T_SPIRAL, 0, y, un_made, 1)
            wo_linear(1)
            pe.wait_ge(diag_made, DH)
            spiral_filter(0)
            after_ln_T(T_FFN, 1, u, ln_out[1], LN_FFN)
            spiral_back(0)
            ffn_linear(1)
            after_ln_T(T_MLP, 0, u, ln_out[0], LN_MLP)
            pe.wait_ge(late_in, 32)
            after_T(T_MLP, 0)
            for c in range(FC):
                if c == 4:
                    after_ln_T(T_SPIRAL, 1, y, un_made, 2)
                if c == 6:
                    spiral_filter(1)
                w1_chunk(0, c)
            spiral_back(1)
            w2_linear(0)
            after_ln_T(T_MLP, 1, u, ln_out[1], LN_MLP)
            after_T(T_MLP, 1)
            for c in range(FC):
                if c == FC - 2:
                    after_ln_T(T_CB, 0, u, ln_out[0], LN_CB)
                w1_chunk(1, c)
            cb_linear(0)
            w2_linear(1)
            after_ln_T(T_CB, 1, u, ln_out[1], LN_CB)
            cb_linear(1)


def kernel(**inputs):
    import numpy as _np
    import concourse.bacc as _bacc
    from concourse import mybir as _mybir
    from concourse.bass_utils import run_bass_kernel_spmd as _run

    nc = _bacc.Bacc("TRN2", target_bir_lowering=False, num_devices=1)
    arrays, args = {}, {}
    for name in _INS:
        v = _np.ascontiguousarray(inputs[name])
        arrays[f"in_{name}"] = v
        args[name] = nc.dram_tensor(f"in_{name}", v.shape, _mybir.dt.from_np(v.dtype), kind="ExternalInput").ap()
    out = nc.dram_tensor("out_0", (64, 8, 256), _mybir.dt.float32, kind="ExternalOutput").ap()
    build_tower(nc, args, out)
    r = _run(nc, [arrays], core_ids=[0])
    return r.results[0]["out_0"]
```

```python
from contextlib import ExitStack

import concourse.bass as bass
from concourse import mybir

F32 = mybir.dt.float32
ALU = mybir.AluOpType
ACT = mybir.ActivationFunctionType
AX = mybir.AxisListType

P = 128
EPS = 1e-5

_INS = ['x', 'L0_tok_conv_w', 'L0_tok_conv_b', 'L0_tok_proj_w', 'L0_tok_proj_b', 'L0_tok_ln_g', 'L0_tok_ln_b',
        'L0_tok_pos_table', 'L0_attn_Wq', 'L0_attn_bq', 'L0_attn_Wk1', 'L0_attn_bk1', 'L0_attn_Wk2', 'L0_attn_bk2',
        'L0_attn_Wv1', 'L0_attn_bv1', 'L0_attn_Wv2', 'L0_attn_bv2', 'L0_attn_g1', 'L0_attn_g2', 'L0_attn_g3',
        'L0_attn_g4', 'L0_attn_ln_g', 'L0_attn_ln_b', 'L0_attn_Wo', 'L0_attn_bo', 'L0_ffn_w_router',
        'L0_ffn_w_block', 'L1_attn_ln_gamma', 'L1_attn_ln_beta', 'L1_attn_phazor_re', 'L1_attn_phazor_im',
        'L1_attn_phazor_init_re', 'L1_attn_phazor_init_im', 'L1_attn_last_conv_re', 'L1_attn_last_conv_im',
        'L1_attn_w1', 'L1_attn_b1', 'L1_attn_w2', 'L1_attn_b2', 'L1_ffn_CB', 'L1_ffn_SCB', 'L1_ffn_bias']


def build_tower(nc, a, out):
    NSEQ, NFRAME, D = a['x'].shape
    KB = a['L0_tok_conv_w'].shape[2]
    NB = -(-NFRAME // KB)
    LAST = NFRAME - (NB - 1) * KB
    HEADS = a['L0_attn_g1'].shape[0]
    FF = a['L1_attn_w1'].shape[1]
    DH = D // P
    TILES = NSEQ * NB // P
    SEQ = P // NB
    PAIRS = TILES // 2
    QUADS = KB * DH // 4
    FC = FF // P
    TOPK = max(1, int(NB * 0.75))
    N = NSEQ * NB
    assert (D, KB, NB, TILES, HEADS) == (256, 16, 8, 4, 16)

    ctx = ExitStack()
    with ctx:
        def sb(name, shape):
            return ctx.enter_context(nc.sbuf_tensor(name, shape, F32))

        def sem(name):
            return ctx.enter_context(nc.semaphore(name))

        psA = ctx.enter_context(nc.psum_tensor("psA", [P, 4, 512], F32))
        psB = ctx.enter_context(nc.psum_tensor("psB", [P, 4, 512], F32))

        region_x = sb("region_x", [P, KB * D])
        region_xT = sb("region_xT", [P, 2 * KB * D])
        region_wT = sb("region_wT", [P, KB * DH * D])
        region_raw = sb("region_raw", [P, DH * KB * D])
        proj_space = sb("proj_space", [P, 4 * DH * 3 * P])
        x_in = region_x[:, :].rearrange("p (k d) -> p k d", k=KB)
        xT = region_xT[:, :].rearrange("p (s k f) -> p s k f", s=2, k=KB)
        wT = region_wT[:, :].rearrange("p (k h o) -> p k h o", k=KB, h=DH)
        conv_raw = region_raw[:, :].rearrange("p (o d k) -> p o d k", o=DH, k=KB)
        centred = region_raw[:, 0:KB * D].rearrange("p (k f) -> p k f", k=KB)
        SMALL = ['L0_attn_Wq', 'L0_attn_Wk1', 'L0_attn_Wv1', 'L0_attn_Wk2', 'L0_attn_Wv2', 'L0_attn_Wo', 'L1_ffn_CB']
        small_raw = region_raw[:, KB * D:KB * D + 7 * 512].rearrange("p (w o i) -> p w o i", w=7, o=DH)

        h = region_raw[:, 0:1024].rearrange("p (t f) -> p t f", t=4)
        haux = region_raw[:, 1024:2048].rearrange("p (t f) -> p t f", t=4)
        u = region_raw[:, 2048:3072].rearrange("p (t f) -> p t f", t=4)
        y = region_raw[:, 3072:4096].rearrange("p (t f) -> p t f", t=4)
        vmix = region_raw[:, 4608:6656].rearrange("p (t v f) -> p t v f", t=4, v=2)
        lastT = region_raw[:, 4096:4352].rearrange("p (h b n) -> p h b n", h=DH, n=NB)

        w1 = region_x[:, 0:DH * FF].rearrange("p (h f) -> p h f", h=DH)
        w2 = region_x[:, DH * FF:DH * FF + FC * D].rearrange("p (c d) -> p c d", c=FC)
        kv = region_xT[:, 0:4096].rearrange("p (t f) -> p t f", t=4)
        gT = region_xT[:, 0:4096].rearrange("p (c n) -> p c n", c=FC)
        g_act = region_wT[:, 0:1024].rearrange("p (t f) -> p t f", t=4)
        uT = region_wT[:, 1024:2048].rearrange("p (h n) -> p h n", h=DH)
        q_tok = region_wT[:, 2048:3072].rearrange("p (t f) -> p t f", t=4)
        qa_tok = region_wT[:, 3072:4096].rearrange("p (t f) -> p t f", t=4)
        filtT = region_wT[:, 2048:3072].rearrange("p (h n) -> p h n", h=DH)
        s12 = region_wT[:, 4096:5120].rearrange("p (s f) -> p s f", s=2)
        smix = region_wT[:, 5120:6144].rearrange("p (s f) -> p s f", s=2)
        vxp = [region_xT[:, 4096:6144].rearrange("p (v b f) -> p v b f", v=2, b=4),
               proj_space[:, 0:2048].rearrange("p (v b f) -> p v b f", v=2, b=4)]
        vxm = [region_xT[:, 6144:8192].rearrange("p (v b f) -> p v b f", v=2, b=4),
               region_wT[:, 6144:8192].rearrange("p (v b f) -> p v b f", v=2, b=4)]

        comb = sb("comb", [P, 3 * DH, N])
        comb_cols = comb[:, :, :].rearrange("p a n -> p (a n)")
        kx = sb("kx", [P, 2, 2, 8, 4, 32])
        qx = comb_cols[:, 0:1024].rearrange("p (g r i) -> p g r i", g=8, r=4)
        qax = comb_cols[:, 1024:2048].rearrange("p (g r i) -> p g r i", g=8, r=4)
        conv_tok = sb("conv_tok", [P, TILES, D])
        proj_raw = proj_space[:, 0:DH * 3 * D].rearrange("p (o i) -> p o i", o=DH)
        projT = proj_space[:, DH * 3 * D:2 * DH * 3 * D].rearrange("p (c o) -> p c o", o=D)
        wqT = sb("wqT", [P, DH, D])
        wkvT = sb("wkvT", [P, DH, 4 * D])
        woT = sb("woT", [P, DH, D])
        cbT = sb("cbT", [P, DH, D])
        wblk = sb("wblk", [P, DH, D])
        diagF = sb("diagF", [P, DH, NB, P])
        negmean = sb("negmean", [P, D])
        ssq_hi = sb("ssq_hi", [P, D])
        ROWS = ['L0_tok_proj_b', 'L0_tok_ln_g', 'L0_tok_ln_b', 'L0_attn_bk1', 'L0_attn_bv1', 'L0_attn_bk2',
                'L0_attn_bv2', 'L0_attn_bq', 'L0_attn_bo', 'L0_ffn_w_router', 'L1_attn_b2', 'L1_ffn_SCB', 'L1_ffn_bias']
        rows = sb("rows", [P, len(ROWS), D])
        g_rows = sb("g_rows", [P, 4, D])
        g13 = g_rows[:, 0:2, :]
        pos = sb("pos", [P, D])
        COLS = ['L0_tok_conv_b', 'L0_attn_ln_g', 'L0_attn_ln_b', 'L1_attn_ln_gamma',
                'L1_attn_ln_beta', 'L1_attn_phazor_re', 'L1_attn_phazor_im', 'L1_attn_phazor_init_re',
                'L1_attn_phazor_init_im', 'L1_attn_last_conv_re', 'L1_attn_last_conv_im']
        NCOL = len(COLS) + FF // D
        last_tok = sb("last_tok", [P, D])
        colrow = last_tok[0:NCOL, :]
        g_raw = sb("g_raw", [P, 4, HEADS])
        col = sb("col", [P, DH, NCOL])
        ident = sb("ident", [P, P])
        ident2 = sb("ident2", [P, 512])
        ones = sb("ones", [P, P])
        seq16 = sb("seq16", [P, SEQ])
        same_seq = sb("same_seq", [P, P])
        before = sb("before", [P, P])
        head8 = sb("head8", [P, 8])
        mask_seq = sb("mask_seq", [P, 4])
        mask_head = sb("mask_head", [P, 2])
        mask_head64 = sb("mask_head64", [P, 2])
        slot = sb("slot", [P, NB])
        slot_lt = sb("slot_lt", [P, NB])
        eps = sb("eps", [P, 1])
        scratch = sb("scratch", [P, 10])
        pw = sb("pw", [P, 2, NB + 1, DH])
        pt = sb("pt", [P, 4, NB, DH])
        filt = sb("filt", [P, NB, DH])
        lastf = sb("lastf", [P, NB, DH])
        mag = sb("mag", [P, 6, DH])
        st = sb("st", [P, TILES, 6])
        mv = sb("mv", [P, TILES, 2])
        sd = sb("sd", [P, TILES])
        rs = sb("rs", [P, TILES])
        uvar, usd, urs = sb("uvar", [P, TILES]), sb("usd", [P, TILES]), sb("urs", [P, TILES])
        score = sb("score", [P, TILES])
        sc_rhs = sb("sc_rhs", [P, TILES, NB])
        sc_t = sb("sc_t", [P, 3, TILES, NB])
        sc_self = sb("sc_self", [P, TILES])
        rank = sb("rank", [P, TILES])
        sel = sb("sel", [P, 2, TILES])

        R = {n: rows[:, j, :] for j, n in enumerate(ROWS)}
        kv_bias = rows[:, 3:7, :].rearrange("p a f -> p (a f)")

        def vec(name, half):
            return col[:, half, COLS.index(name):COLS.index(name) + 1]

        def both(name):
            return col[:, :, COLS.index(name)]

        cols_in, rows_in, raw_in, late_in = sem("cols_in"), sem("rows_in"), sem("raw_in"), sem("late_in")
        conv_w_in = [sem(f"conv_w_in{n}") for n in range(2 * DH)]
        x_in_half = [sem("x_in_lo"), sem("x_in_hi")]
        out_stored = sem("out_stored")
        pool_step, masks_made, consts_made = sem("pool_step"), sem("masks_made"), sem("consts_made")
        x_pad_zero = sem("x_pad_zero")
        cols_out = sem("cols_out")
        cols_T, dve_step, mag2_made, mag_made, decay_made = (sem(n) for n in (
            "cols_T", "dve_step", "mag2_made", "mag_made", "decay_made"))
        filt_made, diag_made, last_rep = sem("filt_made"), sem("diag_made"), sem("last_rep")
        w_T, w_evac_act, w_evac_dve = sem("w_T"), sem("w_evac_act"), sem("w_evac_dve")
        quad_T = sem("quad_T")
        ring_drained = sem("ring_drained")
        conv_bank_free = sem("conv_bank_free")
        conv_done = sem("conv_done")
        negsum, mean_made = sem("negsum"), sem("mean_made")
        max_done = sem("max_done")
        centred_done = sem("centred_done")
        squared, ssq_half = sem("squared"), sem("ssq_half")
        ssq_done = sem("ssq_done")
        small_T, small_evac = sem("small_T"), sem("small_evac")
        std_made, conv_T, conv_comb = sem("std_made"), sem("conv_T"), sem("conv_comb")
        proj_done, proj_biased = sem("proj_done"), sem("proj_biased")
        ln_stat, ln_mv, ln_sd, ln_rs, ln_out, trans_done, trans_evac = (
            [sem(f"{n}{pr}") for pr in range(PAIRS)]
            for n in ("ln_stat", "ln_mv", "ln_sd", "ln_rs", "ln_out", "trans_done", "trans_evac"))
        tok_scaled, tok_out, bpos_made = sem("tok_scaled"), sem("tok_out"), sem("bpos_made")
        kv_done, kv_biased = sem("kv_done"), sem("kv_biased")
        q_done, q_biased, qa_scaled, qa_made = sem("q_done"), sem("q_biased"), sem("qa_scaled"), sem("qa_made")
        kx_made, qx_zero, qx_made = sem("kx_made"), sem("qx_zero"), sem("qx_made")
        uvar_step, usd_made, urs_made, un_made = sem("uvar_step"), sem("usd_made"), sem("urs_made"), sem("un_made")
        vsum_done, vscaled, vmixed = sem("vsum_done"), sem("vscaled"), sem("vmixed")
        vx_plain, vx_mixed = sem("vx_plain"), sem("vx_mixed")
        s_done, s1_masked, s12_made = sem("s_done"), sem("s1_masked"), sem("s12_made")
        smix_done, smix_masked = sem("smix_done"), sem("smix_masked")
        y_done, y_step, y_made = sem("y_done"), sem("y_step"), sem("y_made")
        hbo_made, wo_done, h1_made = sem("hbo_made"), sem("wo_done"), sem("h1_made")
        score_made, score_rhs, score_all, sel_made = (sem(n) for n in ("score_made", "score_rhs", "score_all", "sel_made"))
        blk_done, gelu_done, kept, h2_made = sem("blk_done"), sem("gelu_done"), sem("kept"), sem("h2_made")
        u_last, spiral_done, x1_made, hx_made = sem("u_last"), sem("spiral_done"), sem("x1_made"), sem("hx_made")
        last_tok_made = sem("last_tok_made")
        filt_conv, filt_out = sem("filt_conv"), sem("filt_out")
        w1_done, silu_done, w2_done, h3_made = sem("w1_done"), sem("silu_done"), sem("w2_done"), sem("h3_made")
        hb_made, cb_done, cb_scaled, out_made = sem("hb_made"), sem("cb_done"), sem("cb_scaled"), sem("out_made")

        T_ATTN, T_WO, T_FFN, T_SPIRAL, T_MLP, T_CB = range(6)
        LN_TOK, LN_ATTN, LN_Y, LN_FFN, LN_L1, LN_MLP, LN_CB = range(7)
        STEPS = 2 * TILES

        def kv_bank(t, j):
            return psA[:, 2 * ((t + 1) % 2) + j, :]

        def wT_quad(n):
            dh, oh, kk = n // 8, n // 4 % 2, n % 4
            return wT[:, 4 * kk:4 * kk + 4, dh, oh * P:(oh + 1) * P]

        def y_bank(n):
            return psB[:, 1 + 2 * (n % 2), :]

        def tail_w2(t):
            return (psA[:, 3, :], psA[:, 0, :])[t - 2]

        def tail_T(t):
            return (psB[:, 3, :], psB[:, 1, :])[t - 2]

        def tail_cb(t):
            return (psA[:, 3, :], psA[:, 1, :])[t - 2]

        def w1_bank(n):
            return (psA[:, 0, :], psA[:, 1, :], psB[:, 0, :], psB[:, 1, :])[n % 4]

        block = ctx.enter_context(nc.Block())

        @block.sync
        def _(sp):
            def load_conv_w(dh):
                for oh in range(DH):
                    sp.dma_start(conv_raw[:, oh, dh * P:(dh + 1) * P, :],
                                 a['L0_tok_conv_w'][oh * P:(oh + 1) * P, dh * P:(dh + 1) * P, :]).then_inc(conv_w_in[DH * dh + oh], 16)

            def load_x(i, half):
                k0, k1 = half * KB // 2, (half + 1) * KB // 2
                FULL = NB - 1
                sp.dma_start(x_in[0:FULL * SEQ, k0:k1, :],
                             a['x'][bass.ds(i * SEQ, SEQ), 0:FULL * KB, :].rearrange("b (n k) d -> n b k d", k=KB)[:, :, k0:k1, :]
                             .rearrange("n b k d -> n b (k d)")).then_inc(x_in_half[half], 16)
                ke = min(k1, LAST)
                sp.dma_start(x_in[FULL * SEQ:P, k0:ke, :],
                             a['x'][bass.ds(i * SEQ, SEQ), FULL * KB + k0:FULL * KB + ke, :]).then_inc(x_in_half[half], 16)

            def load_next_x(i):
                for half in range(2):
                    sp.wait_ge(quad_T, i * QUADS - QUADS // 2 + half * (QUADS // 2))
                    load_x(i, half)

            load_conv_w(0)
            sp.wait_ge(x_pad_zero, 1)
            load_x(0, 0)
            load_x(0, 1)
            load_conv_w(1)
            for j, name in enumerate(COLS):
                sp.dma_start(colrow[j:j + 1, :], a[name].rearrange("(a d) -> a d", a=1)).then_inc(cols_in, 16)
            sp.dma_start(colrow[len(COLS):NCOL, :], a['L1_attn_b1'].rearrange("(a d) -> a d", d=D)).then_inc(cols_in, 16)
            with sp.Fori(1, TILES - 1) as i:
                load_next_x(i)
            sp.dma_start(proj_raw[:, :, :], a['L0_tok_proj_w'].rearrange("(o p) i -> p o i", p=P)).then_inc(raw_in, 16)
            sp.dma_start(wblk[:, :, :], a['L0_ffn_w_block'].rearrange("(c p) e -> p c e", p=P)).then_inc(raw_in, 16)
            sp.wait_ge(w_T, 16)
            for j, name in enumerate(SMALL):
                sp.dma_start(small_raw[:, j, :, :], a[name].rearrange("(o p) i -> p o i", p=P)).then_inc(raw_in, 16)
            load_next_x(TILES - 1)
            for j, name in enumerate(ROWS):
                sp.dma_start(rows[:, j, :], a[name].partition_broadcast(P)).then_inc(rows_in, 16)
            for j, name in enumerate(('L0_attn_g1', 'L0_attn_g3', 'L0_attn_g4', 'L0_attn_g2')):
                sp.dma_start(g_raw[:, j, :], a[name].partition_broadcast(P)).then_inc(rows_in, 16)
            sp.dma_start(pos[:, :],
                         a['L0_tok_pos_table'][0:NB, :].unsqueeze(0).to_broadcast([SEQ, NB, D])).then_inc(rows_in, 16)
            sp.wait_ge(quad_T, TILES * QUADS)
            sp.dma_start(w1, a['L1_attn_w1'].rearrange("(c p) f -> p c f", p=P)).then_inc(late_in, 16)
            sp.dma_start(w2, a['L1_attn_w2'].rearrange("(c p) d -> p c d", p=P)).then_inc(late_in, 16)
            out_v = out.rearrange("b n d -> (b n) d").rearrange("(t p) d -> p t d", p=P)
            sp.wait_ge(out_made, 1)
            sp.dma_start(out_v[:, 0:2, :], h[:, 0:2, :]).then_inc(out_stored, 16)
            for t in (2, 3):
                sp.wait_ge(out_made, t)
                sp.dma_start(out_v[:, t, :], h[:, t, :]).then_inc(out_stored, 16)
            sp.wait_ge(out_stored, 16 * 3)

        @block.gpsimd
        def _(pool):
            steps = [0]

            def step(ins):
                steps[0] += 1
                ins.then_inc(pool_step, 1)
                pool.wait_ge(pool_step, steps[0])

            k_lo = LAST
            nc.gpsimd.memset(x_in[96:P, k_lo:KB, :], 0.0).then_inc(x_pad_zero, 1)
            pool.wait_ge(x_pad_zero, 1)
            nc.gpsimd.memset(ones[:, :], 1.0)
            nc.gpsimd.memset(eps[:, :], EPS)
            step(nc.gpsimd.memset(ident2[:, :], 0.0))
            step(nc.gpsimd.affine_select(out=ident[:, :], in_=ones[:, :], compare_op=ALU.is_equal, fill=0.0, base=0,
                                         pattern=[[-1, P]], channel_multiplier=1))
            step(nc.gpsimd.affine_select(out=seq16[:, :], in_=ones[:, 0:SEQ], compare_op=ALU.is_ge, fill=0.0, base=0,
                                         pattern=[[-NB, SEQ]], channel_multiplier=1))
            step(nc.gpsimd.affine_select(out=seq16[:, :], in_=seq16[:, :], compare_op=ALU.is_ge, fill=0.0, base=NB - 1,
                                         pattern=[[NB, SEQ]], channel_multiplier=-1))
            step(nc.gpsimd.affine_select(out=head8[:, :], in_=ones[:, 0:8], compare_op=ALU.is_ge, fill=0.0, base=0,
                                         pattern=[[-16, 8]], channel_multiplier=1))
            step(nc.gpsimd.affine_select(out=head8[:, :], in_=head8[:, :], compare_op=ALU.is_ge, fill=0.0, base=15,
                                         pattern=[[16, 8]], channel_multiplier=-1))
            step(nc.gpsimd.tensor_copy(same_seq[:, :].rearrange("p (b n) -> p b n", n=NB),
                                       seq16[:, :].unsqueeze(2).to_broadcast([P, SEQ, NB])))
            step(nc.gpsimd.affine_select(out=before[:, :], in_=same_seq[:, :], compare_op=ALU.is_gt, fill=0.0, base=0,
                                         pattern=[[-1, P]], channel_multiplier=1))
            nc.gpsimd.tensor_copy(ident2[:, 0:P], ident[:, :])
            nc.gpsimd.tensor_copy(ident2[:, 3 * P:4 * P], ident[:, :]).then_inc(consts_made, 1)

            for sl in range(2):
                for which in range(2):
                    nc.gpsimd.memset(kx[:, sl, which, :, :, :].rearrange("p g r i -> p (g r i)"), 0.0).then_inc(centred_done, 1)

            def centre(i):
                pool.wait_ge(mean_made, i + 1)
                for half in range(2):
                    if half == 1:
                        pool.wait_ge(ssq_done, i + 1)
                    ks = slice(half * KB // 2, (half + 1) * KB // 2)
                    nc.gpsimd.tensor_tensor(out=centred[:, ks, :],
                                            in0=xT[:, bass.ds(i % 2, 1), ks, :].rearrange("p s k f -> p (s k) f"),
                                            in1=negmean[:, :].unsqueeze(1).to_broadcast([P, KB // 2, D]),
                                            op=ALU.add).then_inc(centred_done, 1)

            def diagonals(dh):
                pool.wait_ge(filt_made, 1)
                for t in range(NB):
                    last = nc.gpsimd.tensor_scalar(diagF[:, dh, t, :], ident[:, :], filt[:, t, dh:dh + 1], None, ALU.mult)
                last.then_inc(diag_made, 1)

            pool.wait_ge(w_T, 16)
            for i in range(DH):
                centre(i)
                diagonals(i)
            with pool.Fori(DH, TILES) as i:
                centre(i)
            pool.wait_ge(rows_in, 16 * (len(ROWS) + 5))
            nc.gpsimd.tensor_tensor(out=pos[:, :], in0=pos[:, :], in1=R['L0_tok_ln_b'], op=ALU.add).then_inc(bpos_made, 1)
            pool.wait_ge(small_T, 10)
            for dh in range(DH):
                last = nc.gpsimd.tensor_copy(lastT[:, dh, :, :],
                                             lastf[:, :, dh].unsqueeze(1).to_broadcast([P, SEQ, NB]))
            last.then_inc(last_rep, 1)

            def row2(name):
                return R[name].unsqueeze(1).to_broadcast([P, 2, D])

            def pair(buf, pr):
                return buf[:, 2 * pr:2 * pr + 2, :]

            pool.wait_ge(proj_done, PAIRS)
            nc.gpsimd.memset(comb_cols[:, 0:2048], 0.0).then_inc(qx_zero, 1)

            def residual_bo(pr):
                pool.wait_ge(tok_out, pr + 1)
                nc.gpsimd.tensor_tensor(out=pair(haux, pr), in0=pair(h, pr), in1=row2('L0_attn_bo'), op=ALU.add).then_inc(hbo_made, 1)

            def scaled_queries(t):
                pool.wait_ge(q_biased, t + 1)
                nc.gpsimd.tensor_tensor(out=qa_tok[:, t, :], in0=q_tok[:, t, :], in1=g_rows[:, 2, :], op=ALU.mult).then_inc(qa_scaled, 1)
                pool.wait_ge(qa_scaled, t + 1)
                nc.gpsimd.tensor_tensor(out=qa_tok[:, t, :], in0=qa_tok[:, t, :], in1=g_rows[:, 3, :], op=ALU.add).then_inc(qa_made, 1)

            def expand_plain(t):
                pool.wait_ge(kv_biased, 2 * t + 2)
                if t >= 2:
                    pool.wait_ge(s_done, 2 * (t - 1))
                vv = kv[:, t, :].rearrange("p (a b f) -> p a b f", a=2, b=2)[:, :, 1, :]
                for j in range(4):
                    last = nc.gpsimd.tensor_tensor(out=vxp[t % 2][:, :, j, :], in0=vv, in1=mask_seq[:, j:j + 1].unsqueeze(2).to_broadcast([P, 2, D]),
                                                   op=ALU.mult)
                last.then_inc(vx_plain, 1)

            pool.wait_ge(masks_made, 1)
            for t in range(TILES):
                if t == 1:
                    residual_bo(0)
                    residual_bo(1)
                expand_plain(t)
                scaled_queries(t)
            for pr in range(PAIRS):
                pool.wait_ge(ln_out[pr], LN_L1)
                pool.wait_ge(last_tok_made, 1)
                nc.gpsimd.tensor_tensor(out=pair(g_act, pr), in0=pair(u, pr),
                                        in1=last_tok[:, :].unsqueeze(1).to_broadcast([P, 2, D]), op=ALU.add).then_inc(u_last, 1)
                nc.gpsimd.tensor_tensor(out=pair(haux, pr), in0=pair(h, pr), in1=row2('L1_attn_b2'), op=ALU.add).then_inc(hx_made, 1)
                pool.wait_ge(hx_made, 2 * pr + 1)
                pool.wait_ge(x1_made, pr + 1)
                nc.gpsimd.tensor_tensor(out=pair(haux, pr), in0=pair(haux, pr), in1=pair(y, pr), op=ALU.add).then_inc(hx_made, 1)
            pool.wait_ge(h3_made, 1)
            nc.gpsimd.tensor_tensor(out=pair(haux, 0), in0=pair(h, 0), in1=row2('L1_ffn_bias'), op=ALU.add).then_inc(hb_made, 1)
            for t in (2, 3):
                pool.wait_ge(h3_made, t)
                nc.gpsimd.tensor_tensor(out=haux[:, t, :], in0=h[:, t, :], in1=R['L1_ffn_bias'], op=ALU.add).then_inc(hb_made, 1)

        @block.scalar
        def _(act):
            preloads = [0]

            def preload(func):
                n = preloads[0]
                preloads[0] += 1
                nc.scalar.activation(scratch[:, n:n + 1], eps[:, 0:1], func)

            act.wait_ge(pool_step, 1)
            preload(ACT.Copy)

            def conv_weights_out(quads):
                for n in quads:
                    act.wait_ge(w_T, n + 1)
                    nc.scalar.activation(wT_quad(n), psB[:, n % 4, :].rearrange("p (k o) -> p k o", k=4), ACT.Copy).then_inc(w_evac_act, 1)

            def tile_a(i, after_quad=()):
                act.wait_ge(max_done, i + 1)
                act.wait_ge(centred_done, 2 * i + 2)
                for q in range(QUADS):
                    act.wait_ge(quad_T, i * QUADS + q + 1)
                    nc.scalar.activation(
                        xT[:, bass.ds(i % 2, 1), 2 * q:2 * q + 2, :].rearrange("p s k (h b n) -> p (s k h) b n", h=DH, n=NB),
                        psB[:, q % 4, :].rearrange("p (g n b) -> p g b n", g=4, n=NB), ACT.Copy).then_inc(ring_drained, 1)
                    for at, what in after_quad:
                        if at == q:
                            what()

            def conv_out(i):
                act.wait_ge(conv_done, i + 1)
                nc.scalar.activation(conv_tok[:, bass.ds(i, 1), :].rearrange("p s f -> p (s f)"),
                                     psA[:, bass.ds(i % 2, 1), 0:D].rearrange("p s f -> p (s f)"), ACT.Copy).then_inc(conv_bank_free, 1)

            def square(i, half):
                act.wait_ge(centred_done, 4 + 2 * i + half + 1)
                piece = centred[:, half * KB // 2:(half + 1) * KB // 2, :]
                nc.scalar.activation(piece, piece, ACT.Square).then_inc(squared, 1)

            def std(pr):
                act.wait_ge(ssq_done, 1 + 2 * pr + 2)
                part = comb[:, DH:2 * DH, 2 * P * pr:2 * P * (pr + 1)]
                nc.scalar.activation(part, part, ACT.Sqrt, scale=1.0 / (KB - 1)).then_inc(std_made, 1)

            def small_out(n):
                act.wait_ge(small_T, n + 1)
                dst = projT[:, 2 * n:2 * n + 2, :] if n < 3 else (woT[:, :, :], cbT[:, :, :])[n - 3]
                nc.scalar.activation(dst, psB[:, n % 4, :].rearrange("p (c o) -> p c o", c=2), ACT.Copy).then_inc(small_evac, 1)

            def columns():
                act.wait_ge(cols_T, 1)
                for dh in range(DH):
                    nc.scalar.activation(col[:, dh, :], psA[:, 2, dh * NCOL:(dh + 1) * NCOL], ACT.Copy).then_inc(cols_out, 1)
                act.wait_ge(mag2_made, 1)
                nc.scalar.activation(mag[:, 1, :], mag[:, 0, :], ACT.Sqrt).then_inc(mag_made, 1)
                act.wait_ge(mag_made, 1)
                nc.scalar.activation(mag[:, 2, :], mag[:, 1, :], ACT.Exp, scale=-1.0).then_inc(decay_made, 1)

            conv_weights_out((0, 2, 4, 6))
            tile_a(0)
            conv_weights_out((8, 10, 12, 14))
            columns()
            tile_a(1, ((5, lambda: square(0, 0)), (7, lambda: square(0, 1))))
            with act.Fori(2, TILES) as i:
                tile_a(i, ((1, lambda: conv_out(i - 2)), (5, lambda: square(i - 1, 0)), (7, lambda: square(i - 1, 1))))
            small_out(0)
            small_out(1)
            conv_out(TILES - 2)
            small_out(2)
            std(0)

            def conv_comb_out(pr):
                act.wait_ge(conv_T, pr + 1)
                for hh in range(DH):
                    last = nc.scalar.activation(comb[:, hh, 2 * P * pr:2 * P * (pr + 1)],
                                                psA[:, (2, 0)[pr], 2 * P * hh:2 * P * (hh + 1)],
                                                ACT.Identity, bias=vec('L0_tok_conv_b', hh))
                last.then_inc(conv_comb, 1)

            conv_comb_out(0)
            small_out(3)
            square(TILES - 1, 0)
            small_out(4)
            square(TILES - 1, 1)
            std(1)


            def ln_sqrt(k, pr):
                act.wait_ge(ln_mv[pr], 2 * k + 2)
                nc.scalar.activation(sd[:, 2 * pr:2 * pr + 2], mv[:, 2 * pr:2 * pr + 2, 1], ACT.Sqrt, bias=eps[:, 0:1]).then_inc(ln_sd[pr], 1)

            def evac_T(s, pr, scale=None, bias=None):
                act.wait_ge(trans_done[pr], s + 1)
                src = psB[:, 2 + pr, :].rearrange("p (h n) -> p h n", h=DH)
                if scale is None:
                    nc.scalar.activation(uT[:, :, 256 * pr:256 * pr + 256], src, ACT.Copy).then_inc(trans_evac[pr], 1)
                    return
                for hh in range(DH):
                    last = nc.scalar.activation(uT[:, hh, 256 * pr:256 * pr + 256], src[:, hh, :], ACT.Identity, scale=vec(scale, hh), bias=vec(bias, hh))
                last.then_inc(trans_evac[pr], 1)

            def spread_keys(t):
                act.wait_ge(kv_biased, 2 * t + 2)
                if t >= 2:
                    act.wait_ge(smix_done, 2 * (t - 1))
                kk = kv[:, t, :].rearrange("p (a b g i) -> p a b g i", a=2, b=2, i=32)[:, :, 0]
                for r in range(4):
                    rr = slice(32 * r, 32 * r + 32)
                    last = nc.scalar.activation(kx[rr, t % 2, :, :, r, :], kk[rr], ACT.Copy)
                last.then_inc(kx_made, 1)

            def expand_mixed(t):
                act.wait_ge(vmixed, t + 1)
                if t >= 2:
                    act.wait_ge(smix_done, 2 * (t - 1))
                for j in range(4):
                    last = nc.scalar.activation(vxm[t % 2][:, :, j, :], vmix[:, t], ACT.Copy, scale=mask_seq[:, j:j + 1])
                last.then_inc(vx_mixed, 1)

            def head_masked(dst, ps, mask):
                d = dst.rearrange("p (g m e) -> p g m e", m=2, e=16)
                s = ps.rearrange("p (g m e) -> p g m e", m=2, e=16)
                for m in range(2):
                    last = nc.scalar.activation(d[:, :, m, :], s[:, :, m, :], ACT.Copy, scale=mask[:, m:m + 1])
                return last

            def s1_step(n):
                if n >= 2:
                    act.wait_ge(y_done, n - 1)
                act.wait_ge(s_done, n + 1)
                head_masked(s12[:, n % 2, :], psA[:, 0, :], mask_head64).then_inc(s1_masked, 1)

            def mix_step(n):
                act.wait_ge(smix_done, n + 1)
                head_masked(smix[:, n % 2, :], psB[:, 0, :], mask_head).then_inc(smix_masked, 1)

            def gelu(pr):
                preload(ACT.Gelu_apprx_tanh)
                act.wait_ge(blk_done, pr + 1)
                nc.scalar.activation(g_act[:, 2 * pr:2 * pr + 2, :], psA[:, 2 + pr, :].rearrange("p (t f) -> p t f", t=2),
                                     ACT.Gelu_apprx_tanh).then_inc(gelu_done, 1)

            def u_sqrt(pr):
                act.wait_ge(uvar_step, 2 * pr + 2)
                nc.scalar.activation(usd[:, 2 * pr:2 * pr + 2], uvar[:, 2 * pr:2 * pr + 2], ACT.Sqrt, bias=eps[:, 0:1]).then_inc(usd_made, 1)

            def filtered(pr):
                act.wait_ge(filt_conv, pr + 1)
                nc.scalar.activation(filtT[:, :, 256 * pr:256 * pr + 256], psA[:, 2 + pr, :].rearrange("p (h n) -> p h n", h=DH),
                                     ACT.Copy).then_inc(filt_out, 1)

            def silu(pr, c):
                n = FC * pr + c
                act.wait_ge(w1_done, n + 1)
                cc = len(COLS) + c // 2
                nc.scalar.activation(gT[:, c, 2 * P * pr:2 * P * (pr + 1)], w1_bank(n)[:, 0:2 * P], ACT.Silu,
                                     bias=col[:, c % 2, cc:cc + 1]).then_inc(silu_done, 1)

            ln_sqrt(LN_TOK, 0)
            conv_out(TILES - 1)
            conv_comb_out(1)
            ln_sqrt(LN_ATTN, 0)
            evac_T(T_ATTN, 0)
            ln_sqrt(LN_TOK, 1)
            ln_sqrt(LN_ATTN, 1)
            act.wait_ge(masks_made, 1)
            act.wait_ge(centred_done, 4)
            spread_keys(0)
            evac_T(T_ATTN, 1)
            spread_keys(1)
            expand_mixed(0)
            expand_mixed(1)
            for n in range(STEPS):
                if n == 6:
                    ln_sqrt(LN_FFN, 0)
                s1_step(n)
                if n == 7:
                    gelu(0)
                if n == 5:
                    ln_sqrt(LN_Y, 0)
                mix_step(n)
                if n == 7:
                    preload(ACT.Sqrt)
                if n in (1, 3):
                    spread_keys(n // 2 + 2)
                if n in (2, 4):
                    expand_mixed(n // 2 + 1)
                if n == 5:
                    evac_T(T_WO, 0, 'L0_attn_ln_g', 'L0_attn_ln_b')
                if n == 6:
                    evac_T(T_FFN, 0)
            ln_sqrt(LN_L1, 0)
            u_sqrt(0)
            evac_T(T_SPIRAL, 0, 'L1_attn_ln_gamma', 'L1_attn_ln_beta')
            ln_sqrt(LN_Y, 1)
            filtered(0)
            evac_T(T_WO, 1, 'L0_attn_ln_g', 'L0_attn_ln_b')
            ln_sqrt(LN_MLP, 0)
            evac_T(T_MLP, 0, 'L1_attn_ln_gamma', 'L1_attn_ln_beta')
            ln_sqrt(LN_FFN, 1)
            preload(ACT.Silu)
            silu(0, 0)
            evac_T(T_FFN, 1)
            for c in range(1, FC):
                silu(0, c)
            gelu(1)
            preload(ACT.Sqrt)
            ln_sqrt(LN_L1, 1)
            u_sqrt(1)
            evac_T(T_SPIRAL, 1, 'L1_attn_ln_gamma', 'L1_attn_ln_beta')
            ln_sqrt(LN_CB, 0)
            filtered(1)
            evac_T(T_CB, 0)
            ln_sqrt(LN_MLP, 1)
            preload(ACT.Silu)
            evac_T(T_MLP, 1, 'L1_attn_ln_gamma', 'L1_attn_ln_beta')
            for c in range(FC):
                silu(1, c)
            preload(ACT.Sqrt)
            for n in range(2):
                t = 2 + n
                act.wait_ge(ln_mv[1], 2 * LN_CB + n + 1)
                nc.scalar.activation(sd[:, t:t + 1], mv[:, t, 1:2], ACT.Sqrt, bias=eps[:, 0:1]).then_inc(ln_sd[1], 1)
                act.wait_ge(trans_done[1], T_CB + n + 1)
                nc.scalar.activation(uT[:, :, t * P:(t + 1) * P], tail_T(t)[:, 0:D].rearrange("p (h n) -> p h n", h=DH),
                                     ACT.Copy).then_inc(trans_evac[1], 1)

        @block.vector
        def _(dve):
            steps = [0]

            def step(ins):
                steps[0] += 1
                ins.then_inc(dve_step, 1)
                dve.wait_ge(dve_step, steps[0])

            V = nc.vector
            dve.wait_ge(consts_made, 1)
            V.tensor_reduce(out=mask_seq[:, :], in_=seq16[:, :].rearrange("p (r j) -> p j r", j=4), axis=AX.X, op=ALU.add).then_inc(max_done, 1)
            dve.wait_ge(max_done, 1)
            V.tensor_reduce(out=slot[:, :], in_=ident[:, :].rearrange("p (b n) -> p n b", n=NB), axis=AX.X, op=ALU.add).then_inc(max_done, 1)
            V.tensor_reduce(out=slot_lt[:, :], in_=before[:, :].rearrange("p (b n) -> p n b", n=NB), axis=AX.X, op=ALU.add).then_inc(ssq_done, 1)
            step(V.tensor_reduce(out=mask_head[:, :], in_=head8[:, :].rearrange("p (c m) -> p m c", m=2), axis=AX.X, op=ALU.add))
            V.tensor_scalar(mask_head64[:, :], mask_head[:, :], 1.0 / (NB * NB), None, ALU.mult).then_inc(masks_made, 1)

            def conv_weights_out(quads):
                for n in quads:
                    dve.wait_ge(w_T, n + 1)
                    V.tensor_copy(wT_quad(n), psB[:, n % 4, :].rearrange("p (k o) -> p k o", k=4)).then_inc(w_evac_dve, 1)

            def by_feature(buf3):
                return buf3.rearrange("p k f -> p f k")

            def slot_xT(i):
                return xT[:, bass.ds(i % 2, 1), :, :].rearrange("p s k f -> p (s f) k")

            def cols_of(chunk, i):
                return comb[:, chunk:chunk + DH, bass.ds(i * P, P)]

            def mean(i):
                dve.wait_ge(ring_drained, QUADS * i + QUADS)
                dve.wait_ge(centred_done, 4 + 2 * i)
                V.tensor_reduce(out=negmean[:, :], in_=slot_xT(i), axis=AX.X, op=ALU.add).then_inc(negsum, 1)
                dve.wait_ge(negsum, i + 1)
                V.tensor_scalar(negmean[:, :], negmean[:, :], -1.0 / KB, None, ALU.mult).then_inc(mean_made, 1)

            def maximum(i):
                V.tensor_reduce(out=cols_of(2 * DH, i), in_=slot_xT(i), axis=AX.X, op=ALU.max).then_inc(max_done, 1)

            def sum_squares(i, half):
                dve.wait_ge(squared, 2 * i + half + 1)
                dst = cols_of(DH, i) if half == 0 else ssq_hi[:, :]
                V.tensor_reduce(out=dst, in_=by_feature(centred[:, half * KB // 2:(half + 1) * KB // 2, :]),
                                axis=AX.X, op=ALU.add).then_inc(ssq_half, 1)

            def add_halves(i):
                dve.wait_ge(ssq_half, 2 * i + 2)
                V.tensor_tensor(out=cols_of(DH, i), in0=cols_of(DH, i), in1=ssq_hi[:, :].rearrange("p (h f) -> p h f", h=DH),
                                op=ALU.add).then_inc(ssq_done, 1)
                dve.wait_ge(ssq_done, i + 2)

            def plus_identity(n):
                dve.wait_ge(small_T, 6 + n)
                dst = wqT[:, :, :] if n == 0 else wkvT[:, :, (n - 1) * D:n * D]
                V.tensor_tensor(out=dst,
                                in0=psB[:, (5 + n) % 4, :].rearrange("p (h o) -> p h o", h=DH),
                                in1=ident2[:, :].rearrange("p (h o) -> p h o", h=DH), op=ALU.add).then_inc(w_evac_dve, 1)

            conv_weights_out((1, 3, 5, 7))
            conv_weights_out((9, 11, 13, 15))

            dve.wait_ge(cols_out, 2)
            V.tensor_tensor(out=mag[:, 3, :], in0=both('L1_attn_phazor_re'), in1=both('L1_attn_phazor_re'), op=ALU.mult)
            step(V.tensor_tensor(out=mag[:, 4, :], in0=both('L1_attn_phazor_im'), in1=both('L1_attn_phazor_im'), op=ALU.mult))
            V.tensor_tensor(out=mag[:, 0, :], in0=mag[:, 3, :], in1=mag[:, 4, :], op=ALU.add).then_inc(mag2_made, 1)

            mean(0)
            dve.wait_ge(decay_made, 1)
            V.memset(pw[:, 0, 0, :], 1.0)
            V.memset(pw[:, 1, 0, :], 0.0)
            step(V.reciprocal(mag[:, 3, :], mag[:, 1, :]))
            step(V.tensor_tensor(out=mag[:, 4, :], in0=mag[:, 2, :], in1=mag[:, 3, :], op=ALU.mult))
            V.tensor_tensor(out=pw[:, 0, 1, :], in0=both('L1_attn_phazor_re'), in1=mag[:, 4, :], op=ALU.mult)
            step(V.tensor_tensor(out=pw[:, 1, 1, :], in0=both('L1_attn_phazor_im'), in1=mag[:, 4, :], op=ALU.mult))
            for m in (1, 2, 4):
                def low(ri):
                    return pw[:, ri, 1:m + 1, :]

                def top(ri):
                    return pw[:, ri, m:m + 1, :].to_broadcast([P, m, DH])
                V.tensor_tensor(out=pt[:, 0, 0:m, :], in0=low(0), in1=top(0), op=ALU.mult)
                V.tensor_tensor(out=pt[:, 1, 0:m, :], in0=low(1), in1=top(1), op=ALU.mult)
                V.tensor_tensor(out=pt[:, 2, 0:m, :], in0=low(0), in1=top(1), op=ALU.mult)
                step(V.tensor_tensor(out=pt[:, 3, 0:m, :], in0=low(1), in1=top(0), op=ALU.mult))
                V.tensor_tensor(out=pw[:, 0, m + 1:2 * m + 1, :], in0=pt[:, 0, 0:m, :], in1=pt[:, 1, 0:m, :], op=ALU.subtract)
                step(V.tensor_tensor(out=pw[:, 1, m + 1:2 * m + 1, :], in0=pt[:, 2, 0:m, :], in1=pt[:, 3, 0:m, :], op=ALU.add))
            def colb(name):
                return both(name).unsqueeze(1).to_broadcast([P, NB, DH])
            V.tensor_tensor(out=pt[:, 0, :, :], in0=pw[:, 0, 0:NB, :], in1=colb('L1_attn_phazor_init_re'), op=ALU.mult)
            V.tensor_tensor(out=pt[:, 1, :, :], in0=pw[:, 1, 0:NB, :], in1=colb('L1_attn_phazor_init_im'), op=ALU.mult)
            V.tensor_tensor(out=pt[:, 2, :, :], in0=pw[:, 0, 1:NB + 1, :], in1=colb('L1_attn_last_conv_re'), op=ALU.mult)
            step(V.tensor_tensor(out=pt[:, 3, :, :], in0=pw[:, 1, 1:NB + 1, :], in1=colb('L1_attn_last_conv_im'), op=ALU.mult))
            V.tensor_tensor(out=filt[:, :, :], in0=pt[:, 0, :, :], in1=pt[:, 1, :, :], op=ALU.subtract)
            V.tensor_tensor(out=lastf[:, :, :], in0=pt[:, 2, :, :], in1=pt[:, 3, :, :], op=ALU.subtract).then_inc(filt_made, 1)

            maximum(0)
            sum_squares(0, 0)
            with dve.Fori(1, TILES - 1) as i:
                mean(i)
                sum_squares(i - 1, 1)
                add_halves(i - 1)
                maximum(i)
                sum_squares(i, 0)
            i = TILES - 1
            mean(i)
            sum_squares(i - 1, 1)
            add_halves(i - 1)
            maximum(i)
            sum_squares(i, 0)
            plus_identity(0)
            sum_squares(i, 1)
            add_halves(i)
            plus_identity(1)

            def stats(k, pr, src):
                for t in (2 * pr, 2 * pr + 1):
                    V.bn_stats(st[:, t, :], src[:, t, :]).then_inc(ln_stat[pr], 1)
                for n, t in enumerate((2 * pr, 2 * pr + 1)):
                    dve.wait_ge(ln_stat[pr], 2 * k + n + 1)
                    V.bn_aggr(mv[:, t, :], st[:, t, :]).then_inc(ln_mv[pr], 1)

            def rstd(k, pr):
                dve.wait_ge(ln_sd[pr], k + 1)
                V.reciprocal(rs[:, 2 * pr:2 * pr + 2], sd[:, 2 * pr:2 * pr + 2]).then_inc(ln_rs[pr], 1)
                dve.wait_ge(ln_rs[pr], k + 1)

            def normalise(k, pr, src, dst):
                rstd(k, pr)
                for t in (2 * pr, 2 * pr + 1):
                    last = V.tensor_scalar(dst[:, t, :], src[:, t, :], mv[:, t, 0:1], rs[:, t:t + 1], ALU.subtract, ALU.mult)
                last.then_inc(ln_out[pr], 1)

            def pair(buf, pr):
                return buf[:, 2 * pr:2 * pr + 2, :]

            def bank2(bank):
                return bank.rearrange("p (t f) -> p t f", t=2)

            def row2(name):
                return R[name].unsqueeze(1).to_broadcast([P, 2, D])

            def tok_bias(pr):
                dve.wait_ge(proj_done, pr + 1)
                V.tensor_tensor(out=pair(y, pr), in0=bank2(psA[:, (3, 1)[pr], :]), in1=row2('L0_tok_proj_b'), op=ALU.add).then_inc(proj_biased, 1)
                dve.wait_ge(proj_biased, pr + 1)
                stats(LN_TOK, pr, y)

            def tok_norm(pr):
                rstd(LN_TOK, pr)
                for t in (2 * pr, 2 * pr + 1):
                    V.scalar_tensor_tensor(out=y[:, t, :], in0=y[:, t, :], scalar=mv[:, t, 0:1], in1=R['L0_tok_ln_g'],
                                           op0=ALU.subtract, op1=ALU.mult).then_inc(tok_scaled, 1)
                for t in (2 * pr, 2 * pr + 1):
                    dve.wait_ge(tok_scaled, t + 1)
                    last = V.scalar_tensor_tensor(out=h[:, t, :], in0=y[:, t, :], scalar=rs[:, t:t + 1], in1=pos[:, :],
                                                  op0=ALU.mult, op1=ALU.add)
                last.then_inc(tok_out, 1)
                dve.wait_ge(tok_out, pr + 1)
                stats(LN_ATTN, pr, h)

            def vv(t):
                return kv[:, t, :].rearrange("p (a b f) -> p a b f", a=2, b=2)[:, :, 1, :]

            def q_bias_add(t):
                dve.wait_ge(q_done, t + 1)
                V.tensor_tensor(out=q_tok[:, t, :], in0=psB[:, 1, 0:D], in1=R['L0_attn_bq'], op=ALU.add).then_inc(q_biased, 1)

            def kv_bias_add(t):
                for j in range(2):
                    dve.wait_ge(kv_done, 2 * t + j + 1)
                    V.tensor_tensor(out=kv[:, t, 512 * j:512 * j + 512], in0=kv_bank(t, j),
                                    in1=kv_bias[:, 512 * j:512 * j + 512], op=ALU.add).then_inc(kv_biased, 1)

            def mix_values(t):
                dve.wait_ge(vsum_done, t + 1)
                V.tensor_tensor(out=vmix[:, t], in0=bank2(psB[:, 0, :]), in1=g13, op=ALU.mult).then_inc(vscaled, 1)
                dve.wait_ge(vscaled, t + 1)
                V.tensor_tensor(out=vmix[:, t], in0=vmix[:, t], in1=vv(t), op=ALU.mult).then_inc(vmixed, 1)

            def spread_queries(n):
                t, hh = divmod(n, 2)
                if n == 0:
                    dve.wait_ge(qx_zero, 1)
                if n >= 2:
                    dve.wait_ge(y_done, n - 1)
                dve.wait_ge(qa_made, t + 1)
                for dst, src in ((qx, q_tok), (qax, qa_tok)):
                    for r in range(4):
                        rr = slice(32 * r, 32 * r + 32)
                        last = V.transpose(dst[rr, 4 * hh:4 * hh + 4, r, :],
                                           src[rr, t, hh * P:(hh + 1) * P].rearrange("p (g i) -> p g i", i=32))
                last.then_inc(qx_made, 1)

            def own_sequence(n):
                t, hh = divmod(n, 2)
                dve.wait_ge(y_done, n + 1)
                yv = y[:, t, hh * P:(hh + 1) * P].rearrange("p (g i) -> p g i", i=32)
                ps = y_bank(n).rearrange("p (g b i) -> p g b i", b=4, i=32)
                V.tensor_scalar(yv, ps[:, :, 0, :], mask_seq[:, 0:1], None, ALU.mult).then_inc(y_step, 1)
                for j in range(1, 4):
                    dve.wait_ge(y_step, 3 * n + j)
                    ins = V.scalar_tensor_tensor(out=yv, in0=ps[:, :, j, :], scalar=mask_seq[:, j:j + 1],
                                                 in1=yv, op0=ALU.mult, op1=ALU.add)
                    ins.then_inc(y_step if j < 3 else y_made, 1)

            def s12_step(n):
                dve.wait_ge(s1_masked, n + 1)
                V.tensor_tensor(out=s12[:, n % 2, :], in0=s12[:, n % 2, :], in1=psA[:, 1, :],
                                op=ALU.mult).then_inc(s12_made, 1)

            def y_stats(pr):
                dve.wait_ge(y_made, 4 * pr + 4)
                stats(LN_Y, pr, y)

            def wo_residual(pr):
                dve.wait_ge(wo_done, pr + 1)
                dve.wait_ge(hbo_made, pr + 1)
                V.tensor_tensor(out=pair(h, pr), in0=bank2(psA[:, 2 + pr, :]), in1=pair(haux, pr), op=ALU.add).then_inc(h1_made, 1)
                dve.wait_ge(h1_made, pr + 1)
                stats(LN_FFN, pr, h)

            def tok2(m):
                return m.unsqueeze(1).to_broadcast([P, 2, NB])

            def slot2(m):
                return m.unsqueeze(2).to_broadcast([P, 2, NB])

            def router_scores(pr):
                normalise(LN_FFN, pr, h, u)
                dve.wait_ge(ln_out[pr], LN_FFN)
                for t in (2 * pr, 2 * pr + 1):
                    V.scalar_tensor_tensor(out=y[:, t, :], in0=u[:, t, :], scalar=1.0, in1=R['L0_ffn_w_router'],
                                           op0=ALU.mult, op1=ALU.mult, accum_out=score[:, t:t + 1]).then_inc(score_made, 1)
                dve.wait_ge(score_made, 2 * pr + 2)
                part = slice(2 * pr, 2 * pr + 2)
                V.tensor_tensor(out=sc_rhs[:, part, :], in0=slot2(score[:, part]), in1=tok2(slot[:, :]), op=ALU.mult).then_inc(score_rhs, 1)

            def router_select(pr):
                part = slice(2 * pr, 2 * pr + 2)
                dve.wait_ge(score_all, pr + 1)
                allsc = psB[:, 2 + pr, 0:2 * NB].rearrange("p (t j) -> p t j", t=2)
                own, higher, tied = (sc_t[:, n, part] for n in range(3))
                step(V.tensor_tensor(out=own, in0=allsc, in1=tok2(slot[:, :]), op=ALU.mult))
                step(V.tensor_reduce(out=sc_self[:, part], in_=own, axis=AX.X, op=ALU.add))
                V.tensor_tensor(out=higher, in0=allsc, in1=slot2(sc_self[:, part]), op=ALU.is_gt)
                step(V.tensor_tensor(out=tied, in0=allsc, in1=slot2(sc_self[:, part]), op=ALU.is_equal))
                step(V.tensor_tensor(out=tied, in0=tied, in1=tok2(slot_lt[:, :]), op=ALU.mult))
                step(V.tensor_tensor(out=higher, in0=higher, in1=tied, op=ALU.add))
                step(V.tensor_reduce(out=rank[:, part], in_=higher, axis=AX.X, op=ALU.add))
                V.tensor_scalar(sel[:, 0, part], rank[:, part], TOPK - 0.5, None, ALU.is_lt)
                V.tensor_scalar(sel[:, 1, part], rank[:, part], TOPK - 0.5, None, ALU.is_gt).then_inc(sel_made, 1)
                dve.wait_ge(sel_made, pr + 1)
                for t in (2 * pr, 2 * pr + 1):
                    V.scalar_tensor_tensor(out=h[:, t, :], in0=u[:, t, :], scalar=sel[:, 1, t:t + 1], in1=h[:, t, :],
                                           op0=ALU.mult, op1=ALU.add).then_inc(kept, 1)

            def ffn_residual(pr):
                dve.wait_ge(gelu_done, pr + 1)
                for t in (2 * pr, 2 * pr + 1):
                    dve.wait_ge(kept, t + 1)
                    V.scalar_tensor_tensor(out=h[:, t, :], in0=g_act[:, t, :], scalar=sel[:, 0, t:t + 1], in1=h[:, t, :],
                                           op0=ALU.mult, op1=ALU.add).then_inc(h2_made, 1)
                dve.wait_ge(h2_made, 2 * pr + 2)
                stats(LN_L1, pr, h)

            def l1_norm(pr):
                normalise(LN_L1, pr, h, u)
                part = slice(2 * pr, 2 * pr + 2)
                V.scalar_tensor_tensor(out=uvar[:, part], in0=mv[:, part, 1], scalar=1.0, in1=rs[:, part],
                                       op0=ALU.mult, op1=ALU.mult).then_inc(uvar_step, 1)
                dve.wait_ge(uvar_step, 2 * pr + 1)
                V.tensor_tensor(out=uvar[:, part], in0=uvar[:, part], in1=rs[:, part], op=ALU.mult).then_inc(uvar_step, 1)

            def u_norm(pr):
                part = slice(2 * pr, 2 * pr + 2)
                dve.wait_ge(usd_made, pr + 1)
                V.reciprocal(urs[:, part], usd[:, part]).then_inc(urs_made, 1)
                dve.wait_ge(urs_made, pr + 1)
                dve.wait_ge(ln_out[pr], LN_L1)
                for t in (2 * pr, 2 * pr + 1):
                    last = V.tensor_scalar(y[:, t, :], u[:, t, :], urs[:, t:t + 1], None, ALU.mult)
                last.then_inc(un_made, 1)

            def spiral_residual(pr):
                dve.wait_ge(spiral_done, pr + 1)
                dve.wait_ge(u_last, pr + 1)
                V.tensor_tensor(out=pair(y, pr), in0=bank2(psB[:, 2 + pr, :]), in1=pair(g_act, pr), op=ALU.add).then_inc(x1_made, 1)
                dve.wait_ge(x1_made, pr + 1)
                stats(LN_MLP, pr, y)

            def mlp_residual(pr):
                dve.wait_ge(w2_done, pr + 1)
                dve.wait_ge(hx_made, 2 * pr + 2)
                V.tensor_tensor(out=pair(h, pr), in0=bank2(psA[:, 2 + pr, :]), in1=pair(haux, pr), op=ALU.add).then_inc(h3_made, 1)
                dve.wait_ge(h3_made, pr + 1)
                stats(LN_CB, pr, h)

            def cb_residual(pr):
                dve.wait_ge(cb_done, pr + 1)
                V.tensor_tensor(out=pair(y, pr), in0=bank2(psA[:, 2 + pr, :]), in1=row2('L1_ffn_SCB'), op=ALU.mult).then_inc(cb_scaled, 1)
                dve.wait_ge(cb_scaled, pr + 1)
                dve.wait_ge(hb_made, pr + 1)
                V.tensor_tensor(out=pair(h, pr), in0=pair(y, pr), in1=pair(haux, pr), op=ALU.add).then_inc(out_made, 1)

            dve.wait_ge(rows_in, 16 * (len(ROWS) + 5))
            tok_bias(0)
            dve.wait_ge(bpos_made, 1)
            tok_norm(0)
            plus_identity(2)
            normalise(LN_ATTN, 0, h, u)
            plus_identity(3)
            plus_identity(4)
            for part, factor in ((slice(0, 2), 1.0 / (NB * NB)), (slice(2, 4), 1.0)):
                V.tensor_scalar(g_rows[:, part, :].rearrange("p a (h e) -> p (a h) e", h=HEADS),
                                g_raw[:, part, :].rearrange("p a h -> p (a h)").unsqueeze(2).to_broadcast([P, 2 * HEADS, D // HEADS]),
                                factor, None, ALU.mult)
            step(V.tensor_scalar(R['L1_ffn_SCB'], R['L1_ffn_SCB'], 1.0 / 127.0, None, ALU.mult))

            tok_bias(1)
            q_bias_add(0)
            tok_norm(1)
            dve.wait_ge(cols_T, 2)
            V.tensor_copy(last_tok[:, :], psB[:, 0, 0:D]).then_inc(last_tok_made, 1)
            normalise(LN_ATTN, 1, h, u)
            kv_bias_add(0)
            q_bias_add(1)
            kv_bias_add(1)
            for t in (2, 3):
                mix_values(t - 2)
                q_bias_add(t)
                kv_bias_add(t)
            for t in (2, 3):
                mix_values(t)
            spread_queries(0)
            for n in range(STEPS):
                if n == 5:
                    normalise(LN_Y, 0, y, y)
                if n == 6:
                    wo_residual(0)
                s12_step(n)
                if n == 7:
                    router_select(0)
                if n == 6:
                    router_scores(0)
                if n == 5:
                    spread_queries(n)
                if n == 7:
                    ffn_residual(0)
                    l1_norm(0)
                    u_norm(0)
                if n >= 1:
                    own_sequence(n - 1)
                if n == 4:
                    y_stats(0)
                if n not in (4, 7):
                    spread_queries(n + 1)
            own_sequence(STEPS - 1)
            y_stats(1)
            normalise(LN_Y, 1, y, y)
            spiral_residual(0)
            normalise(LN_MLP, 0, y, u)
            wo_residual(1)
            router_scores(1)
            router_select(1)
            ffn_residual(1)
            l1_norm(1)
            u_norm(1)
            mlp_residual(0)
            normalise(LN_CB, 0, h, u)
            spiral_residual(1)
            normalise(LN_MLP, 1, y, u)
            cb_residual(0)
            for n in range(2):
                t = 2 + n
                dve.wait_ge(w2_done, t)
                dve.wait_ge(hx_made, 4)
                V.tensor_tensor(out=h[:, t, :], in0=tail_w2(t)[:, 0:D], in1=haux[:, t, :], op=ALU.add).then_inc(h3_made, 1)
                dve.wait_ge(h3_made, t)
                V.bn_stats(st[:, t, :], h[:, t, :]).then_inc(ln_stat[1], 1)
                dve.wait_ge(ln_stat[1], 2 * LN_CB + n + 1)
                V.bn_aggr(mv[:, t, :], st[:, t, :]).then_inc(ln_mv[1], 1)
                dve.wait_ge(ln_sd[1], LN_CB + n + 1)
                V.reciprocal(rs[:, t:t + 1], sd[:, t:t + 1]).then_inc(ln_rs[1], 1)
                dve.wait_ge(ln_rs[1], LN_CB + n + 1)
                V.tensor_scalar(u[:, t, :], h[:, t, :], mv[:, t, 0:1], rs[:, t:t + 1], ALU.subtract, ALU.mult).then_inc(ln_out[1], 1)
            for t in (2, 3):
                dve.wait_ge(cb_done, t)
                V.tensor_tensor(out=y[:, t, :], in0=tail_cb(t)[:, 0:D], in1=R['L1_ffn_SCB'], op=ALU.mult).then_inc(cb_scaled, 1)
                dve.wait_ge(cb_scaled, t)
                dve.wait_ge(hb_made, t)
                V.tensor_tensor(out=h[:, t, :], in0=y[:, t, :], in1=haux[:, t, :], op=ALU.add).then_inc(out_made, 1)

        @block.tensor
        def _(pe):
            T = nc.tensor.transpose
            M = nc.tensor.matmul

            def stay_warm(bank, n):
                for _ in range(n):
                    T(bank[:, 0:P], ident[:, :], ident[:, :])

            pe.wait_ge(pool_step, 2)
            stay_warm(psA[:, 3, :], 14)
            pe.wait_ge(consts_made, 1)

            def conv_weights_T(n):
                dh, oh, kk = n // 8, n // 4 % 2, n % 4
                if kk == 0:
                    pe.wait_ge(conv_w_in[DH * dh + oh], 16)
                if oh == 1:
                    pe.wait_ge((w_evac_act, w_evac_dve)[n % 2], (n - 4) // 2 + 1)
                elif dh == 1:
                    pe.wait_ge(ring_drained, 4 + kk + 1)
                for k in range(4):
                    last = T(psB[:, n % 4, k * P:(k + 1) * P],
                             conv_raw[:, oh, dh * P:(dh + 1) * P, 4 * kk + k], ident[:, :])
                last.then_inc(w_T, 1)

            def transpose_quad(n):
                i, q = divmod(n, QUADS)
                if q % (QUADS // 2) == 0:
                    pe.wait_ge(x_in_half[q // (QUADS // 2)], 32 * (i + 1))
                if n in (0, QUADS):
                    pe.wait_ge(w_evac_act, 4 * (i + 1))
                    pe.wait_ge(w_evac_dve, 4 * (i + 1))
                if n not in (0, 1, 2, 3, 8, 9, 10, 11):
                    pe.wait_ge(ring_drained, n - 3)
                for k in range(2):
                    for dh in range(DH):
                        last = T(psB[:, q % 4, (2 * k + dh) * P:(2 * k + dh + 1) * P],
                                 x_in[:, 2 * q + k, dh * P:(dh + 1) * P], ident[:, :])
                last.then_inc(quad_T, 1)

            def conv_quad(n, halves=range(DH)):
                i, q = divmod(n, QUADS)
                if q == 0 and i >= 2:
                    pe.wait_ge(conv_bank_free, i - 1)
                pe.wait_ge(ring_drained, n + 1)
                for k in range(2):
                    for dh in halves:
                        last = M(psA[:, i % 2, 0:D], xT[:, i % 2, 2 * q + k, dh * P:(dh + 1) * P], wT[:, 2 * q + k, dh, :],
                                 start=(q == 0 and k == 0 and dh == 0), stop=(q == QUADS - 1 and k == 1 and dh == 1))
                if q == QUADS - 1 and DH - 1 in halves:
                    last.then_inc(conv_done, 1)

            order = [('p', 0), ('p', 1), ('p', 2), ('s', 5), ('s', 6), ('s', 0), ('s', 1), ('s', 2), ('s', 3), ('s', 4)]

            def small_quad(n):
                if n == 0:
                    pe.wait_ge(raw_in, 16 * (2 + len(SMALL)))
                    pe.wait_ge(ring_drained, TILES * QUADS)
                if n >= 4:
                    m = n - 4
                    if m < 5:
                        pe.wait_ge(small_evac, m + 1)
                    else:
                        pe.wait_ge(w_evac_dve, 8 + m - 5 + 1)
                kind, j = order[n]
                for c in range(2):
                    for oh in range(DH):
                        if kind == 's':
                            src = small_raw[:, j, oh, c * P:(c + 1) * P]
                        else:
                            src = proj_raw[:, oh, (2 * j + c) * P:(2 * j + c + 1) * P]
                        last = T(psB[:, n % 4, (2 * c + oh) * P:(2 * c + oh + 1) * P], src, ident[:, :])
                last.then_inc(small_T, 1)

            def conv_tokens_T(pr):
                if pr == 0:
                    pe.wait_ge(cols_out, 2)
                pe.wait_ge(conv_bank_free, 2 * pr + 2)
                for hh in range(DH):
                    for t in range(2):
                        last = T(psA[:, (2, 0)[pr], (2 * hh + t) * P:(2 * hh + t + 1) * P],
                                 conv_tok[:, 2 * pr + t, hh * P:(hh + 1) * P], ident[:, :])
                last.then_inc(conv_T, 1)

            def project(pr):
                pe.wait_ge(small_evac, 3)
                pe.wait_ge(conv_comb, pr + 1)
                pe.wait_ge(std_made, pr + 1)
                pe.wait_ge(max_done, 2 + 2 * pr + 2)
                for t in (2 * pr, 2 * pr + 1):
                    if t == TILES - 1:
                        attn_T(0)
                    for c in range(3 * DH):
                        last = M(psA[:, (3, 1)[pr], (t % 2) * D:(t % 2 + 1) * D], comb[:, c, t * P:(t + 1) * P], projT[:, c, :],
                                 start=(c == 0), stop=(c == 3 * DH - 1))
                last.then_inc(proj_done, 1)

            def transpose_pair(s, pr, src):
                for hh in range(DH):
                    for t in range(2):
                        last = T(psB[:, 2 + pr, (2 * hh + t) * P:(2 * hh + t + 1) * P],
                                 src[:, 2 * pr + t, hh * P:(hh + 1) * P], ident[:, :])
                last.then_inc(trans_done[pr], 1)

            def attn_T(pr):
                pe.wait_ge(ln_out[pr], LN_ATTN)
                transpose_pair(T_ATTN, pr, u)

            for n in range(QUADS):
                conv_weights_T(n)
            transpose_quad(0)
            transpose_quad(1)
            for q in range(QUADS):
                conv_quad(q, (0,))
                if q + 2 < QUADS:
                    transpose_quad(q + 2)
                elif q + 2 == QUADS:
                    conv_weights_T(QUADS)
                    conv_weights_T(QUADS + 1)
            for n in range(QUADS + 2, 2 * QUADS):
                conv_weights_T(n)
            pe.wait_ge(cols_in, 16 * (len(COLS) + 1))
            for hh in range(DH):
                last = T(psA[:, 2, hh * NCOL:(hh + 1) * NCOL], colrow[:, hh * P:(hh + 1) * P], ident[0:NCOL, 0:NCOL])
            last.then_inc(cols_T, 1)
            done = QUADS
            for m in range(TILES * QUADS):
                if m < QUADS:
                    pe.wait_ge((w_evac_act, w_evac_dve)[m // 2 % 2], 4 + 2 + m // 4 + 1)
                    conv_quad(m, (1,))
                while done < m + QUADS + 1:
                    if done < TILES * QUADS:
                        transpose_quad(done)
                    else:
                        small_quad(done - TILES * QUADS)
                    done += 1
                if m == TILES * QUADS - 4:
                    conv_tokens_T(0)
                if m == TILES * QUADS - 2:
                    project(0)
                if m >= QUADS:
                    conv_quad(m)
            for n in range(done - TILES * QUADS, len(order) - 1):
                small_quad(n)
            conv_tokens_T(1)
            small_quad(len(order) - 1)
            project(1)
            pe.wait_ge(last_rep, 1)
            pe.wait_ge(w_evac_dve, 8 + 5)
            pe.wait_ge(small_evac, 5)
            for dh in range(DH):
                last = T(psB[:, 0, dh * P:(dh + 1) * P], lastT[:, dh, :, :], ident[:, :])
            last.then_inc(cols_T, 1)

            def linear_tile(t, lhs, rhs, chunks, of):
                for c in chunks:
                    last = M(psA[:, 2 + t // 2, (t % 2) * D:(t % 2 + 1) * D], lhs[:, c, t * P:(t + 1) * P], rhs[:, c, :],
                             start=(c == 0), stop=(c == of - 1))
                return last

            def linear_pair(pr, lhs, rhs, chunks, done):
                for t in (2 * pr, 2 * pr + 1):
                    last = linear_tile(t, lhs, rhs, range(chunks), chunks)
                last.then_inc(done, 1)

            def keys_queries(t):
                if t % 2 == 0:
                    pe.wait_ge(trans_evac[t // 2], T_ATTN + 1)
                if t >= 1:
                    pe.wait_ge(q_biased, t)
                for c in range(DH):
                    last = M(psB[:, 1, 0:D], uT[:, c, t * P:(t + 1) * P], wqT[:, c, :], start=(c == 0), stop=(c == DH - 1))
                last.then_inc(q_done, 1)
                if t == 1:
                    pe.wait_ge(proj_biased, PAIRS)
                if t >= 2:
                    pe.wait_ge(kv_biased, 2 * (t - 1))
                for j in range(2):
                    for c in range(DH):
                        last = M(kv_bank(t, j), uT[:, c, t * P:(t + 1) * P], wkvT[:, c, 512 * j:512 * j + 512],
                                 start=(c == 0), stop=(c == DH - 1))
                    last.then_inc(kv_done, 1)

            def value_sums(t):
                pe.wait_ge(kv_biased, 2 * t + 2)
                if t == 0:
                    pe.wait_ge(last_tok_made, 1)
                else:
                    pe.wait_ge(vscaled, t)
                for j in range(2):
                    v = kv[:, t, 768:1024] if j == 0 else kv[:, t, 256:512]
                    last = M(psB[:, 0, j * D:(j + 1) * D], same_seq[:, :], v, start=True, stop=True)
                last.then_inc(vsum_done, 1)

            def keys_values(n, bank, terms):
                t, hh = divmod(n, 2)
                for g in range(4):
                    for m, (which, v) in enumerate(terms):
                        G = 4 * hh + g
                        last = M(bank[:, g * P:(g + 1) * P].rearrange("p (b i) -> p b i", b=4),
                                 kx[:, t % 2, which, G, :, :], v[:, :, 32 * G:32 * G + 32],
                                 start=(m == 0), stop=(m == len(terms) - 1))
                return last

            def s_step(n):
                t = n // 2
                pe.wait_ge(kx_made, t + 1)
                pe.wait_ge(vx_plain, t + 1)
                if n == 0:
                    pe.wait_ge(kv_biased, 2 * TILES)
                else:
                    pe.wait_ge(s12_made, n)
                keys_values(n, psA[:, 0, :], ((0, vxp[t % 2][:, 0]),))
                keys_values(n, psA[:, 1, :], ((1, vxp[t % 2][:, 1]),)).then_inc(s_done, 1)

            def mix_step(n):
                t = n // 2
                pe.wait_ge(vx_mixed, t + 1)
                if n == 0:
                    pe.wait_ge(vscaled, TILES)
                else:
                    pe.wait_ge(smix_masked, n)
                keys_values(n, psB[:, 0, :], ((0, vxm[t % 2][:, 0]), (1, vxm[t % 2][:, 1]))).then_inc(smix_done, 1)

            def query_step(n):
                t, hh = divmod(n, 2)
                pe.wait_ge(qx_made, n + 1)
                pe.wait_ge(s12_made, n + 1)
                pe.wait_ge(smix_masked, n + 1)
                if n == 0:
                    pe.wait_ge(q_biased, TILES)
                if n >= 2:
                    pe.wait_ge(y_made, n - 1)
                for g in range(4):
                    for m, (q, s) in enumerate(((qx, smix), (qax, s12))):
                        last = M(y_bank(n)[:, g * P:(g + 1) * P], q[:, 4 * hh + g, :, :], s[:, n % 2, g * P:(g + 1) * P],
                                 start=(m == 0), stop=(m == 1))
                last.then_inc(y_done, 1)

            def after_ln_T(s, pr, src, made, count):
                pe.wait_ge(made, count)
                transpose_pair(s, pr, src)

            def after_T(s, pr):
                pe.wait_ge(trans_evac[pr], s + 1)

            def wo_linear(pr):
                after_T(T_WO, pr)
                linear_pair(pr, uT, woT, DH, wo_done)

            def ffn_linear(pr):
                after_T(T_FFN, pr)
                linear_pair(pr, uT, wblk, DH, blk_done)
                pe.wait_ge(score_rhs, pr + 1)
                M(psB[:, 2 + pr, 0:2 * NB], same_seq[:, :], sc_rhs[:, 2 * pr:2 * pr + 2, :].rearrange("p t j -> p (t j)"),
                  start=True, stop=True).then_inc(score_all, 1)

            def spiral_filter(pr):
                after_T(T_SPIRAL, pr)
                for dh in range(DH):
                    seqs = slice(256 * pr, 256 * pr + 256)
                    o = psA[:, 2 + pr, dh * D:(dh + 1) * D].rearrange("p (b n) -> p b n", n=NB)
                    i = uT[:, dh, seqs].rearrange("p (b n) -> p b n", n=NB)
                    for tau in range(NB):
                        last = M(o[:, :, tau:NB], diagF[:, dh, tau, :], i[:, :, 0:NB - tau], start=(tau == 0), stop=(tau == NB - 1))
                last.then_inc(filt_conv, 1)

            def spiral_back(pr):
                pe.wait_ge(filt_out, pr + 1)
                for t in range(2):
                    for dh in range(DH):
                        last = T(psB[:, 2 + pr, t * D + dh * P:t * D + (dh + 1) * P],
                                 filtT[:, dh, (2 * pr + t) * P:(2 * pr + t + 1) * P], ident[:, :])
                last.then_inc(spiral_done, 1)

            def w1_chunk(pr, c):
                n = FC * pr + c
                if n >= 4:
                    pe.wait_ge(silu_done, n - 3)
                for k in range(DH):
                    last = M(w1_bank(n)[:, 0:2 * P], w1[:, k, c * P:(c + 1) * P], uT[:, k, 2 * P * pr:2 * P * (pr + 1)],
                             start=(k == 0), stop=(k == DH - 1))
                last.then_inc(w1_done, 1)

            def cb_linear(pr):
                after_T(T_CB, pr)
                linear_pair(pr, uT, cbT, DH, cb_done)

            keys_queries(0)
            keys_queries(1)
            attn_T(1)
            for t in (2, 3):
                value_sums(t - 2)
                keys_queries(t)
            for t in (2, 3):
                value_sums(t)
            for n in range(STEPS):
                s_step(n)
                if n == 7:
                    ffn_linear(0)
                mix_step(n)
                if n == 5:
                    after_ln_T(T_WO, 0, y, ln_out[0], LN_Y)
                if n >= 1:
                    query_step(n - 1)
                if n == 5:
                    wo_linear(0)
                if n == 6:
                    after_ln_T(T_FFN, 0, u, ln_out[0], LN_FFN)
            query_step(STEPS - 1)
            stay_warm(psA[:, 0, :], 16)
            after_ln_T(T_SPIRAL, 0, y, un_made, 1)
            pe.wait_ge(diag_made, DH)
            stay_warm(psA[:, 0, :], 10)
            spiral_filter(0)
            after_ln_T(T_WO, 1, y, ln_out[1], LN_Y)
            spiral_back(0)
            wo_linear(1)
            stay_warm(psA[:, 0, :], 8)
            after_ln_T(T_MLP, 0, u, ln_out[0], LN_MLP)
            pe.wait_ge(late_in, 32)
            stay_warm(psA[:, 0, :], 8)
            after_T(T_MLP, 0)
            for c in range(FC):
                if c == 2:
                    after_ln_T(T_FFN, 1, u, ln_out[1], LN_FFN)
                if c == 3:
                    ffn_linear(1)
                w1_chunk(0, c)
            for c in range(FC):
                pe.wait_ge(silu_done, c + 1)
                linear_tile(0, gT, w2, (c,), FC)
            linear_tile(1, gT, w2, range(0, FC - 3), FC)
            after_ln_T(T_SPIRAL, 1, y, un_made, 2)
            linear_tile(1, gT, w2, range(FC - 3, FC), FC).then_inc(w2_done, 1)
            spiral_filter(1)
            stay_warm(psA[:, 0, :], 6)
            spiral_back(1)
            after_ln_T(T_CB, 0, u, ln_out[0], LN_CB)
            stay_warm(psA[:, 0, :], 6)
            cb_linear(0)
            stay_warm(psA[:, 0, :], 5)
            after_ln_T(T_MLP, 1, u, ln_out[1], LN_MLP)
            stay_warm(psA[:, 0, :], 10)
            after_T(T_MLP, 1)
            for c in range(FC):
                w1_chunk(1, c)
            for t in (2, 3):
                for c in range(FC):
                    if t == 2:
                        pe.wait_ge(silu_done, FC + c + 1)
                    last = M(tail_w2(t)[:, 0:D], gT[:, c, t * P:(t + 1) * P], w2[:, c, :], start=(c == 0), stop=(c == FC - 1))
                last.then_inc(w2_done, 1)
            for n in range(2):
                t = 2 + n
                pe.wait_ge(ln_out[1], LN_CB + n)
                for hh in range(DH):
                    last = T(tail_T(t)[:, hh * P:(hh + 1) * P], u[:, t, hh * P:(hh + 1) * P], ident[:, :])
                last.then_inc(trans_done[1], 1)
                pe.wait_ge(trans_evac[1], T_CB + n + 1)
                for c in range(DH):
                    last = M(tail_cb(t)[:, 0:D], uT[:, c, t * P:(t + 1) * P], cbT[:, c, :], start=(c == 0), stop=(c == DH - 1))
                last.then_inc(cb_done, 1)


def kernel(**inputs):
    import numpy as _np
    import concourse.bacc as _bacc
    from concourse import mybir as _mybir
    from concourse.bass_utils import run_bass_kernel_spmd as _run

    nc = _bacc.Bacc("TRN2", target_bir_lowering=False, num_devices=1)
    arrays, args = {}, {}
    for name in _INS:
        v = _np.ascontiguousarray(inputs[name])
        arrays[f"in_{name}"] = v
        args[name] = nc.dram_tensor(f"in_{name}", v.shape, _mybir.dt.from_np(v.dtype), kind="ExternalInput").ap()
    out = nc.dram_tensor("out_0", (64, 8, 256), _mybir.dt.float32, kind="ExternalOutput").ap()
    build_tower(nc, args, out)
    r = _run(nc, [arrays], core_ids=[0])
    return r.results[0]["out_0"]
```
